# Optimizing a Trainium2 kernel written in Bass

```python
import numpy as np
import jax
import jax.numpy as jnp

def _softmax(x, axis=-1):
    return jax.nn.softmax(x, axis=axis)

def _gelu(x):
    return jax.nn.gelu(x, approximate=True)

def _silu(x):
    return jax.nn.silu(x)

def _sigmoid(x):
    return jax.nn.sigmoid(x)

def _layernorm(x, axis=-1, eps=1e-05):
    m = jnp.mean(x, axis=axis, keepdims=True)
    v = jnp.var(x, axis=axis, keepdims=True)
    return (x - m) / jnp.sqrt(v + eps)

def _scatter_add(tgt, idx, src, axis=0):
    return tgt.at[idx].add(src)

def _segment_sum(src, seg, n):
    return jax.ops.segment_sum(src, seg, n)
kernel_name = 'mk_xattn_ffn_d2_seqx_r4_b95a49'

def setup_inputs(seed: int=0):
    np.random.seed(seed)
    _w = jnp.asarray

    def _rec_inputs():
        import jax
        import jax.numpy as jnp
        _rk = jax.random.key(seed)
        x = 0.5 + 0.2887 * jax.random.normal(jax.random.fold_in(_rk, 1), (4, 512, 512), jnp.float32)
        _lenS = 512 - jax.random.randint(jax.random.fold_in(_rk, 7), (4,), 0, max(1, 512 // 4) + 1, jnp.int32)
        _lenS2 = 512 - jax.random.randint(jax.random.fold_in(_rk, 8), (4,), 0, max(1, 512 // 4) + 1, jnp.int32)
        _ctx_512P = jax.random.normal(jax.random.fold_in(_rk, 11), (4, 16, 128), jnp.float32)
        _ctx_512c = jax.random.dirichlet(jax.random.fold_in(_rk, 511), 0.3 * jnp.ones((16,), jnp.float32), (4, 512))
        _ctx_512t = jnp.einsum('bsk,bkd->bsd', _ctx_512c, _ctx_512P)
        _ctx_512t = _ctx_512t * jax.lax.rsqrt(jnp.mean(jnp.square(_ctx_512t)) + 1e-12) * 0.953939
        ctx_512 = 7.22013e-05 + 1.00017 * (_ctx_512t + 0.3 * jax.random.normal(jax.random.fold_in(_rk, 611), (4, 512, 128), jnp.float32))
        _validS = jnp.arange(512)[None, :] < _lenS[:, None]
        _validS2 = jnp.arange(512)[None, :] < _lenS2[:, None]
        _causal = jnp.tril(jnp.ones((512, 512), dtype=bool))
        mask_SxS2_bk1 = jnp.broadcast_to(_validS2[0:1, :], (512, 512))
        mask_BxS2_bf0 = jnp.logical_not(jnp.ones((4, 512), dtype=bool))
        return (x, ctx_512, mask_SxS2_bk1, mask_BxS2_bf0)
    x, ctx_512, mask_SxS2_bk1, mask_BxS2_bf0 = _rec_inputs()

    def _L0_xattn_setup():
        import jax, jax.numpy as jnp
        import numpy as np
        B, S, H = (8, 512, 128)
        key = jax.random.key(seed)
        kq, kk, kqc, kwq, kwk = jax.random.split(key, 5)
        q = jax.random.normal(kq, (B, S, H), dtype=jnp.float32)
        k = jax.random.normal(kk, (B, S, H), dtype=jnp.float32)
        qc_score = jax.random.uniform(kqc, (B, S, S), dtype=jnp.float32)
        attn_mask = jnp.triu(jnp.ones((S, S), dtype=bool), k=1)
        key_padding_mask = jnp.zeros((B, S), dtype=bool)
        scale = 1.0 / np.sqrt(H)
        Wq = jax.random.normal(kwq, (H, H), dtype=jnp.float32) * scale
        Wk = jax.random.normal(kwk, (H, H), dtype=jnp.float32) * scale
        bq = jnp.zeros((H,), dtype=jnp.float32)
        bk = jnp.zeros((H,), dtype=jnp.float32)
        return {'q': q, 'k': k, 'attn_mask': attn_mask, 'key_padding_mask': key_padding_mask, 'qc_score': qc_score, 'Wq': Wq, 'bq': bq, 'Wk': Wk, 'bk': bk}
    _L0_xattn_all = _L0_xattn_setup()
    _L0_xattn_in = {k: v for k, v in _L0_xattn_all.items() if k in ('Wq', 'bq', 'Wk', 'bk')}
    del _L0_xattn_all

    def _L0_ffn_setup():
        import jax, jax.numpy as jnp
        import numpy as np
        FP8_MAX = 448.0
        GLOBAL_DIV = 448.0 * 6.0

        def _fp8(x):
            return x.astype(jnp.float8_e4m3fn).astype(jnp.float32)

        def _reorder_quantize_x(x, idx):
            scale = jnp.max(jnp.abs(x)) / GLOBAL_DIV
            xr = (x / scale)[:, idx]
            scale_x = jnp.max(jnp.abs(xr), axis=1, keepdims=True) / FP8_MAX
            qx = _fp8(xr / scale_x)
            return (qx, scale_x, scale)

        def _qlinear(qx, scale_x, scale, W, idx, out_idx=None):
            Wr = W[:, idx]
            w_scale = jnp.max(jnp.abs(Wr), axis=1, keepdims=True) / FP8_MAX
            qw = _fp8(Wr / w_scale)
            y = qx * scale_x @ (qw * w_scale).T * scale
            if out_idx is not None:
                y = y[:, out_idx]
            return y
        key = jax.random.key(seed)
        ks = jax.random.split(key, 6)
        B, S, H, I = (2, 256, 512, 1408)
        return {'x': jax.random.normal(ks[0], (B, S, H), jnp.float32), 'w_gate': jax.random.normal(ks[1], (I, H), jnp.float32) * 0.02, 'w_up': jax.random.normal(ks[2], (I, H), jnp.float32) * 0.02, 'w_down': jax.random.normal(ks[3], (H, I), jnp.float32) * 0.02, 'up_reorder_index': jax.random.permutation(ks[4], jnp.arange(H, dtype=jnp.int64)), 'down_reorder_index': jax.random.permutation(ks[5], jnp.arange(I, dtype=jnp.int64))}
    _L0_ffn_all = _L0_ffn_setup()
    _L0_ffn_in = {k: v for k, v in _L0_ffn_all.items() if k in ('w_gate', 'w_up', 'w_down', 'up_reorder_index', 'down_reorder_index')}
    del _L0_ffn_all

    def _L1_xattn_setup():
        import jax, jax.numpy as jnp
        import numpy as np
        B, S, L = (2, 256, 256)
        DIM_Q, H, K, D_C, D_CQ, R = (512, 16, 128, 128, 384, 64)

        def _rope_tables(seq_len, dim, dtype):
            inv_freq = 1.0 / 10000.0 ** (jnp.arange(0, dim, 2, dtype=dtype) / dim)
            t = jnp.arange(seq_len, dtype=dtype)
            freqs = t[:, None] * inv_freq[None, :]
            sin = jnp.repeat(jnp.sin(freqs), 2, axis=-1)
            cos = jnp.repeat(jnp.cos(freqs), 2, axis=-1)
            return (sin, cos)

        def _rotate_half(x):
            h = x.shape[-1] // 2
            return jnp.concatenate([-x[..., h:], x[..., :h]], axis=-1)
        key = jax.random.key(seed)
        ks = jax.random.split(key, 8)
        s_in = 1.0 / np.sqrt(DIM_Q)
        s_k = 1.0 / np.sqrt(K)
        s_cq = 1.0 / np.sqrt(D_CQ)
        s_c = 1.0 / np.sqrt(D_C)
        return {'hidden_q': jax.random.normal(ks[0], (B, S, DIM_Q), jnp.float32), 'kv_c': jax.random.normal(ks[1], (B, L, D_C), jnp.float32), 'Wq': jax.random.normal(ks[2], (H * K, DIM_Q), jnp.float32) * s_in, 'w_kc_q': jax.random.normal(ks[3], (H, K, D_CQ), jnp.float32) * s_k, 'w_kc_kv': jax.random.normal(ks[4], (H, K, D_C), jnp.float32) * s_k, 'W_qr': jax.random.normal(ks[5], (H, D_CQ, R), jnp.float32) * s_cq / np.sqrt(R), 'W_kr': jax.random.normal(ks[6], (H, D_C, R), jnp.float32) * s_c, 'Wo': jax.random.normal(ks[7], (DIM_Q, H * K), jnp.float32) * s_k}
    _L1_xattn_all = _L1_xattn_setup()
    _L1_xattn_in = {k: v for k, v in _L1_xattn_all.items() if k in ('Wq', 'w_kc_q', 'w_kc_kv', 'W_qr', 'W_kr', 'Wo')}
    del _L1_xattn_all

    def _L1_ffn_setup():
        import jax, jax.numpy as jnp
        import numpy as np
        TOPK = 2
        key = jax.random.key(seed)
        ks = jax.random.split(key, 6)
        B, T, H, S, r, ad = (2, 1024, 512, 32, 16, 32)
        h = jax.random.normal(ks[0], (B, T, H), dtype=jnp.float32)
        Wr = jax.random.normal(ks[1], (S, H), dtype=jnp.float32) * 0.02
        U = jax.random.normal(ks[2], (S, H, r), dtype=jnp.float32) * 0.02
        V = jax.random.normal(ks[3], (S, r, H), dtype=jnp.float32) * 0.02
        attr = jax.random.normal(ks[4], (S, ad), dtype=jnp.float32) * 0.02
        Wa = jax.random.normal(ks[5], (1, ad), dtype=jnp.float32) * 0.02
        return {'h': h, 'Wr': Wr, 'U': U, 'V': V, 'attr': attr, 'Wa': Wa}
    _L1_ffn_all = _L1_ffn_setup()
    _L1_ffn_in = {k: v for k, v in _L1_ffn_all.items() if k in ('Wr', 'U', 'V', 'attr', 'Wa')}
    del _L1_ffn_all
    return {'x': x, 'ctx_512': ctx_512, 'mask_SxS2_bk1': mask_SxS2_bk1, 'mask_BxS2_bf0': mask_BxS2_bf0, 'L0_xattn_Wq': _L0_xattn_in['Wq'], 'L0_xattn_bq': _L0_xattn_in['bq'], 'L0_xattn_Wk': _L0_xattn_in['Wk'], 'L0_xattn_bk': _L0_xattn_in['bk'], 'L0_ffn_w_gate': _L0_ffn_in['w_gate'], 'L0_ffn_w_up': _L0_ffn_in['w_up'], 'L0_ffn_w_down': _L0_ffn_in['w_down'], 'L0_ffn_up_reorder_index': _L0_ffn_in['up_reorder_index'], 'L0_ffn_down_reorder_index': _L0_ffn_in['down_reorder_index'], 'L1_xattn_Wq': _L1_xattn_in['Wq'], 'L1_xattn_w_kc_q': _L1_xattn_in['w_kc_q'], 'L1_xattn_w_kc_kv': _L1_xattn_in['w_kc_kv'], 'L1_xattn_W_qr': _L1_xattn_in['W_qr'], 'L1_xattn_W_kr': _L1_xattn_in['W_kr'], 'L1_xattn_Wo': _L1_xattn_in['Wo'], 'L1_ffn_Wr': _L1_ffn_in['Wr'], 'L1_ffn_U': _L1_ffn_in['U'], 'L1_ffn_V': _L1_ffn_in['V'], 'L1_ffn_attr': _L1_ffn_in['attr'], 'L1_ffn_Wa': _L1_ffn_in['Wa']}

def reference(x, ctx_512, mask_SxS2_bk1, mask_BxS2_bf0, L0_xattn_Wq, L0_xattn_bq, L0_xattn_Wk, L0_xattn_bk, L0_ffn_w_gate, L0_ffn_w_up, L0_ffn_w_down, L0_ffn_up_reorder_index, L0_ffn_down_reorder_index, L1_xattn_Wq, L1_xattn_w_kc_q, L1_xattn_w_kc_kv, L1_xattn_W_qr, L1_xattn_W_kr, L1_xattn_Wo, L1_ffn_Wr, L1_ffn_U, L1_ffn_V, L1_ffn_attr, L1_ffn_Wa):
    import jax
    import jax.numpy as jnp

    def _L0_xattn_ref(q, k, attn_mask, key_padding_mask, qc_score, Wq, bq, Wk, bk):
        import jax, jax.numpy as jnp
        import numpy as np
        B, S, H = (8, 512, 128)
        qp = jnp.einsum('bsh,oh->bso', q, Wq) + bq
        kp = jnp.einsum('bth,oh->bto', k, Wk) + bk
        scaling = jnp.asarray(float(H) ** (-0.5), dtype=qp.dtype)
        scores = jnp.einsum('bsh,bth->bst', qp, kp) * scaling
        scores = scores * qc_score
        mask = attn_mask[None, :, :] | key_padding_mask[:, None, :]
        scores = jnp.where(mask, -jnp.inf, scores)
        return jax.nn.softmax(scores, axis=-1)

    def _L0_ffn_ref(x, w_gate, w_up, w_down, up_reorder_index, down_reorder_index):
        import jax, jax.numpy as jnp
        import numpy as np
        FP8_MAX = 448.0
        GLOBAL_DIV = 448.0 * 6.0

        def _fp8(x):
            return x.astype(jnp.float8_e4m3fn).astype(jnp.float32)

        def _reorder_quantize_x(x, idx):
            scale = jnp.max(jnp.abs(x)) / GLOBAL_DIV
            xr = (x / scale)[:, idx]
            scale_x = jnp.max(jnp.abs(xr), axis=1, keepdims=True) / FP8_MAX
            qx = _fp8(xr / scale_x)
            return (qx, scale_x, scale)

        def _qlinear(qx, scale_x, scale, W, idx, out_idx=None):
            Wr = W[:, idx]
            w_scale = jnp.max(jnp.abs(Wr), axis=1, keepdims=True) / FP8_MAX
            qw = _fp8(Wr / w_scale)
            y = qx * scale_x @ (qw * w_scale).T * scale
            if out_idx is not None:
                y = y[:, out_idx]
            return y
        B, S, H = x.shape
        xf = x.reshape(B * S, H)
        qx, sx, sc = _reorder_quantize_x(xf, up_reorder_index)
        g = _qlinear(qx, sx, sc, w_gate, up_reorder_index, out_idx=down_reorder_index)
        u = _qlinear(qx, sx, sc, w_up, up_reorder_index, out_idx=down_reorder_index)
        t = jax.nn.silu(g) * u
        qt, st, sct = _reorder_quantize_x(t, down_reorder_index)
        y = _qlinear(qt, st, sct, w_down, down_reorder_index)
        return y.reshape(B, S, H)

    def _L1_xattn_ref(hidden_q, kv_c, Wq, w_kc_q, w_kc_kv, W_qr, W_kr, Wo):
        import jax, jax.numpy as jnp
        import numpy as np
        B, S, L = (2, 256, 256)
        DIM_Q, H, K, D_C, D_CQ, R = (512, 16, 128, 128, 384, 64)

        def _rope_tables(seq_len, dim, dtype):
            inv_freq = 1.0 / 10000.0 ** (jnp.arange(0, dim, 2, dtype=dtype) / dim)
            t = jnp.arange(seq_len, dtype=dtype)
            freqs = t[:, None] * inv_freq[None, :]
            sin = jnp.repeat(jnp.sin(freqs), 2, axis=-1)
            cos = jnp.repeat(jnp.cos(freqs), 2, axis=-1)
            return (sin, cos)

        def _rotate_half(x):
            h = x.shape[-1] // 2
            return jnp.concatenate([-x[..., h:], x[..., :h]], axis=-1)
        b, s, _ = hidden_q.shape
        l = kv_c.shape[1]
        q_hk = (hidden_q @ Wq.T).reshape(b, s, H, K)
        q_big = jnp.einsum('bshk,hkq->bshq', q_hk, w_kc_q)
        sin, cos = _rope_tables(l, D_C, kv_c.dtype)
        kv_rope = kv_c * cos[None] + _rotate_half(kv_c) * sin[None]
        q_r = jnp.einsum('bshq,hqr->bhsr', q_big, W_qr)
        k_r = jnp.einsum('bld,hdr->bhlr', kv_rope, W_kr)
        scores = jnp.einsum('bhsr,bhlr->bhsl', q_r, k_r)
        attn = jax.nn.softmax(scores, axis=-1)
        ctx_c = jnp.einsum('bhsl,bld->bhsd', attn, kv_rope)
        ctx_lat = jnp.einsum('bhsd,hkd->bshk', ctx_c, w_kc_kv)
        out = ctx_lat.reshape(b, s, H * K) @ Wo.T
        return out

    def _L1_ffn_ref(h, Wr, U, V, attr, Wa):
        import jax, jax.numpy as jnp
        import numpy as np
        TOPK = 2
        S = Wr.shape[0]
        sc = jnp.einsum('bth,sh->bts', h, Wr)
        _, idx = jax.lax.top_k(sc, TOPK)
        m = jax.nn.one_hot(idx, S, dtype=sc.dtype).sum(axis=-2)
        g = jax.nn.softmax(sc, axis=-1) * m
        g = g / (g.sum(axis=-1, keepdims=True) + 1e-08)
        hU = jnp.einsum('bth,shr->btsr', h, U)
        out = jnp.einsum('bts,btsr,srh->bth', g, hU, V)
        aw = jax.nn.sigmoid(attr @ Wa[0])
        gate = (g @ aw)[..., None]
        return out * (0.9 + 0.2 * gate)
    x = x + _L0_xattn_ref(ctx_512, ctx_512, mask_SxS2_bk1, mask_BxS2_bf0, _layernorm(x, axis=-1), L0_xattn_Wq, L0_xattn_bq, L0_xattn_Wk, L0_xattn_bk)
    x = x + _L0_ffn_ref(_layernorm(x, axis=-1), L0_ffn_w_gate, L0_ffn_w_up, L0_ffn_w_down, L0_ffn_up_reorder_index, L0_ffn_down_reorder_index)
    x = x + _L1_xattn_ref(_layernorm(x, axis=-1), ctx_512, L1_xattn_Wq, L1_xattn_w_kc_q, L1_xattn_w_kc_kv, L1_xattn_W_qr, L1_xattn_W_kr, L1_xattn_Wo)
    x = x + _L1_ffn_ref(_layernorm(x, axis=-1), L1_ffn_Wr, L1_ffn_U, L1_ffn_V, L1_ffn_attr, L1_ffn_Wa)
    return x

_drawn_inputs = setup_inputs


def setup_inputs(seed=0):
    import zlib

    import numpy as np

    out = dict(_drawn_inputs(seed))
    spreads = {'L0_xattn_bq': (0.0, 0.8), 'L0_xattn_bk': (0.0, 0.8)}
    factors = {'L1_ffn_Wr': 3.237,
     'L1_ffn_U': 3.194,
     'L1_ffn_V': 3.1,
     'L1_ffn_attr': 8.0,
     'L1_ffn_Wa': 8.0}
    for name, (base, spread) in spreads.items():
        noise = np.random.default_rng([zlib.crc32(name.encode()), seed]).standard_normal(out[name].shape)
        drawn = base * np.exp(spread * noise) if base else spread * noise
        out[name] = jnp.asarray(drawn.astype(out[name].dtype))
    for name, factor in factors.items():
        out[name] = (out[name] * factor).astype(out[name].dtype)
    return out
```

```python
from contextlib import ExitStack

import numpy as np

import concourse.bass as bass
from concourse import mybir

P = 128
B, S, D = 4, 512, 512
T = B * S
NT = T // P
TPB = S // P
KC = D // P
DC = 128
FF = 1408
FC = FF // P
LN_EPS = 1e-5
FP8_MAX = 448.0
MASKED = -1e30

F32 = mybir.dt.float32
F32R = mybir.dt.float32r
BF16 = mybir.dt.bfloat16
U32 = mybir.dt.uint32
I32 = mybir.dt.int32
U8 = mybir.dt.uint8
ALU = mybir.AluOpType
ACT = mybir.ActivationFunctionType
AX_X = mybir.AxisListType.X


def ring(ctx, nc):
    def sb(name, shape, dt=F32):
        return ctx.enter_context(nc.sbuf_tensor(name, shape, dt))

    def ps(name, shape, dt=F32):
        return ctx.enter_context(nc.psum_tensor(name, shape, dt))

    def sem(name):
        return ctx.enter_context(nc.semaphore(name))
    return sb, ps, sem


def tile_of(a, n):
    return a[:, bass.ds(n, 1), :].rearrange("p o d -> p (o d)")


def past(eng, sem, value, ticks):
    eng.wait_ge(sem, value)
    if not isinstance(value, int):
        eng.sem_inc(ticks, 1)


def stage_masked_attention(nc, sems, d, x_res, mean, rstd, ident):
    with ExitStack() as ctx:
        sb, ps, _ = ring(ctx, nc)
        sem = sems
        ctxT = sb("a_ctxT", [P, T])
        wT = sb("a_wT", [P, 2, P])
        bias_qk = sb("a_bqk", [P, 2])
        mask8 = sb("a_mask8", [P, TPB, S], U8)
        pad8 = sb("a_pad8", [P, B, S], U8)
        mask_bias = sb("a_maskb", [P, TPB, S])
        pad_bias = sb("a_padb", [P, B, S])
        both_bias = sb("a_bothb", [P, TPB, S])
        stats = sb("a_stats", [P, NT, 6])
        mv = sb("a_mv", [P, NT, 2])
        var_eps = sb("a_vareps", [P, NT])
        m_half = sb("a_mhalf", [P, NT])
        qT = sb("a_qT", [P, S])
        kT = sb("a_kT", [P, S])
        xn = sb("a_xn", [P, 2, S])
        z = sb("a_z", [P, 2, S])
        prob = sb("a_prob", [P, 2, S])
        nmax = sb("a_nmax", [P, 2])
        rsum = sb("a_rsum", [P, 2])
        rinv = sb("a_rinv", [P, 2])
        ps_q = ps("a_psq", [P, S])
        ps_k = ps("a_psk", [P, S])
        ps_s = ps("a_pss", [P, 2, S])

        x_loaded = [sem(f"a_x_loaded{b}") for b in range(B)]
        w_loaded = sem("a_w_loaded")
        m_loaded = sem("a_m_loaded")
        halves = sem("a_halves")
        stats_done = sem("a_stats_done")
        rstd_done = sem("a_rstd_done")
        bias_made = sem("a_bias_made")
        batch_bias = sem("a_batch_bias")
        qk_mm = sem("a_qk_mm")
        qk_ready = sem("a_qk_ready")
        score_mm = sem("a_score_mm")
        xn_done = sem("a_xn_done")
        z_scaled = sem("a_z_scaled")
        z_done = sem("a_z_done")
        max_done = sem("a_max_done")
        exp_done = sem("a_exp_done")
        rinv_done = sem("a_rinv_done")
        x_done = sem("a_x_done")
        id_zero = sem("a_id_zero")
        ticks = sem("a_ticks")
        SCALE = float(DC) ** -0.5
        FREE_HALVES, FREE_QK, FREE_BATCH = 2, 1, TPB

        block = ctx.enter_context(nc.Block())

        @block.sync
        def _(sp):
            sp.dma_start(wT[:, 0, :], d["L0_WqT"]).then_inc(w_loaded, 16)
            sp.dma_start(wT[:, 1, :], d["L0_WkT"]).then_inc(w_loaded, 16)
            sp.dma_start(bias_qk[:, 0:1], d["L0_xattn_bq"].rearrange("(p o) -> p o", o=1)).then_inc(w_loaded, 16)
            sp.dma_start(bias_qk[:, 1:2], d["L0_xattn_bk"].rearrange("(p o) -> p o", o=1)).then_inc(w_loaded, 16)
            sp.dma_start(ctxT[:], d["ctxT"]).then_inc(w_loaded, 16)
            sp.dma_start(mask8[:], d["attn_mask"].rearrange("(t p) l -> p t l", p=P)).then_inc(m_loaded, 16)
            sp.dma_start(pad8[:], d["pad_mask"].rearrange("(o b) l -> o b l", o=1).broadcast_to([P, B, S])).then_inc(m_loaded, 16)
            for b in range(B):
                sp.dma_start(x_res[:, TPB * b:TPB * (b + 1), :],
                             d["x"].rearrange("(n p) c -> p n c", p=P)[:, TPB * b:TPB * (b + 1), :]).then_inc(x_loaded[b], 16)

        @block.gpsimd
        def _(pool):
            pool.memset(ident[:], 0.0).then_inc(id_zero, 1)
            pool.memset(m_half[:], -0.5).then_inc(halves, 1)
            pool.wait_ge(id_zero, 1)
            pool.affine_select(out=ident[:], in_=ident[:], compare_op=ALU.not_equal, fill=1.0, base=0,
                               pattern=[[-1, P]], channel_multiplier=1).then_inc(id_zero, 1)
            pool.wait_ge(m_loaded, 32)
            pool.tensor_scalar(mask_bias[:], mask8[:], MASKED, 1.0, ALU.mult, ALU.mult).then_inc(bias_made, 1)
            pool.tensor_scalar(pad_bias[:], pad8[:], MASKED, 1.0, ALU.mult, ALU.mult).then_inc(bias_made, 1)
            pool.wait_ge(stats_done, 2 * NT + 1)
            pool.wait_ge(halves, 1)
            pool.tensor_tensor(rstd[:], var_eps[:], m_half[:], ALU.pow).then_inc(rstd_done, 1)
            pool.wait_ge(bias_made, 2)
            with pool.Fori(0, B) as b:
                for t in range(TPB):
                    past(pool, z_done, b * TPB + t + 1, ticks)
                    pool.tensor_tensor(both_bias[:, t, :], mask_bias[:, t, :], tile_of(pad_bias, b), ALU.add).then_inc(batch_bias, 1)

        @block.tensor
        def _(pe):
            pe.wait_ge(w_loaded, 80)
            with pe.Fori(0, B) as b:
                pe.wait_ge(qk_ready, b * 2 + 1)
                pe.matmul(ps_q[:], wT[:, 0, :], ctxT[:, bass.ds(b * S, S)], start=True, stop=True).then_inc(qk_mm, 1)
                pe.matmul(ps_k[:], wT[:, 1, :], ctxT[:, bass.ds(b * S, S)], start=True, stop=True).then_inc(qk_mm, 1)
                pe.wait_ge(qk_ready, b * 2 + 2 + FREE_QK)
                for t in range(TPB):
                    pe.wait_ge(z_scaled, b * TPB + t + 1)
                    pe.matmul(ps_s[:, t % 2, :], qT[:, t * P:(t + 1) * P], kT[:], start=True, stop=True).then_inc(score_mm, 1)

        @block.scalar
        def _(act):
            act.wait_ge(w_loaded, 80)
            with act.Fori(0, B) as b:
                act.wait_ge(score_mm, b * TPB + 1)
                act.wait_ge(qk_mm, b * 2 + 1)
                act.activation(qT[:], ps_q[:], ACT.Identity, bias=bias_qk[:, 0:1]).then_inc(qk_ready, 1)
                act.wait_ge(qk_mm, b * 2 + 2)
                act.activation(kT[:], ps_k[:], ACT.Identity, bias=bias_qk[:, 1:2]).then_inc(qk_ready, 1)
                for t in range(TPB):
                    act.wait_ge(max_done, b * TPB + t + 1)
                    act.wait_ge(x_done, b * TPB + t + 1)
                    act.activation(prob[:, t % 2, :], z[:, t % 2, :], ACT.Exp, bias=nmax[:, t % 2:t % 2 + 1],
                                   accum_out=rsum[:, t % 2:t % 2 + 1]).then_inc(exp_done, 1)

        @block.vector
        def _(dve):
            dve.sem_inc(z_scaled, FREE_HALVES)
            dve.sem_inc(exp_done, FREE_HALVES)
            dve.sem_inc(x_done, FREE_HALVES)
            dve.sem_inc(qk_ready, FREE_QK)
            dve.sem_inc(z_done, FREE_BATCH)
            dve.sem_inc(score_mm, FREE_BATCH)
            for n in range(NT):
                dve.wait_ge(x_loaded[n // TPB], 16)
                dve.bn_stats(stats[:, n, :], x_res[:, n, :]).then_inc(stats_done, 1)
            for n in range(NT):
                dve.wait_ge(stats_done, n + 1)
                dve.bn_aggr(mv[:, n, :], stats[:, n, :]).then_inc(stats_done, 1)
            dve.wait_ge(stats_done, 2 * NT)
            dve.tensor_scalar(var_eps[:], mv[:, :, 1], LN_EPS, None, ALU.add).then_inc(stats_done, 1)
            dve.tensor_copy(mean[:], mv[:, :, 0]).then_inc(stats_done, 1)
            dve.wait_ge(rstd_done, 1)
            dve.wait_ge(stats_done, 2 * NT + 2)
            with dve.Fori(0, B) as b:
                for t in range(TPB):
                    n = b * TPB + t
                    s = t % 2
                    dve.tensor_scalar(xn[:, s, :], tile_of(x_res, n), mean[:, bass.ds(n, 1)], rstd[:, bass.ds(n, 1)],
                                      ALU.subtract, ALU.mult).then_inc(xn_done, 1)
                    dve.wait_ge(xn_done, n + 1)
                    dve.wait_ge(score_mm, n + 1 + FREE_BATCH)
                    dve.wait_ge(exp_done, n + 1)
                    dve.scalar_tensor_tensor(z[:, s, :], ps_s[:, s, :], SCALE, xn[:, s, :], ALU.mult, ALU.mult).then_inc(z_scaled, 1)
                    dve.wait_ge(z_scaled, n + 1 + FREE_HALVES)
                    dve.wait_ge(batch_bias, n + 1)
                    dve.tensor_tensor(z[:, s, :], z[:, s, :], both_bias[:, t, :], ALU.add).then_inc(z_done, 1)
                    dve.wait_ge(z_done, n + 1 + FREE_BATCH)
                    dve.tensor_reduce(nmax[:, s:s + 1], z[:, s, :], AX_X, ALU.max, negate=True).then_inc(max_done, 1)
                    dve.wait_ge(exp_done, n + 1 + FREE_HALVES)
                    dve.reciprocal(rinv[:, s:s + 1], rsum[:, s:s + 1]).then_inc(rinv_done, 1)
                    dve.wait_ge(rinv_done, n + 1)
                    dve.scalar_tensor_tensor(tile_of(x_res, n), prob[:, s, :], rinv[:, s:s + 1], tile_of(x_res, n),
                                             ALU.mult, ALU.add).then_inc(x_done, 1)
            dve.wait_ge(x_done, NT + FREE_HALVES)


SUBNORMAL_TOP = 2.0 ** -6
MAGIC = 1.5 * 2.0 ** 20


def exponent_of(dve, e, v, done):
    dve.tensor_scalar(e.bitcast(U32), v.bitcast(U32), 0x7F800000, None, ALU.bitwise_and).then_inc(done, 1)


def rounder_of(dve, e, done):
    dve.tensor_scalar(e, e, SUBNORMAL_TOP, MAGIC, ALU.max, ALU.mult).then_inc(done, 1)


def stage_quantize_weights(nc, sem, d, w_guT, w_dT, scale_rows, ident_b):
    N = 2 * FC
    with ExitStack() as ctx:
        sb, ps, _ = ring(ctx, nc)
        idx = sb("w_idx", [P, FC], I32)
        raw = sb("w_raw", [P, N, D])
        raw_d = sb("w_rawd", [P, KC, FF])
        top = sb("w_top", [P, N + KC])
        scale = sb("w_scale", [P, N + KC])
        inv = sb("w_inv", [P, N + KC])
        scaleT = sb("w_scaleT", [N + KC, P])
        identf = sb("w_identf", [P, P])
        v = sb("w_v", [P, 2, FF])
        e = sb("w_e", [P, 2, FF])
        q = sb("w_q", [P, 2, FF], BF16)
        ps_t = [ps(f"w_pst{s}", [P, 2, 1024], BF16) for s in range(2)]
        ps_st = ps("w_psst", [N + KC, 512])
        scale_dram = nc.dram_tensor("w_scale_rows", [N + KC, P], F32).ap()

        idx_loaded = sem("w_idx_loaded")
        gathered = sem("w_gathered")
        down_loaded = sem("w_down_loaded")
        ids = sem("w_ids")
        maxima = sem("w_maxima")
        scales = sem("w_scales")
        scaleT_mm = sem("w_scaleT_mm")
        scaleT_done = sem("w_scaleT_done")
        scale_stored = sem("w_scale_stored")
        rows_loaded = sem("w_rows_loaded")
        scaled = sem("w_scaled")
        exps = sem("w_exps")
        rounders = sem("w_rounders")
        shifted = sem("w_shifted")
        rounded = sem("w_rounded")
        turned = sem("w_turned")
        kept = sem("w_kept")
        FREE = 2
        PAIRS = FC
        DOWN_PAIRS = KC // 2

        def chunk(i, s, down):
            if down:
                n = 2 * i + s
                return tile_of(raw_d, n), inv[:, bass.ds(N + n, 1)], FF
            n = 2 * i + s
            return tile_of(raw, n), inv[:, bass.ds(n, 1)], D

        block = ctx.enter_context(nc.Block())

        @block.sync
        def _(sp):
            sp.dma_start(idx[:], d["down_idx"].rearrange("(c p) -> p c", p=P), allow_slow_non_contiguous=True).then_inc(idx_loaded, 16)
            sp.dma_start(raw_d[:], d["L0_ffn_w_down"].rearrange("(c p) k -> p c k", p=P)).then_inc(down_loaded, 16)
            sp.wait_ge(scaleT_done, 1)
            sp.dma_start(scale_dram, scaleT[:]).then_inc(scale_stored, 16)
            sp.wait_ge(scale_stored, 16)
            sp.dma_start(scale_rows[:], scale_dram.rearrange("(o c) p -> o (c p)", o=1).broadcast_to([P, (N + KC) * P])).then_inc(rows_loaded, 16)
            sp.wait_ge(rows_loaded, 16)

        @block.gpsimd
        def _(pool):
            pool.wait_ge(idx_loaded, 16)
            for h, w in enumerate(("L0_ffn_w_gate", "L0_ffn_w_up")):
                for c in range(FC):
                    pool.indirect_dma_start(raw[:, h * FC + c, :], None, d[w],
                                            bass.IndirectOffsetOnAxis(ap=idx[:, c:c + 1], axis=0)).then_inc(gathered, 16)
            pool.memset(identf[:], 0.0).then_inc(ids, 1)
            pool.memset(ident_b[:], 0.0).then_inc(ids, 1)
            pool.wait_ge(ids, 2)
            for m in (identf, ident_b):
                pool.affine_select(out=m[:], in_=m[:], compare_op=ALU.not_equal, fill=1.0, base=0,
                                   pattern=[[-1, P]], channel_multiplier=1).then_inc(ids, 1)
            for down, count, seen in ((False, PAIRS, 0), (True, DOWN_PAIRS, 2 * PAIRS)):
                with pool.Fori(0, count) as i:
                    for s in range(2):
                        w = FF if down else D
                        pool.wait_ge(rounders, 2 * i + s + 1 + seen)
                        pool.tensor_tensor(v[:, s, :w], v[:, s, :w], e[:, s, :w], ALU.add).then_inc(shifted, 1)

        @block.scalar
        def _(act):
            def scale_pair(i, down, seen):
                for s in range(2):
                    src, by, w = chunk(i, s, down)
                    act.wait_ge(rounded, 2 * i + s + 1 + seen)
                    act.activation(v[:, s, :w], src, ACT.Copy, scale=by).then_inc(scaled, 1)

            def keep_pair(i, down, seen):
                for s in range(2):
                    act.wait_ge(turned, 2 * i + s + 1 + seen + FREE)
                    if down:
                        for g, (a, b) in enumerate(((0, 8), (8, FC))):
                            out = w_dT[:, a:b, bass.ds((2 * i + s) * P, P)]
                            ins = act.activation(out, ps_t[s][:, g, :(b - a) * P].rearrange("p (c n) -> p c n", n=P), ACT.Copy)
                    else:
                        out = w_guT[:, :, bass.ds((2 * i + s) * P, P)]
                        ins = act.activation(out, ps_t[s][:, 0, :D].rearrange("p (c n) -> p c n", n=P), ACT.Copy)
                    ins.then_inc(kept, 1)

            act.wait_ge(scales, 2)
            for down, count, seen in ((False, PAIRS, 0), (True, DOWN_PAIRS, 2 * PAIRS)):
                scale_pair(0, down, seen)
                with act.Fori(0, count - 1) as i:
                    scale_pair(i + 1, down, seen)
                    keep_pair(i, down, seen)
                keep_pair(count - 1, down, seen)
            act.wait_ge(scaleT_mm, 1)
            act.activation(scaleT[:], ps_st[:, :P], ACT.Copy).then_inc(scaleT_done, 1)

        @block.tensor
        def _(pe):
            pe.wait_ge(ids, 4)
            for down, count, seen in ((False, PAIRS, 0), (True, DOWN_PAIRS, 2 * PAIRS)):
                with pe.Fori(0, count) as i:
                    for s in range(2):
                        pe.wait_ge(rounded, 2 * i + s + 1 + seen + FREE)
                        pe.wait_ge(kept, 2 * i + s + 1 + seen)
                        for c in range(FC if down else KC):
                            ins = pe.transpose(ps_t[s][:, c // 8, (c % 8) * P:(c % 8 + 1) * P], q[:, s, c * P:(c + 1) * P], ident_b[:])
                        ins.then_inc(turned, 1)
            pe.wait_ge(scales, 2)
            pe.transpose(ps_st[:, :P], scale[:], identf[:]).then_inc(scaleT_mm, 1)

        @block.vector
        def _(dve):
            dve.sem_inc(rounded, FREE)
            dve.sem_inc(turned, FREE)
            dve.sem_inc(kept, FREE)
            dve.wait_ge(down_loaded, 16)
            dve.tensor_reduce(top[:, N:], raw_d[:], AX_X, ALU.max, apply_absolute_value=True).then_inc(maxima, 1)
            dve.wait_ge(gathered, 16 * N)
            dve.tensor_reduce(top[:, :N], raw[:], AX_X, ALU.max, apply_absolute_value=True).then_inc(maxima, 1)
            dve.wait_ge(maxima, 2)
            dve.tensor_scalar(scale[:], top[:], 1.0 / FP8_MAX, None, ALU.mult).then_inc(scales, 1)
            dve.wait_ge(scales, 1)
            dve.reciprocal(inv[:], scale[:]).then_inc(scales, 1)
            for down, count, seen in ((False, PAIRS, 0), (True, DOWN_PAIRS, 2 * PAIRS)):
                w = FF if down else D
                with dve.Fori(0, count) as i:
                    for s in range(2):
                        done = 2 * i + s + 1 + seen
                        dve.wait_ge(scaled, done)
                        exponent_of(dve, e[:, s, :w], v[:, s, :w], exps)
                        dve.wait_ge(exps, done)
                        rounder_of(dve, e[:, s, :w], rounders)
                    for s in range(2):
                        done = 2 * i + s + 1 + seen
                        dve.wait_ge(shifted, done)
                        dve.wait_ge(turned, done)
                        dve.tensor_tensor(q[:, s, :w], v[:, s, :w], e[:, s, :w], ALU.subtract).then_inc(rounded, 1)
            dve.wait_ge(rounded, 2 * PAIRS + 2 * DOWN_PAIRS + FREE)


def stage_quantized_gated(nc, sem, d, x_res, mean, rstd, w_guT, w_dT, scale_rows, ident_b):
    with ExitStack() as ctx:
        sb, ps, _ = ring(ctx, nc)
        stats = sb("g_stats", [P, NT, 6])
        mv = sb("g_mv", [P, NT, 2])
        var_eps = sb("g_vareps", [P, NT])
        m_half = sb("g_mhalf", [P, NT])
        v = sb("g_v", [P, 2, D])
        e = sb("g_e", [P, 2, D])
        q = sb("g_q", [P, 2, D], BF16)
        qT = sb("g_qT", [P, 2, KC, P], BF16)
        top = sb("g_top", [P, 2, 4])
        gate = sb("g_gate", [P, 2, FF])
        up = sb("g_up", [P, 2, FF])
        he = sb("g_he", [P, 2, FF])
        hq = sb("g_hq", [P, 2, FF], BF16)
        hqT = sb("g_hqT", [P, 2, FC, P], BF16)
        htop = sb("g_htop", [P, 2, 4])
        y = sb("g_y", [P, 2, D])
        ps_g = ps("g_psg", [P, 3, 512])
        ps_u = ps("g_psu", [P, 3, 512])
        ps_t = ps("g_pst", [P, 1024], BF16)
        ps_y = ps("g_psy", [P, D])

        halves = sem("g_halves")
        stats_done = sem("g_stats_done")
        rstd_done = sem("g_rstd_done")
        centred = sem("g_centred")
        tops = sem("g_tops")
        scaled = sem("g_scaled")
        exps = sem("g_exps")
        rounders = sem("g_rounders")
        shifted = sem("g_shifted")
        rounded = sem("g_rounded")
        turned = sem("g_turned")
        qT_done = sem("g_qT_done")
        gate_mm = sem("g_gate_mm")
        up_mm = sem("g_up_mm")
        gate_out = sem("g_gate_out")
        up_out = sem("g_up_out")
        silu_done = sem("g_silu_done")
        prod_done = sem("g_prod_done")
        htops = sem("g_htops")
        hscaled = sem("g_hscaled")
        hexps = sem("g_hexps")
        hrounders = sem("g_hrounders")
        hshifted = sem("g_hshifted")
        hrounded = sem("g_hrounded")
        hturned = sem("g_hturned")
        hqT_done = sem("g_hqT_done")
        down_mm = sem("g_down_mm")
        y_out = sem("g_y_out")
        x_done = sem("g_x_done")
        FREE = 2
        CH = ((0, 512), (512, 1024), (1024, FF))
        TURNS = ((0, 8), (8, FC))

        def steps(eng, step):
            step(0, 0, first=True)
            with eng.Fori(0, NT // 2 - 1) as i:
                step(2 * i + 1, 1)
                step(2 * i + 2, 0)
            step(NT - 1, 1, last=True)

        block = ctx.enter_context(nc.Block())

        @block.gpsimd
        def _(pool):
            pool.memset(m_half[:], -0.5).then_inc(halves, 1)
            pool.wait_ge(halves, 1)
            pool.wait_ge(stats_done, 2 * NT + 1)
            pool.tensor_tensor(rstd[:], var_eps[:], m_half[:], ALU.pow).then_inc(rstd_done, 1)

            def shift_tokens(n, s):
                pool.wait_ge(rounders, n + 1)
                pool.tensor_tensor(v[:, s, :], v[:, s, :], e[:, s, :], ALU.add).then_inc(shifted, 1)

            def step(n, s, first=False, last=False):
                pool.wait_ge(silu_done, n + 1)
                pool.wait_ge(up_out, n + 1 + FREE)
                pool.tensor_tensor(gate[:, s, :], gate[:, s, :], up[:, s, :], ALU.mult).then_inc(prod_done, 1)
                if not last:
                    shift_tokens(n + 1, 1 - s)
                pool.wait_ge(hrounders, n + 1)
                pool.tensor_tensor(gate[:, s, :], gate[:, s, :], he[:, s, :], ALU.add).then_inc(hshifted, 1)

            shift_tokens(0, 0)
            steps(pool, step)

        @block.scalar
        def _(act):
            def scale_tokens(n, s):
                act.wait_ge(tops, 4 * (n + 1))
                act.activation(v[:, s, :], v[:, s, :], ACT.Copy, scale=top[:, s, 2:3]).then_inc(scaled, 1)

            def keep_qT(n, s):
                act.wait_ge(turned, n + 1)
                act.wait_ge(up_mm, n + 1)
                act.activation(qT[:, s, :, :], ps_t[:, :D].rearrange("p (c n) -> p c n", n=P), ACT.Copy).then_inc(qT_done, 1)

            def keep_hqT(n, s):
                act.wait_ge(down_mm, n + 1)
                for g, (a, b) in enumerate(TURNS):
                    act.wait_ge(hturned, 2 * n + g + 1)
                    act.activation(hqT[:, s, a:b, :], ps_t[:, :(b - a) * P].rearrange("p (c n) -> p c n", n=P), ACT.Copy).then_inc(hqT_done, 1)

            def step(n, s, first=False, last=False):
                act.wait_ge(gate_out, n + 1)
                act.activation(gate[:, s, :], gate[:, s, :], ACT.Silu, scale=top[:, s, 3:4]).then_inc(silu_done, 1)
                if not last:
                    scale_tokens(n + 1, 1 - s)
                if not first:
                    keep_hqT(n - 1, 1 - s)
                if not last:
                    keep_qT(n + 1, 1 - s)
                act.wait_ge(htops, 4 * n + 3)
                act.activation(gate[:, s, :], gate[:, s, :], ACT.Copy, scale=htop[:, s, 2:3]).then_inc(hscaled, 1)

            scale_tokens(0, 0)
            keep_qT(0, 0)
            steps(act, step)
            keep_hqT(NT - 1, 1)

        @block.tensor
        def _(pe):
            def turn_tokens(n, s):
                pe.wait_ge(rounded, n + 1)
                if not (isinstance(n, int) and n < 2):
                    pe.wait_ge(hqT_done, 2 * (n - 1))
                for c in range(KC):
                    ins = pe.transpose(ps_t[:, c * P:(c + 1) * P], q[:, s, c * P:(c + 1) * P], ident_b[:])
                ins.then_inc(turned, 1)

            def hidden(n, s):
                pe.wait_ge(qT_done, n + 1)
                for base, bank, free, done in ((0, ps_g, gate_out, gate_mm), (FF, ps_u, up_out, up_mm)):
                    if free is up_out:
                        pe.wait_ge(free, n + FREE)
                    elif not (isinstance(n, int) and n == 0):
                        pe.wait_ge(free, n)
                    for j, (a, b) in enumerate(CH):
                        for c in range(KC):
                            ins = pe.matmul(bank[:, j, :b - a], qT[:, s, c, :], w_guT[:, c, base + a:base + b],
                                            start=(c == 0), stop=(c == KC - 1))
                    ins.then_inc(done, 1)

            def turn_hidden(n, s):
                pe.wait_ge(hrounded, n + 1)
                for g, (a, b) in enumerate(TURNS):
                    if g:
                        pe.wait_ge(hqT_done, 2 * n + g)
                    for c in range(a, b):
                        ins = pe.transpose(ps_t[:, (c - a) * P:(c - a + 1) * P], hq[:, s, c * P:(c + 1) * P], ident_b[:])
                    ins.then_inc(hturned, 1)

            def down(n, s):
                pe.wait_ge(hqT_done, 2 * n + 2)
                pe.wait_ge(y_out, n + 1)
                for c in range(FC):
                    ins = pe.matmul(ps_y[:], hqT[:, s, c, :], w_dT[:, c, :], start=(c == 0), stop=(c == FC - 1))
                ins.then_inc(down_mm, 1)

            def step(n, s, first=False, last=False):
                hidden(n, s)
                if not first:
                    turn_hidden(n - 1, 1 - s)
                if not last:
                    turn_tokens(n + 1, 1 - s)
                if not first:
                    down(n - 1, 1 - s)

            pe.wait_ge(rounded, 1)
            turn_tokens(0, 0)
            steps(pe, step)
            turn_hidden(NT - 1, 1)
            down(NT - 1, 1)

        @block.vector
        def _(dve):
            dve.sem_inc(up_mm, FREE)
            dve.sem_inc(down_mm, FREE)
            dve.sem_inc(prod_done, 0 + FREE)
            dve.sem_inc(y_out, 1)
            dve.sem_inc(up_out, FREE)
            for n in range(NT):
                dve.bn_stats(stats[:, n, :], x_res[:, n, :]).then_inc(stats_done, 1)
            for n in range(NT):
                dve.wait_ge(stats_done, n + 1)
                dve.bn_aggr(mv[:, n, :], stats[:, n, :]).then_inc(stats_done, 1)
            dve.wait_ge(stats_done, 2 * NT)
            dve.tensor_scalar(var_eps[:], mv[:, :, 1], LN_EPS, None, ALU.add).then_inc(stats_done, 1)
            dve.tensor_copy(mean[:], mv[:, :, 0]).then_inc(stats_done, 1)
            dve.wait_ge(rstd_done, 1)
            dve.wait_ge(stats_done, 2 * NT + 2)

            def col(a, n):
                return a[:, n:n + 1] if isinstance(n, int) else a[:, bass.ds(n, 1)]

            def rows(a, n):
                return a[:, n, :] if isinstance(n, int) else tile_of(a, n)

            def centre(n, s):
                dve.tensor_scalar(v[:, s, :], rows(x_res, n), col(mean, n), None, ALU.subtract).then_inc(centred, 1)
                dve.wait_ge(centred, n + 1)
                dve.tensor_reduce(top[:, s, 0:1], v[:, s, :], AX_X, ALU.max, apply_absolute_value=True).then_inc(tops, 1)
                dve.wait_ge(tops, 4 * n + 1)
                dve.tensor_scalar(top[:, s, 1:2], top[:, s, 0:1], 1.0 / FP8_MAX, None, ALU.mult).then_inc(tops, 1)
                dve.wait_ge(tops, 4 * n + 2)
                dve.reciprocal(top[:, s, 2:3], top[:, s, 1:2]).then_inc(tops, 1)
                dve.tensor_scalar(top[:, s, 3:4], top[:, s, 1:2], col(rstd, n), None, ALU.mult).then_inc(tops, 1)

            def find_rounders(n, s):
                dve.wait_ge(scaled, n + 1)
                exponent_of(dve, e[:, s, :], v[:, s, :], exps)
                dve.wait_ge(exps, n + 1)
                rounder_of(dve, e[:, s, :], rounders)

            def round_tokens(n, s):
                dve.wait_ge(shifted, n + 1)
                dve.tensor_tensor(q[:, s, :], v[:, s, :], e[:, s, :], ALU.subtract).then_inc(rounded, 1)

            def round_hidden(n, s):
                dve.wait_ge(hshifted, n + 1)
                dve.wait_ge(down_mm, n + 1)
                dve.tensor_tensor(hq[:, s, :], gate[:, s, :], he[:, s, :], ALU.subtract).then_inc(hrounded, 1)

            def output(n, s):
                dve.wait_ge(down_mm, n + 1 + FREE)
                dve.tensor_tensor(y[:, s, :], ps_y[:], scale_rows[:, 2 * FF:2 * FF + D], ALU.mult).then_inc(y_out, 1)
                dve.wait_ge(y_out, n + 2)
                dve.wait_ge(htops, 4 * n + 4)
                dve.scalar_tensor_tensor(rows(x_res, n), y[:, s, :], htop[:, s, 3:4], rows(x_res, n), ALU.mult, ALU.add).then_inc(x_done, 1)

            def step(n, s, first=False, last=False):
                dve.wait_ge(gate_mm, n + 1)
                dve.tensor_tensor(gate[:, s, :], ps_g[:].rearrange("p b n -> p (b n)")[:, :FF], scale_rows[:, :FF], ALU.mult).then_inc(gate_out, 1)
                dve.wait_ge(up_mm, n + 1 + FREE)
                dve.wait_ge(prod_done, n + 1)
                dve.tensor_tensor(up[:, s, :], ps_u[:].rearrange("p b n -> p (b n)")[:, :FF], scale_rows[:, FF:2 * FF], ALU.mult).then_inc(up_out, 1)
                if not last:
                    centre(n + 1, 1 - s)
                if not first:
                    round_hidden(n - 1, 1 - s)
                if not last:
                    find_rounders(n + 1, 1 - s)
                dve.wait_ge(prod_done, n + 1 + FREE)
                dve.tensor_reduce(htop[:, s, 0:1], gate[:, s, :], AX_X, ALU.max, apply_absolute_value=True).then_inc(htops, 1)
                if not last:
                    round_tokens(n + 1, 1 - s)
                dve.wait_ge(htops, 4 * n + 1)
                dve.tensor_scalar(htop[:, s, 1:2], htop[:, s, 0:1], 1.0 / FP8_MAX, None, ALU.mult).then_inc(htops, 1)
                dve.wait_ge(htops, 4 * n + 2)
                dve.reciprocal(htop[:, s, 2:3], htop[:, s, 1:2]).then_inc(htops, 1)
                dve.tensor_scalar(htop[:, s, 3:4], htop[:, s, 1:2], top[:, s, 3:4], None, ALU.mult).then_inc(htops, 1)
                if not first:
                    output(n - 1, 1 - s)
                dve.wait_ge(hscaled, n + 1)
                exponent_of(dve, he[:, s, :], gate[:, s, :], hexps)
                dve.wait_ge(hexps, n + 1)
                rounder_of(dve, he[:, s, :], hrounders)

            centre(0, 0)
            find_rounders(0, 0)
            round_tokens(0, 0)
            steps(dve, step)
            round_hidden(NT - 1, 1)
            output(NT - 1, 1)
            dve.wait_ge(x_done, NT)

H = 16
HP = H // 2
R = 64
CQ = 384
QC = CQ // P
NP_ = B * HP
HALF = R


def scratch(nc, name, shape):
    return nc.dram_tensor(name, shape, F32).ap()


def one(a, n):
    names = "bcdefg"[:len(a.shape) - 1]
    spaced = " ".join(names)
    return a[bass.ds(n, 1)].rearrange(f"a {spaced} -> (a {names[0]}) {spaced[2:]}") if not isinstance(n, int) else a[n]


def stage_prepare_heads(nc, sem, d, scr, x_res, mean, rstd, ident, out_w):
    with ExitStack() as ctx:
        sb, ps, _ = ring(ctx, nc)
        kv = sb("p_kv", [P, NT, DC])
        cos = sb("p_cos", [P, TPB, DC])
        sin = sb("p_sin", [P, TPB, DC])
        rot = sb("p_rot", [P, TPB, DC])
        kvs = sb("p_kvs", [P, 2, TPB, DC], F32R)
        kvTs = sb("p_kvTs", [P, 2, S], F32R)
        wkr = sb("p_wkr", [P, H, 2, R])
        wkrs = sb("p_wkrs", [P, HP, 2, 2, P], F32R)
        cqT = sb("p_cqT", [P, 2, QC, P])
        wqr = sb("p_wqr", [P, 2, QC, R])
        wq = sb("p_wq", [P, 2, D])
        wkv = sb("p_wkv", [P, 2, DC])
        woT = sb("p_woT", [P, 2, D])
        mid = sb("p_mid", [P, 2, R])
        a_hl = sb("p_a", [P, KC, 2, P], F32R)
        xn = sb("p_xn", [P, 2, D])
        xT = sb("p_xT", [P, 2, KC, 2, P], F32R)
        stats = sb("p_stats", [P, NT, 6])
        mv = sb("p_mv", [P, NT, 2])
        var_eps = sb("p_vareps", [P, NT])
        m_half = sb("p_mhalf", [P, NT])
        ps_m = ps("p_psm", [P, 2, 512])
        ps_a = ps("p_psa", [P, KC, 2, R])
        ps_b = ps("p_psb", [P, 2, D])
        ps_t = ps("p_pst", [P, 2, 512])

        kv_loaded = sem("p_kv_loaded")
        kr_loaded = sem("p_kr_loaded")
        rope_done = sem("p_rope_done")
        kv_hi = sem("p_kv_hi")
        kv_lo = sem("p_kv_lo")
        kv_turned = sem("p_kv_turned")
        kvT_hi = sem("p_kvT_hi")
        kvT_lo = sem("p_kvT_lo")
        kv_stored = sem("p_kv_stored")
        kr_hi = sem("p_kr_hi")
        kr_lo = sem("p_kr_lo")
        w_loaded = [sem(f"p_w_loaded{s}") for s in range(2)]
        mid_mm = sem("p_mid_mm")
        mid_done = sem("p_mid_done")
        a_mm = sem("p_a_mm")
        a_hi = sem("p_a_hi")
        a_lo = sem("p_a_lo")
        a_stored = sem("p_a_stored")
        b_mm = sem("p_b_mm")
        b_hi = sem("p_b_hi")
        b_lo = sem("p_b_lo")
        halves = sem("p_halves")
        stats_done = sem("p_stats_done")
        rstd_done = sem("p_rstd_done")
        normed = sem("p_normed")
        x_turned = sem("p_x_turned")
        x_hi = sem("p_x_hi")
        x_lo = sem("p_x_lo")
        xT_stored = [sem(f"p_xT_stored{s}") for s in range(2)]
        x_stored = sem("p_x_stored")

        block = ctx.enter_context(nc.Block())

        @block.sync
        def _(sp):
            sp.dma_start(kv[:], d["ctx"].rearrange("(n p) c -> p n c", p=P)).then_inc(kv_loaded, 16)
            sp.dma_start(cos[:], d["rope_cos"].rearrange("(n p) c -> p n c", p=P)).then_inc(kv_loaded, 16)
            sp.dma_start(sin[:], d["rope_sin"].rearrange("(n p) c -> p n c", p=P)).then_inc(kv_loaded, 16)
            for j in range(2):
                sp.dma_start(wkr[:, :, j, :], d["W_krT"].rearrange("c (h r) -> c h r", r=R)).then_inc(kr_loaded, 16)
            sp.dma_start(scr["x2"].rearrange("(n p) c -> p n c", p=P), x_res[:]).then_inc(x_stored, 16)

            def load_head(i, s):
                h = 2 * i + s
                sp.dma_start(cqT[:, s, :, :], one(d["w_kc_qT"], h).rearrange("(c p) k -> p c k", p=P)).then_inc(w_loaded[s], 16)
                sp.dma_start(wqr[:, s, :, :], one(d["W_qr"], h).rearrange("(c p) r -> p c r", p=P)).then_inc(w_loaded[s], 16)
                sp.dma_start(wq[:, s, :], one(d["L1_Wq"], h)).then_inc(w_loaded[s], 16)
                sp.dma_start(wkv[:, s, :], one(d["w_kc_kv"], h)).then_inc(w_loaded[s], 16)
                sp.dma_start(woT[:, s, :], one(d["WoT"], h)).then_inc(w_loaded[s], 16)

            for s in range(2):
                load_head(0, s)
            for b in range(B):
                sp.wait_ge(kv_lo, b + 1)
                sp.dma_start(scr["kv"][b], kvs[:].rearrange("p a t c -> p (a t c)").bitcast(F32)).then_inc(kv_stored, 16)
                sp.wait_ge(kvT_lo, b + 1)
                sp.dma_start(scr["kvT"][b], kvTs[:].rearrange("p a l -> p (a l)").bitcast(F32)).then_inc(kv_stored, 16)
            sp.wait_ge(kr_lo, 2)
            sp.dma_start(scr["kr"].rearrange("g p n -> p g n"), wkrs[:].rearrange("p g h a n -> p g (h a n)").bitcast(F32)).then_inc(kv_stored, 16)
            with sp.Fori(0, HP - 1) as i:
                for s in range(2):
                    sp.wait_ge(a_mm, i + 2)
                    load_head(i + 1, s)
                sp.wait_ge(a_lo, i + 2)
                sp.dma_start(one(scr["a"], i), a_hl[:].rearrange("p c a n -> p (c a n)").bitcast(F32)).then_inc(a_stored, 16)
            sp.wait_ge(a_lo, HP + 1)
            sp.dma_start(scr["a"][HP - 1], a_hl[:].rearrange("p c a n -> p (c a n)").bitcast(F32)).then_inc(a_stored, 16)
            xT_dram = scr["xT"].rearrange("b p (c a t n) -> b t p c a n", c=KC, a=2, t=TPB)
            with sp.Fori(0, B) as b:
                for t in range(TPB):
                    sp.wait_ge(x_lo, TPB * b + t + 1 + 2)
                    sp.dma_start(one(xT_dram, b)[t].rearrange("p c a n -> p (c a) n"),
                                 xT[:, t % 2].rearrange("p c a n -> p (c a) n").bitcast(F32)).then_inc(xT_stored[t % 2], 16)
            sp.wait_ge(x_stored, 16)
            sp.wait_ge(kv_stored, 16 * (2 * B + 1))
            sp.wait_ge(a_stored, 16 * (HP + 1))
            for s in range(2):
                sp.wait_ge(xT_stored[s], 16 * (NT // 2 + 1))

        @block.gpsimd
        def _(pool):
            pool.memset(m_half[:], -0.5).then_inc(halves, 1)
            pool.wait_ge(kv_loaded, 48)
            for b in range(B):
                rows = kv[:, TPB * b:TPB * (b + 1), :]
                if b:
                    pool.wait_ge(rope_done, 4 * b)
                pool.tensor_tensor(rot[:, :, :DC // 2], rows[:, :, DC // 2:], sin[:, :, :DC // 2], ALU.mult).then_inc(rope_done, 1)
                pool.tensor_tensor(rot[:, :, DC // 2:], rows[:, :, :DC // 2], sin[:, :, DC // 2:], ALU.mult).then_inc(rope_done, 1)
                pool.wait_ge(rope_done, 4 * b + 2)
                pool.tensor_tensor(rows, rows, cos[:], ALU.mult).then_inc(rope_done, 1)
                pool.wait_ge(rope_done, 4 * b + 3)
                pool.tensor_tensor(rows, rows, rot[:], ALU.add).then_inc(rope_done, 1)
            pool.wait_ge(halves, 1)
            pool.wait_ge(stats_done, 2 * NT + 1)
            pool.tensor_tensor(rstd[:], var_eps[:], m_half[:], ALU.pow).then_inc(rstd_done, 1)

        @block.tensor
        def _(pe):
            for b in range(B):
                pe.wait_ge(rope_done, 4 * b + 4)
                if b >= 2:
                    pe.wait_ge(kvT_lo, b - 1)
                for t in range(TPB):
                    ins = pe.transpose(ps_t[:, b % 2, t * P:(t + 1) * P], kv[:, TPB * b + t, :], ident[:])
                ins.then_inc(kv_turned, 1)
            with pe.Fori(0, HP) as i:
                for s in range(2):
                    pe.wait_ge(w_loaded[s], 80 * (i + 1))
                    pe.wait_ge(mid_done, 2 * i + s + 1)
                    for c in range(QC):
                        ins = pe.matmul(ps_m[:, s, :R], cqT[:, s, c, :], wqr[:, s, c, :], start=(c == 0), stop=(c == QC - 1))
                    ins.then_inc(mid_mm, 1)
                for s in range(2):
                    pe.wait_ge(b_lo, 2 * i + s + 1)
                    pe.matmul(ps_b[:, s, :], wkv[:, s, :], woT[:, s, :], start=True, stop=True).then_inc(b_mm, 1)
                pe.wait_ge(a_lo, i + 1)
                for s in range(2):
                    pe.wait_ge(mid_done, 2 * i + s + 1 + 2)
                    for c in range(KC):
                        ins = pe.matmul(ps_a[:, c, s, :], wq[:, s, c * P:(c + 1) * P], mid[:, s, :], start=True, stop=True)
                ins.then_inc(a_mm, 1)
            with pe.Fori(0, B) as b:
                for t in range(TPB):
                    pe.wait_ge(normed, TPB * b + t + 1)
                    pe.wait_ge(x_lo, TPB * b + t + 1)
                    for c in range(KC):
                        ins = pe.transpose(ps_t[:, t % 2, c * P:(c + 1) * P], xn[:, t % 2, c * P:(c + 1) * P], ident[:])
                    ins.then_inc(x_turned, 1)

        @block.scalar
        def _(act):
            for b in range(B):
                act.wait_ge(rope_done, 4 * b + 4)
                if b:
                    act.wait_ge(kv_stored, 32 * b)
                act.activation(kvs[:, 0], kv[:, TPB * b:TPB * (b + 1), :], ACT.Copy).then_inc(kv_hi, 1)
                act.wait_ge(kv_turned, b + 1)
                act.activation(kvTs[:, 0, :], ps_t[:, b % 2, :], ACT.Copy).then_inc(kvT_hi, 1)
            act.wait_ge(kr_loaded, 32)
            for h in range(2):
                act.activation(wkrs[:, :, h, 0, :], wkr[:].rearrange("p (g h) j r -> p h g (j r)", h=2)[:, h], ACT.Copy).then_inc(kr_hi, 1)
            with act.Fori(0, HP) as i:
                for s in range(2):
                    act.wait_ge(mid_mm, 2 * i + s + 1)
                    act.wait_ge(a_mm, i + 1)
                    act.activation(mid[:, s, :], ps_m[:, s, :R], ACT.Copy).then_inc(mid_done, 1)
                for s in range(2):
                    act.wait_ge(b_mm, 2 * i + s + 1)
                    act.activation(out_w[:, bass.ds(2 * i + s, 1), 0, :].rearrange("p o n -> p (o n)"), ps_b[:, s, :], ACT.Copy).then_inc(b_hi, 1)
                act.wait_ge(a_mm, i + 2)
                act.wait_ge(a_stored, 16 * (i + 1))
                act.activation(a_hl[:, :, 0, :], ps_a[:].rearrange("p c s r -> p c (s r)"), ACT.Copy).then_inc(a_hi, 1)
            with act.Fori(0, B) as b:
                for t in range(TPB):
                    act.wait_ge(x_turned, TPB * b + t + 1 + 2)
                    act.wait_ge(xT_stored[t % 2], 16 * (2 * b + t // 2 + 1))
                    act.activation(xT[:, t % 2, :, 0, :], ps_t[:, t % 2, :].rearrange("p (c n) -> p c n", n=P), ACT.Copy).then_inc(x_hi, 1)

        @block.vector
        def _(dve):
            dve.sem_inc(mid_done, 2)
            dve.sem_inc(b_lo, 2)
            dve.sem_inc(a_lo, 1)
            dve.sem_inc(a_mm, 1)
            dve.sem_inc(a_stored, 16)
            dve.sem_inc(x_lo, 2)
            dve.sem_inc(x_turned, 2)
            for s in range(2):
                dve.sem_inc(xT_stored[s], 16)
            for n in range(NT):
                dve.bn_stats(stats[:, n, :], x_res[:, n, :]).then_inc(stats_done, 1)
            for n in range(NT):
                dve.wait_ge(stats_done, n + 1)
                dve.bn_aggr(mv[:, n, :], stats[:, n, :]).then_inc(stats_done, 1)
            dve.wait_ge(stats_done, 2 * NT)
            dve.tensor_scalar(var_eps[:], mv[:, :, 1], LN_EPS, None, ALU.add).then_inc(stats_done, 1)
            dve.tensor_copy(mean[:], mv[:, :, 0]).then_inc(stats_done, 1)
            for b in range(B):
                dve.wait_ge(kv_hi, b + 1)
                if b:
                    dve.wait_ge(kv_stored, 32 * b)
                dve.tensor_tensor(kvs[:, 1], kv[:, TPB * b:TPB * (b + 1), :], kvs[:, 0].bitcast(F32), ALU.subtract).then_inc(kv_lo, 1)
                dve.wait_ge(kvT_hi, b + 1)
                dve.tensor_tensor(kvTs[:, 1, :], ps_t[:, b % 2, :], kvTs[:, 0, :].bitcast(F32), ALU.subtract).then_inc(kvT_lo, 1)
            for h in range(2):
                dve.wait_ge(kr_hi, h + 1)
                dve.tensor_tensor(wkrs[:, :, h, 1, :], wkr[:].rearrange("p (g h) j r -> p h g (j r)", h=2)[:, h],
                                  wkrs[:, :, h, 0, :].bitcast(F32), ALU.subtract).then_inc(kr_lo, 1)
            with dve.Fori(0, HP) as i:
                for s in range(2):
                    dve.wait_ge(b_hi, 2 * i + s + 1)
                    dve.tensor_tensor(out_w[:, bass.ds(2 * i + s, 1), 1, :].rearrange("p o n -> p (o n)"), ps_b[:, s, :],
                                      out_w[:, bass.ds(2 * i + s, 1), 0, :].rearrange("p o n -> p (o n)").bitcast(F32), ALU.subtract).then_inc(b_lo, 1)
                dve.wait_ge(a_hi, i + 1)
                dve.tensor_tensor(a_hl[:, :, 1, :], ps_a[:].rearrange("p c s r -> p c (s r)"), a_hl[:, :, 0, :].bitcast(F32), ALU.subtract).then_inc(a_lo, 1)
            dve.wait_ge(rstd_done, 1)
            dve.wait_ge(stats_done, 2 * NT + 2)

            def norm(b, t):
                n = TPB * b + t
                dve.wait_ge(x_turned, n + 1)
                dve.tensor_scalar(xn[:, t % 2, :], tile_of(x_res, n), mean[:, bass.ds(n, 1)], rstd[:, bass.ds(n, 1)],
                                  ALU.subtract, ALU.mult).then_inc(normed, 1)
            with dve.Fori(0, B) as b:
                for t in range(TPB):
                    n = TPB * b + t
                    if t == 0:
                        norm(b, 0)
                    if t < TPB - 1:
                        norm(b, t + 1)
                    dve.wait_ge(x_hi, n + 1)
                    dve.wait_ge(xT_stored[t % 2], 16 * (2 * b + t // 2 + 1))
                    dve.tensor_tensor(xT[:, t % 2, :, 1, :], ps_t[:, t % 2, :].rearrange("p (c n) -> p c n", n=P),
                                      xT[:, t % 2, :, 0, :].bitcast(F32), ALU.subtract).then_inc(x_lo, 1)


def after(eng, sem, value):
    if not isinstance(value, int) or value > 0:
        eng.wait_ge(sem, value)


def stage_latent_attention(nc, sem, scr, x_out, ident, out_w):
    UNITS, HEADS, ITERS = 32, 8, B * H // 8
    TURN_LAG, PV_LAG, OUT_LAG = 2, 6, 23
    QUAD = 4
    with ExitStack() as ctx:
        sb, ps, _ = ring(ctx, nc)
        a_w = sb("l_aw", [P, 2, KC, 2, P], F32R)
        kr_w = sb("l_krw", [P, 2, 2, 2, P], F32R)
        xT = sb("l_xT", [P, KC, 2, S], F32R)
        kvT = sb("l_kvT", [P, 2, S], F32R)
        kv = sb("l_kv", [P, 2, TPB, DC], F32R)
        q_st = sb("l_qst", [P, 2, 2, S], F32R)
        k_st = sb("l_kst", [P, 2, 2, 2, S], F32R)
        prob = sb("l_prob", [P, 4, S])
        pT = sb("l_pT", [P, 2, 2, TPB, S], F32R)
        cT = sb("l_cT", [P, HEADS, 2, S], F32R)
        acc = sb("l_acc", [P, TPB, D])
        nmax = sb("l_nmax", [P, 4])
        rsum = sb("l_rsum", [P, 4])
        rinv = sb("l_rinv", [P, 4])
        ps_s = ps("l_pss", [P, 2, S])
        ps_p = ps("l_psp", [P, 2, S])
        ps_qk = ps("l_psqk", [P, S])
        ps_c = ps("l_psc", [P, 2, S])
        ps_o = ps("l_pso", [P, D])

        w_loaded = [sem(f"l_w_loaded{s}") for s in range(2)]
        xT_loaded = [sem(f"l_xT_loaded{c}") for c in range(KC)]
        kvT_loaded = sem("l_kvT_loaded")
        kv_loaded = sem("l_kv_loaded")
        acc_loaded = [sem(f"l_acc_loaded{t}") for t in range(TPB)]
        acc_stored = [sem(f"l_acc_stored{t}") for t in range(TPB)]
        q_mm = sem("l_q_mm")
        k_mm = sem("l_k_mm")
        st_hi = sem("l_st_hi")
        st_lo = sem("l_st_lo")
        s_mm = sem("l_s_mm")
        max_done = sem("l_max_done")
        exp_done = sem("l_exp_done")
        rinv_done = sem("l_rinv_done")
        normed = sem("l_normed")
        turned = sem("l_turned")
        pT_hi = sem("l_pT_hi")
        pT_lo = sem("l_pT_lo")
        c_mm = sem("l_c_mm")
        c_hi = sem("l_c_hi")
        c_lo = sem("l_c_lo")
        out_mm = sem("l_out_mm")
        added = sem("l_added")

        def flat(a):
            letters = "bcdefg"[:len(a.shape) - 1]
            return a.rearrange(f"p {' '.join(letters)} -> p ({' '.join(letters)})").bitcast(F32)

        def iterations(eng, unit, tail):
            for j in range(UNITS):
                unit(0, j)
            with eng.Fori(1, ITERS - 1) as n:
                for j in range(UNITS):
                    unit(n, j)
            for j in range(UNITS):
                unit(ITERS - 1, j)
            for j in range(UNITS, UNITS + tail):
                unit(ITERS - 1, j)

        def lagged(n, j, lag):
            at = j - lag
            if isinstance(n, int) and n == 0 and at < 0:
                return None
            if at >= UNITS:
                return None
            return at

        def next_pair(n, j):
            if j >= UNITS or (isinstance(n, int) and n == ITERS - 1 and j >= UNITS - 8):
                return None
            return n * 4 + j // 8 + 1, (j // 8 + 1) % 2

        def out_step(n, j):
            at = j - OUT_LAG
            if isinstance(n, int) and n == 0 and at < 0:
                return None
            quad, i = at // 16, at % 16
            if isinstance(n, int) and n == ITERS - 1 and quad > 1:
                return None
            return quad, i // 4, i % 4

        block = ctx.enter_context(nc.Block())

        @block.sync
        def _(sp):
            def load_pair(p, slot, h):
                sp.dma_start(flat(a_w[:, slot]), one(scr["a"], h)).then_inc(w_loaded[slot], 16)
                sp.dma_start(flat(kr_w[:, slot]), one(scr["kr"], h)).then_inc(w_loaded[slot], 16)

            def load_tokens(b):
                for c in range(KC):
                    sp.dma_start(flat(xT[:, c]), one(scr["xT"], b)[:, c * 2 * S:(c + 1) * 2 * S]).then_inc(xT_loaded[c], 16)

            def load_keys(b):
                sp.dma_start(flat(kvT), one(scr["kvT"], b)).then_inc(kvT_loaded, 16)

            x2 = scr["x2"].rearrange("(b t p) c -> b t p c", b=B, p=P)
            x3 = x_out.rearrange("(b t p) c -> b t p c", b=B, p=P)

            load_pair(0, 0, 0)
            load_tokens(0)
            load_keys(0)
            load_pair(1, 1, 1)
            sp.dma_start(flat(kv), scr["kv"][0]).then_inc(kv_loaded, 16)
            for t in range(TPB):
                sp.dma_start(acc[:, t, :], x2[0, t]).then_inc(acc_loaded[t], 16)

            def batch(b, first=False, last=False):
                if not first:
                    sp.wait_ge(c_mm, H * b)
                    sp.dma_start(flat(kv), one(scr["kv"], b)).then_inc(kv_loaded, 16)
                for p in range(HP):
                    if p == HP - 1 and not last:
                        sp.wait_ge(q_mm, HP * (b + 1))
                        load_tokens(b + 1)
                    if not (last and p >= HP - 2):
                        sp.wait_ge(k_mm, 2 * (HP * b + p + 1))
                        load_pair(None, p % 2, (p + 2) % HP)
                    if p == HP - 1 and not last:
                        load_keys(b + 1)
                    if not first and p in (1, 2):
                        for t in (2 * p - 2, 2 * p - 1):
                            swap(b, t)

            def swap(b, t):
                sp.wait_ge(added, (4 * b - 1) * TPB + t + 1)
                sp.dma_start(one(x3, b - 1)[t], acc[:, t, :]).then_inc(acc_stored[t], 16)
                sp.wait_ge(acc_stored[t], 16 * b)
                sp.dma_start(acc[:, t, :], one(x2, b)[t]).then_inc(acc_loaded[t], 16)

            batch(0, first=True)
            with sp.Fori(1, B - 1) as b:
                batch(b)
            batch(B - 1, last=True)
            for t in range(TPB):
                sp.wait_ge(added, (4 * B - 1) * TPB + t + 1)
                sp.dma_start(x3[B - 1, t], acc[:, t, :]).then_inc(acc_stored[t], 16)
            for t in range(TPB):
                sp.wait_ge(acc_stored[t], 16 * B)

        @block.gpsimd
        def _(pool):
            def unit(n, j):
                if j < UNITS:
                    pool.wait_ge(rinv_done, UNITS * n + j + 1)
                    pool.tensor_tensor(prob[:, j % 4, :], prob[:, j % 4, :], rinv[:, j % 4:j % 4 + 1].broadcast_to([P, S]), ALU.mult).then_inc(normed, 1)
            iterations(pool, unit, 0)

        @block.tensor
        def _(pe):
            def queries(p, slot, c):
                if c == 0:
                    after(pe, st_lo, 4 * p)
                    pe.wait_ge(w_loaded[slot], 32 * (p // 2 + 1))
                pe.wait_ge(xT_loaded[c], 16 * (p // HP + 1))
                for m, (x, y) in enumerate(((0, 0), (0, 1), (1, 0))):
                    ins = pe.matmul(ps_qk[:], a_w[:, slot, c, x, :], xT[:, c, y, :], start=(c == 0 and m == 0), stop=(c == KC - 1 and m == 2))
                if c == KC - 1:
                    ins.then_inc(q_mm, 1)

            def keys(p, slot, h):
                pe.wait_ge(st_lo, 4 * p + 2 + h)
                pe.wait_ge(kvT_loaded, 16 * (p // HP + 1))
                for m, (x, y) in enumerate(((0, 0), (0, 1), (1, 0))):
                    ins = pe.matmul(ps_qk[:], kr_w[:, slot, h, x, :], kvT[:, y, :], start=(m == 0), stop=(m == 2))
                ins.then_inc(k_mm, 1)

            def unit(n, j):
                u = UNITS * n + j
                if j < UNITS:
                    pair, h, t = j // 8, j // 4 % 2, j % 4
                    if t == 0:
                        pe.wait_ge(st_lo, 4 * (4 * n + pair) + 3 + h)
                    after(pe, exp_done, u - 1)
                    for x in range(2):
                        ins = pe.matmul(ps_s[:, j % 2, :], q_st[:, pair % 2, h, t * P:(t + 1) * P], k_st[:, pair % 2, h, x, :],
                                        start=(x == 0), stop=(x == 1))
                    ins.then_inc(s_mm, 1)
                if (at := lagged(n, j, TURN_LAG)) is not None:
                    pe.wait_ge(normed, u - TURN_LAG + 1)
                    after(pe, pT_lo, u - TURN_LAG - 1)
                    for c in range(TPB):
                        ins = pe.transpose(ps_p[:, at % 2, c * P:(c + 1) * P], prob[:, at % 4, c * P:(c + 1) * P], ident[:])
                    ins.then_inc(turned, 1)
                if (at := lagged(n, j, PV_LAG)) is not None:
                    c = at % 4
                    g = HEADS * n + at // 4
                    slot = (at // 4) % 2
                    if c == 0:
                        pe.wait_ge(pT_lo, 4 * g + 4)
                        after(pe, c_lo, g - 1)
                        pe.wait_ge(kv_loaded, 16 * (g // H + 1))
                    for m, (x, y) in enumerate(((0, 0), (0, 1), (1, 0))):
                        ins = pe.matmul(ps_c[:, slot, :], kv[:, x, c, :], pT[:, slot, y, c, :],
                                        start=(c == 0 and m == 0), stop=(c == TPB - 1 and m == 2))
                    if c == TPB - 1:
                        ins.then_inc(c_mm, 1)
                if (at := out_step(n, j)) is not None:
                    quad, t, k = at
                    q_index = UNITS // 16 * n + quad
                    if t == 0:
                        pe.wait_ge(c_lo, QUAD * q_index + k + 1)
                    if k == 0:
                        after(pe, added, TPB * q_index + t)
                    slot = (QUAD * quad + k) % HEADS
                    g = (QUAD * (q_index % (H // QUAD))) + k
                    for m, (x, y) in enumerate(((0, 0), (0, 1), (1, 0))):
                        w = out_w[:, g, y, :] if isinstance(g, int) else out_w[:, bass.ds(g, 1), y, :].rearrange("p o n -> p (o n)")
                        ins = pe.matmul(ps_o[:], cT[:, slot, x, t * P:(t + 1) * P], w, start=(k == 0 and m == 0), stop=(k == QUAD - 1 and m == 2))
                    if k == QUAD - 1:
                        ins.then_inc(out_mm, 1)
                if (np := next_pair(n, j)) is not None:
                    p, slot = np
                    prepare(p, slot, j % 8)

            def prepare(p, slot, i):
                if i < KC:
                    queries(p, slot, i)
                elif i in (5, 6):
                    keys(p, slot, i - 5)

            for i in range(8):
                prepare(0, 0, i)
            iterations(pe, unit, OUT_LAG)

        @block.scalar
        def _(act):
            def keep_queries(p, slot):
                act.wait_ge(q_mm, p + 1)
                after(act, s_mm, 8 * (p - 1))
                for h in range(2):
                    rows = slice(h * R, (h + 1) * R)
                    act.activation(q_st[rows, slot, h, :], ps_qk[rows, :], ACT.Copy).then_inc(st_hi, 1)

            def keep_keys(p, slot, h):
                act.wait_ge(k_mm, 2 * p + h + 1)
                act.activation(k_st[:, slot, h, 0, :], ps_qk[:], ACT.Copy).then_inc(st_hi, 1)

            def prepare(p, slot, i):
                if i == 4:
                    keep_queries(p, slot)
                if i in (6, 7):
                    keep_keys(p, slot, i - 6)

            def unit(n, j):
                u = UNITS * n + j
                if (at := lagged(n, j, TURN_LAG)) is not None:
                    act.wait_ge(turned, u - TURN_LAG + 1)
                    g = HEADS * n + at // 4
                    if at % 4 == 0:
                        after(act, c_mm, g - 1)
                    act.activation(pT[:, (at // 4) % 2, 0, :, (at % 4) * P:(at % 4 + 1) * P],
                                   ps_p[:, at % 2, :].rearrange("p (c n) -> p c n", n=P), ACT.Copy).then_inc(pT_hi, 1)
                if j < UNITS:
                    act.wait_ge(max_done, u + 1)
                    after(act, turned, u - 3)
                    act.activation(prob[:, j % 4, :], ps_s[:, j % 2, :], ACT.Exp, bias=nmax[:, j % 4:j % 4 + 1],
                                   accum_out=rsum[:, j % 4:j % 4 + 1]).then_inc(exp_done, 1)
                if j % 4 == 2 and (at := lagged(n, j, PV_LAG + 4)) is not None:
                    g = HEADS * n + at // 4
                    act.wait_ge(c_mm, g + 1)
                    after(act, out_mm, TPB * (UNITS // 16 * n + at // 16))
                    act.activation(cT[:, (at // 4) % HEADS, 0, :], ps_c[:, (at // 4) % 2, :], ACT.Copy).then_inc(c_hi, 1)
                if (np := next_pair(n, j)) is not None:
                    prepare(np[0], np[1], j % 8)

            for i in range(8):
                prepare(0, 0, i)
            iterations(act, unit, PV_LAG + 5)

        @block.vector
        def _(dve):
            def keep_queries(p, slot):
                for h in range(2):
                    rows, other = slice(h * R, (h + 1) * R), slice((1 - h) * R, (2 - h) * R)
                    dve.wait_ge(st_hi, 4 * p + h + 1)
                    dve.tensor_tensor(q_st[other, slot, h, :], ps_qk[rows, :], q_st[rows, slot, h, :].bitcast(F32), ALU.subtract).then_inc(st_lo, 1)

            def keep_keys(p, slot, h):
                dve.wait_ge(st_hi, 4 * p + 3 + h)
                dve.tensor_tensor(k_st[:, slot, h, 1, :], ps_qk[:], k_st[:, slot, h, 0, :].bitcast(F32), ALU.subtract).then_inc(st_lo, 1)

            def prepare(p, slot, i):
                if i == 4:
                    keep_queries(p, slot)
                if i in (6, 7):
                    keep_keys(p, slot, i - 6)

            def invert(n, j):
                dve.wait_ge(exp_done, UNITS * n + j + 1)
                dve.reciprocal(rinv[:, j % 4:j % 4 + 1], rsum[:, j % 4:j % 4 + 1]).then_inc(rinv_done, 1)

            def unit(n, j):
                u = UNITS * n + j
                if (at := lagged(n, j, 1)) is not None:
                    invert(n, at)
                if j < UNITS:
                    dve.wait_ge(s_mm, u + 1)
                    dve.tensor_reduce(nmax[:, j % 4:j % 4 + 1], ps_s[:, j % 2, :], AX_X, ALU.max, negate=True).then_inc(max_done, 1)
                if (at := lagged(n, j, TURN_LAG)) is not None:
                    dve.wait_ge(pT_hi, u - TURN_LAG + 1)
                    slot, cols = (at // 4) % 2, slice((at % 4) * P, (at % 4 + 1) * P)
                    dve.tensor_tensor(pT[:, slot, 1, :, cols], ps_p[:, at % 2, :].rearrange("p (c n) -> p c n", n=P),
                                      pT[:, slot, 0, :, cols].bitcast(F32), ALU.subtract).then_inc(pT_lo, 1)
                if j % 4 == 2 and (at := lagged(n, j, PV_LAG + 4)) is not None:
                    g = HEADS * n + at // 4
                    dve.wait_ge(c_hi, g + 1)
                    slot = (at // 4) % HEADS
                    dve.tensor_tensor(cT[:, slot, 1, :], ps_c[:, (at // 4) % 2, :], cT[:, slot, 0, :].bitcast(F32), ALU.subtract).then_inc(c_lo, 1)
                if j % 4 == 3 and (at := out_step(n, j - 1)) is not None:
                    quad, t, _ = at
                    q_index = UNITS // 16 * n + quad
                    dve.wait_ge(out_mm, TPB * q_index + t + 1 + TPB)
                    dve.wait_ge(acc_loaded[t], 16 * (q_index // (H // QUAD) + 1))
                    dve.wait_ge(added, TPB * q_index + t) if not isinstance(n, int) or n or quad or t else None
                    dve.tensor_tensor(acc[:, t, :], ps_o[:], acc[:, t, :], ALU.add).then_inc(added, 1)
                if (np := next_pair(n, j)) is not None:
                    prepare(np[0], np[1], j % 8)

            dve.sem_inc(out_mm, TPB)
            for i in range(8):
                prepare(0, 0, i)
            iterations(dve, unit, OUT_LAG + 1)

E = 32
RE = 16
TOP = 2


def stage_routed_experts(nc, sem, d, x_in, out, ident):
    with ExitStack() as ctx:
        sb, ps, _ = ring(ctx, nc)
        raw_u = sb("e_rawu", [P, KC, E * RE])
        raw_v = sb("e_rawv", [P, KC, D])
        raw_r = sb("e_rawr", [P, KC, E])
        u_w = sb("e_uw", [P, KC, 2, E * RE], F32R)
        v_w = sb("e_vw", [P, KC, 2, D], F32R)
        r_w = sb("e_rw", [P, KC, 2, E], F32R)
        attr = sb("e_attr", [P, E, 32])
        wa = sb("e_wa", [P, 32])
        aw = sb("e_aw", [P, 4, E])
        order = sb("e_order", [P, E])
        eps = sb("e_eps", [P, 2])
        x = sb("e_x", [P, NT, D])
        xn = sb("e_xn", [P, D])
        stats = sb("e_stats", [P, 2, 6])
        mv = sb("e_mv", [P, 2, 2])
        var_eps = sb("e_vareps", [P, 2])
        rstd = sb("e_rstd", [P, 2])
        xT = sb("e_xT", [P, 2, KC, 2, P], F32R)
        sc = sb("e_sc", [P, 2, E])
        best = sb("e_best", [P, 2, 8])
        which = sb("e_which", [P, 2, 8], U32)
        whichf = sb("e_whichf", [P, 2, TOP])
        nbest = sb("e_nbest", [P, 2])
        g = sb("e_g", [P, 2, 4, E])
        small = sb("e_small", [P, 2, 8])
        hid = sb("e_hid", [P, 2, E * RE])
        hT = sb("e_hT", [P, 2, KC, 2, P], F32R)
        res = sb("e_res", [P, 2, D])
        ps_t = ps("e_pst", [P, 2, D])
        ps_s = ps("e_pss", [P, 2, D])
        ps_h = ps("e_psh", [P, 2, E * RE])
        ps_v = ps("e_psv", [P, 2, D])

        w_loaded = sem("e_w_loaded")
        a_loaded = sem("e_a_loaded")
        x_loaded = sem("e_x_loaded")
        setup = sem("e_setup")
        aw_done = sem("e_aw_done")
        aw_exp = sem("e_aw_exp")
        w_hi = sem("e_w_hi")
        w_lo = sem("e_w_lo")
        stats_done = sem("e_stats_done")
        rstd_done = sem("e_rstd_done")
        normed = sem("e_normed")
        x_turned = sem("e_x_turned")
        xT_hi = sem("e_xT_hi")
        xT_lo = sem("e_xT_lo")
        route_mm = sem("e_route_mm")
        hid_mm = sem("e_hid_mm")
        route = sem("e_route")
        exp_done = sem("e_exp_done")
        hid_done = sem("e_hid_done")
        hid_turned = sem("e_hid_turned")
        hT_hi = sem("e_hT_hi")
        hT_lo = sem("e_hT_lo")
        v_mm = sem("e_v_mm")
        res_done = sem("e_res_done")
        stored = [sem(f"e_stored{s}") for s in range(2)]
        ticks = sem("e_ticks")
        ROUTE_STEPS = 16
        passes = ((0, 0), (0, 1), (1, 0))

        def steps(eng, step):
            for n in range(3):
                step(n, n % 2)
            with eng.Fori(1, NT // 2 - 1) as i:
                step(2 * i + 1, 1)
                step(2 * i + 2, 0)
            step(NT - 1, 1)
            step(NT, 0)

        def runs(n, shift):
            return not isinstance(n, int) or 0 <= n + shift < NT

        block = ctx.enter_context(nc.Block())

        @block.sync
        def _(sp):
            out_rows = out.rearrange("(n p) c -> n p c", p=P)
            for b in range(B):
                sp.dma_start(x[:, TPB * b:TPB * (b + 1), :], x_in.rearrange("(n p) c -> p n c", p=P)[:, TPB * b:TPB * (b + 1), :]).then_inc(x_loaded, 16)
            sp.dma_start(raw_u[:], d["U"].rearrange("(c p) n -> p c n", p=P)).then_inc(w_loaded, 16)
            sp.dma_start(raw_r[:], d["WrT"].rearrange("(c p) n -> p c n", p=P)).then_inc(w_loaded, 16)
            sp.dma_start(raw_v[:], d["V"].rearrange("(c p) n -> p c n", p=P)).then_inc(w_loaded, 16)
            sp.dma_start(attr[:], d["attr"].rearrange("(o e) a -> o e a", o=1).broadcast_to([P, E, 32])).then_inc(a_loaded, 16)
            sp.dma_start(wa[:], d["Wa"].broadcast_to([P, 32])).then_inc(a_loaded, 16)

            def store(n, s):
                sp.wait_ge(res_done, n + 1)
                sp.dma_start(out_rows[n] if isinstance(n, int) else one(out_rows, n), res[:, s, :]).then_inc(stored[s], 16)

            def step(n, s):
                if runs(n, -1):
                    store(n - 1, 1 - s)
            steps(sp, step)
            for s in range(2):
                sp.wait_ge(stored[s], 16 * (NT // 2 + 1))

        @block.gpsimd
        def _(pool):
            pool.iota(order[:], pattern=[[1, E]], base=0, channel_multiplier=0, allow_small_or_imprecise_dtypes=True).then_inc(setup, 1)
            pool.memset(eps[:], -0.5).then_inc(setup, 1)
            pool.wait_ge(setup, 2)

            def invert_std(n, s):
                pool.wait_ge(stats_done, 3 * (n + 1))
                pool.tensor_tensor(rstd[:, s:s + 1], var_eps[:, s:s + 1], eps[:, 0:1], ALU.pow).then_inc(rstd_done, 1)

            invert_std(0, 0)

            def step(n, s):
                if runs(n, 1):
                    invert_std(n + 1, 1 - s)
            steps(pool, step)

        @block.scalar
        def _(act):
            act.wait_ge(aw_done, 2)
            act.activation(aw[:, 1, :], aw[:, 0, :], ACT.Exp, scale=-1.0).then_inc(aw_exp, 1)
            act.wait_ge(w_loaded, 48)
            for raw, w in ((raw_u, u_w), (raw_r, r_w), (raw_v, v_w)):
                act.activation(w[:, :, 0, :], raw[:], ACT.Copy).then_inc(w_hi, 1)

            def keep_xT(n, s):
                act.wait_ge(x_turned, n + 1)
                after(act, hid_mm, n - 1)
                act.activation(xT[:, s, :, 0, :], ps_t[:, 0, :].rearrange("p (c n) -> p c n", n=P), ACT.Copy).then_inc(xT_hi, 1)

            keep_xT(0, 0)

            def step(n, s):
                if runs(n, 0):
                    act.wait_ge(route, ROUTE_STEPS * n + 2)
                    act.activation(g[:, s, 0, :], sc[:, s, :], ACT.Exp, bias=nbest[:, s:s + 1], accum_out=small[:, s, 0:1]).then_inc(exp_done, 1)
                if runs(n, 1):
                    keep_xT(n + 1, 1 - s)
                if runs(n, -1):
                    act.wait_ge(hid_turned, n)
                    after(act, v_mm, n - 2)
                    act.activation(hT[:, 1 - s, :, 0, :], ps_t[:, 1, :].rearrange("p (c n) -> p c n", n=P), ACT.Copy).then_inc(hT_hi, 1)
            steps(act, step)

        @block.tensor
        def _(pe):
            def turn_x(n):
                pe.wait_ge(normed, n + 1)
                after(pe, xT_lo, n)
                for c in range(KC):
                    ins = pe.transpose(ps_t[:, 0, c * P:(c + 1) * P], xn[:, c * P:(c + 1) * P], ident[:])
                ins.then_inc(x_turned, 1)

            turn_x(0)
            pe.wait_ge(w_lo, 3)

            def step(n, s):
                if runs(n, 0):
                    pe.wait_ge(xT_lo, n + 1)
                    after(pe, route, ROUTE_STEPS * (n - 1))
                    for c in range(KC):
                        for m, (a, b) in enumerate(passes):
                            ins = pe.matmul(ps_s[:, s, :E], xT[:, s, c, a, :], r_w[:, c, b, :], start=(c == 0 and m == 0), stop=(c == KC - 1 and m == 2))
                    ins.then_inc(route_mm, 1)
                    after(pe, hid_done, n - 1)
                    for c in range(KC):
                        for m, (a, b) in enumerate(passes):
                            ins = pe.matmul(ps_h[:, s, :], xT[:, s, c, a, :], u_w[:, c, b, :], start=(c == 0 and m == 0), stop=(c == KC - 1 and m == 2))
                    ins.then_inc(hid_mm, 1)
                if runs(n, 1):
                    turn_x(n + 1)
                if runs(n, -1):
                    pe.wait_ge(hid_done, n)
                    after(pe, hT_lo, n - 1)
                    for c in range(KC):
                        ins = pe.transpose(ps_t[:, 1, c * P:(c + 1) * P], hid[:, 1 - s, c * P:(c + 1) * P], ident[:])
                    ins.then_inc(hid_turned, 1)
                    pe.wait_ge(hT_lo, n)
                    after(pe, res_done, n - 2)
                    for c in range(KC):
                        for m, (a, b) in enumerate(passes):
                            ins = pe.matmul(ps_v[:, 1 - s, :], hT[:, 1 - s, c, a, :], v_w[:, c, b, :], start=(c == 0 and m == 0), stop=(c == KC - 1 and m == 2))
                    ins.then_inc(v_mm, 1)
            steps(pe, step)

        @block.vector
        def _(dve):
            for s in range(2):
                dve.sem_inc(stored[s], 16)
            dve.wait_ge(a_loaded, 32)
            dve.tensor_tensor(attr[:], attr[:], wa[:].rearrange("p (o a) -> p o a", o=1).broadcast_to([P, E, 32]), ALU.mult).then_inc(aw_done, 1)
            dve.wait_ge(aw_done, 1)
            dve.tensor_reduce(aw[:, 0, :], attr[:], AX_X, ALU.add).then_inc(aw_done, 1)
            dve.wait_ge(aw_exp, 1)
            dve.tensor_scalar(aw[:, 2, :], aw[:, 1, :], 1.0, None, ALU.add).then_inc(aw_done, 1)
            dve.wait_ge(aw_done, 3)
            dve.reciprocal(aw[:, 3, :], aw[:, 2, :]).then_inc(aw_done, 1)
            dve.wait_ge(aw_done, 4)
            for i, (raw, w) in enumerate(((raw_u, u_w), (raw_r, r_w), (raw_v, v_w))):
                dve.wait_ge(w_hi, i + 1)
                dve.tensor_tensor(w[:, :, 1, :], raw[:], w[:, :, 0, :].bitcast(F32), ALU.subtract).then_inc(w_lo, 1)

            def rows(n):
                return x[:, n, :] if isinstance(n, int) else tile_of(x, n)

            def statistics(n, s):
                dve.bn_stats(stats[:, s, :], rows(n)).then_inc(stats_done, 1)
                past(dve, stats_done, 3 * n + 1, ticks)
                dve.bn_aggr(mv[:, s, :], stats[:, s, :]).then_inc(stats_done, 1)
                dve.wait_ge(stats_done, 3 * n + 2)
                dve.tensor_scalar(var_eps[:, s:s + 1], mv[:, s, 1:2], LN_EPS, None, ALU.add).then_inc(stats_done, 1)

            def normalize(n, s):
                dve.wait_ge(rstd_done, n + 1)
                after(dve, x_turned, n)
                dve.tensor_scalar(xn[:], rows(n), mv[:, s, 0:1], rstd[:, s:s + 1], ALU.subtract, ALU.mult).then_inc(normed, 1)

            def split_xT(n, s):
                dve.wait_ge(xT_hi, n + 1)
                dve.tensor_tensor(xT[:, s, :, 1, :], ps_t[:, 0, :].rearrange("p (c n) -> p c n", n=P),
                                  xT[:, s, :, 0, :].bitcast(F32), ALU.subtract).then_inc(xT_lo, 1)

            dve.wait_ge(x_loaded, 16 * B)
            statistics(0, 0)
            normalize(0, 0)
            split_xT(0, 0)

            def step(n, s):
                if runs(n, 1):
                    statistics(n + 1, 1 - s)
                    normalize(n + 1, 1 - s)
                if runs(n, 0):
                    base = ROUTE_STEPS * n

                    def then(ins, done):
                        ins.then_inc(route, 1)
                        past(dve, route, base + done, ticks)

                    dve.wait_ge(route_mm, n + 1)
                    dve.tensor_copy(sc[:, s, :], ps_s[:, s, :E]).then_inc(route, 1)
                    dve.tensor_reduce(nbest[:, s:s + 1], ps_s[:, s, :E], AX_X, ALU.max, negate=True).then_inc(route, 1)
                    past(dve, route, base + 2, ticks)
                    then(dve.max(best[:, s, :], sc[:, s, :]), 3)
                    then(dve.max_index(which[:, s, :], best[:, s, :], sc[:, s, :]), 4)
                    then(dve.tensor_copy(whichf[:, s, :], which[:, s, :TOP]), 5)
                    then(dve.tensor_scalar(g[:, s, 1, :], order[:], whichf[:, s, 0:1], None, ALU.is_equal), 6)
                    then(dve.scalar_tensor_tensor(g[:, s, 2, :], order[:], whichf[:, s, 1:2], g[:, s, 1, :], ALU.is_equal, ALU.add), 7)
                    dve.wait_ge(exp_done, n + 1)
                    then(dve.reciprocal(small[:, s, 1:2], small[:, s, 0:1]), 8)
                    then(dve.scalar_tensor_tensor(g[:, s, 3, :], g[:, s, 0, :], small[:, s, 1:2], g[:, s, 2, :], ALU.mult, ALU.mult), 9)
                    then(dve.tensor_reduce(small[:, s, 2:3], g[:, s, 3, :], AX_X, ALU.add), 10)
                    then(dve.tensor_scalar(small[:, s, 3:4], small[:, s, 2:3], 1e-8, None, ALU.add), 11)
                    then(dve.reciprocal(small[:, s, 4:5], small[:, s, 3:4]), 12)
                    then(dve.tensor_scalar(g[:, s, 0, :], g[:, s, 3, :], small[:, s, 4:5], None, ALU.mult), 13)
                    dve.wait_ge(hid_mm, n + 1)
                    after(dve, hid_turned, n - 1)
                    dve.tensor_tensor(hid[:, s, :].rearrange("p (e r) -> p e r", r=RE), ps_h[:, s, :].rearrange("p (e r) -> p e r", r=RE),
                                      g[:, s, 0, :].rearrange("p (e o) -> p e o", o=1).broadcast_to([P, E, RE]), ALU.mult).then_inc(hid_done, 1)
                    then(dve.tensor_tensor(g[:, s, 1, :], g[:, s, 0, :], aw[:, 3, :], ALU.mult), 14)
                    then(dve.tensor_reduce(small[:, s, 5:6], g[:, s, 1, :], AX_X, ALU.add), 15)
                    then(dve.tensor_scalar(small[:, s, 6:7], small[:, s, 5:6], 0.2, 0.9, ALU.mult, ALU.add), 16)
                if runs(n, 1):
                    split_xT(n + 1, 1 - s)
                if runs(n, -1):
                    dve.wait_ge(hT_hi, n)
                    dve.tensor_tensor(hT[:, 1 - s, :, 1, :], ps_t[:, 1, :].rearrange("p (c n) -> p c n", n=P),
                                      hT[:, 1 - s, :, 0, :].bitcast(F32), ALU.subtract).then_inc(hT_lo, 1)
                    dve.wait_ge(v_mm, n)
                    if not (isinstance(n, int) and n < 3):
                        dve.wait_ge(stored[1 - s], 16 * ((n - 1) // 2 + 1))
                    dve.scalar_tensor_tensor(res[:, 1 - s, :], ps_v[:, 1 - s, :], small[:, 1 - s, 6:7], rows(n - 1), ALU.mult, ALU.add).then_inc(res_done, 1)
            steps(dve, step)


def latent_tables():
    step = np.float32(1.0) / np.float32(10000.0) ** (np.arange(0, DC, 2, dtype=np.float32) / np.float32(DC))
    angle = np.arange(S, dtype=np.float32)[:, None] * step[None, :]
    sin, cos = np.repeat(np.sin(angle), 2, axis=-1), np.repeat(np.cos(angle), 2, axis=-1)
    sin[:, :DC // 2] *= -1
    return cos, sin


def stage(nc, build, *args):
    with ExitStack() as ctx:
        used = []

        def sem(name):
            used.append(ctx.enter_context(nc.semaphore(name)))
            return used[-1]

        build(nc, sem, *args)
        with nc.Block() as block:
            @block.sync
            def _(sp):
                for s in used:
                    sp.sem_clear(s)


def program(nc, d, out):
    with ExitStack() as ctx:
        sb, _, _ = ring(ctx, nc)
        ident = sb("ident", [P, P])
        scr = {
            "x2": scratch(nc, "s_x2", [T, D]),
            "x3": scratch(nc, "s_x3", [T, D]),
            "kv": scratch(nc, "s_kv", [B, P, 2 * TPB * DC]),
            "kvT": scratch(nc, "s_kvT", [B, P, 2 * S]),
            "kr": scratch(nc, "s_kr", [HP, P, 4 * P]),
            "a": scratch(nc, "s_a", [HP, P, 2 * KC * P]),
            "xT": scratch(nc, "s_xT", [B, P, 2 * KC * S]),
        }
        with ExitStack() as heads:
            with ExitStack() as first:
                sb1, _, _ = ring(first, nc)
                x_res = sb1("x_res", [P, NT, D])
                mean = sb1("mean", [P, NT])
                rstd = sb1("rstd", [P, NT])
                stage(nc, stage_masked_attention, d, x_res, mean, rstd, ident)
                with ExitStack() as gated:
                    sb2, _, _ = ring(gated, nc)
                    w_guT = sb2("w_guT", [P, KC, 2 * FF], BF16)
                    w_dT = sb2("w_dT", [P, FC, D], BF16)
                    scale_rows = sb2("scale_rows", [P, 2 * FF + D])
                    ident_b = sb2("ident_b", [P, P], BF16)
                    stage(nc, stage_quantize_weights, d, w_guT, w_dT, scale_rows, ident_b)
                    stage(nc, stage_quantized_gated, d, x_res, mean, rstd, w_guT, w_dT, scale_rows, ident_b)
                out_w = heads.enter_context(nc.sbuf_tensor("out_w", [P, H, 2, D], F32R, side="right"))
                stage(nc, stage_prepare_heads, d, scr, x_res, mean, rstd, ident, out_w)
            stage(nc, stage_latent_attention, scr, scr["x3"], ident, out_w)
        stage(nc, stage_routed_experts, d, scr["x3"], out, ident)


def kernel(**inputs):
    import concourse.bacc as bacc
    from concourse.bass_utils import run_bass_kernel_spmd

    def laid(a, *axes):
        a = np.asarray(a)
        return np.ascontiguousarray(a.transpose(axes) if axes else a)

    cos, sin = latent_tables()
    flat_ctx = laid(inputs["ctx_512"]).reshape(T, DC)
    arrays = {
        "x": laid(inputs["x"]).reshape(T, D),
        "ctx": flat_ctx,
        "ctxT": laid(flat_ctx, 1, 0),
        "attn_mask": laid(inputs["mask_SxS2_bk1"]),
        "pad_mask": laid(inputs["mask_BxS2_bf0"]),
        "L0_WqT": laid(inputs["L0_xattn_Wq"], 1, 0),
        "L0_WkT": laid(inputs["L0_xattn_Wk"], 1, 0),
        "L0_xattn_bq": laid(inputs["L0_xattn_bq"]),
        "L0_xattn_bk": laid(inputs["L0_xattn_bk"]),
        "L0_ffn_w_gate": laid(inputs["L0_ffn_w_gate"]),
        "L0_ffn_w_up": laid(inputs["L0_ffn_w_up"]),
        "L0_ffn_w_down": laid(inputs["L0_ffn_w_down"]),
        "down_idx": laid(inputs["L0_ffn_down_reorder_index"]),
        "rope_cos": cos,
        "rope_sin": sin,
        "W_krT": laid(inputs["L1_xattn_W_kr"], 1, 0, 2).reshape(DC, H * R),
        "w_kc_qT": laid(inputs["L1_xattn_w_kc_q"], 0, 2, 1),
        "W_qr": laid(inputs["L1_xattn_W_qr"]),
        "L1_Wq": laid(inputs["L1_xattn_Wq"]).reshape(H, P, D),
        "w_kc_kv": laid(inputs["L1_xattn_w_kc_kv"]),
        "WoT": laid(inputs["L1_xattn_Wo"], 1, 0).reshape(H, P, D),
        "U": laid(inputs["L1_ffn_U"], 1, 0, 2).reshape(D, E * RE),
        "V": laid(inputs["L1_ffn_V"]).reshape(E * RE, D),
        "WrT": laid(inputs["L1_ffn_Wr"], 1, 0),
        "attr": laid(inputs["L1_ffn_attr"]),
        "Wa": laid(inputs["L1_ffn_Wa"]),
    }
    nc = bacc.Bacc("TRN2", target_bir_lowering=False, num_devices=1)
    d = {k: nc.dram_tensor(f"in_{k}", a.shape, mybir.dt.from_np(a.dtype), kind="ExternalInput").ap() for k, a in arrays.items()}
    out = nc.dram_tensor("out_x", [T, D], F32, kind="ExternalOutput").ap()
    program(nc, d, out)
    r = run_bass_kernel_spmd(nc, [{f"in_{k}": a for k, a in arrays.items()}], core_ids=[0])
    return r.results[0]["out_x"].reshape(B, S, D)
```

```python
from contextlib import ExitStack

import numpy as np

import concourse.bass as bass
from concourse import mybir

P = 128
B, S, D = 4, 512, 512
T = B * S
NT = T // P
TPB = S // P
KC = D // P
DC = 128
FF = 1408
FC = FF // P
LN_EPS = 1e-5
FP8_MAX = 448.0
MASKED = -1e30

F32 = mybir.dt.float32
F32R = mybir.dt.float32r
BF16 = mybir.dt.bfloat16
U32 = mybir.dt.uint32
I32 = mybir.dt.int32
U8 = mybir.dt.uint8
ALU = mybir.AluOpType
ACT = mybir.ActivationFunctionType
AX_X = mybir.AxisListType.X


def ring(ctx, nc):
    def sb(name, shape, dt=F32):
        return ctx.enter_context(nc.sbuf_tensor(name, shape, dt))

    def ps(name, shape, dt=F32):
        return ctx.enter_context(nc.psum_tensor(name, shape, dt))

    def sem(name):
        return ctx.enter_context(nc.semaphore(name))
    return sb, ps, sem


def tile_of(a, n):
    return a[:, bass.ds(n, 1), :].rearrange("p o d -> p (o d)")


def tile_or(a, n):
    return a[:, n, :] if isinstance(n, int) else tile_of(a, n)


def column(a, n):
    return a[:, n:n + 1] if isinstance(n, int) else a[:, bass.ds(n, 1)]


def after(eng, sem, value):
    if not isinstance(value, int) or value > 0:
        eng.wait_ge(sem, value)


def past(eng, sem, value, ticks):
    eng.wait_ge(sem, value)
    if not isinstance(value, int):
        eng.sem_inc(ticks, 1)


def stage_masked_attention(nc, sem, d, x_res, mean, rstd, ident, w_in):
    with ExitStack() as ctx:
        sb, ps, _ = ring(ctx, nc)
        ctxT = sb("a_ctxT", [P, T])
        wT = sb("a_wT", [P, 2, P])
        bias_qk = sb("a_bqk", [P, 2])
        mask8 = sb("a_mask8", [P, TPB, S], U8)
        pad8 = sb("a_pad8", [P, B, S], U8)
        mask_bias = sb("a_maskb", [P, TPB, S])
        pad_bias = sb("a_padb", [P, B, S])
        both_bias = sb("a_bothb", [P, TPB, S])
        stats = sb("a_stats", [P, NT, 6])
        mv = sb("a_mv", [P, NT, 2])
        var_eps = sb("a_vareps", [P, NT])
        m_half = sb("a_mhalf", [P, NT])
        qT = sb("a_qT", [P, S])
        kT = sb("a_kT", [P, B, S])
        xn = sb("a_xn", [P, 2, S])
        z = sb("a_z", [P, 2, S])
        prob = sb("a_prob", [P, 2, S])
        nmax = sb("a_nmax", [P, 2])
        rsum = sb("a_rsum", [P, 2])
        rinv = sb("a_rinv", [P, 2])
        ps_q = ps("a_psq", [P, S])
        ps_k = ps("a_psk", [P, 2, S])
        ps_s = ps("a_pss", [P, 2, S])

        x_loaded = [sem(f"a_x_loaded{b}") for b in range(B)]
        w_loaded = sem("a_w_loaded")
        m_loaded = sem("a_m_loaded")
        halves = sem("a_halves")
        stats_done = sem("a_stats_done")
        rstd_done = sem("a_rstd_done")
        bias_made = sem("a_bias_made")
        both_made = sem("a_both_made")
        k_mm = sem("a_k_mm")
        k_ready = sem("a_k_ready")
        q_mm = sem("a_q_mm")
        q_ready = sem("a_q_ready")
        score_mm = sem("a_score_mm")
        xn_done = sem("a_xn_done")
        z_scaled = sem("a_z_scaled")
        z_done = sem("a_z_done")
        max_done = sem("a_max_done")
        exp_done = sem("a_exp_done")
        rinv_done = sem("a_rinv_done")
        x_done = sem("a_x_done")
        id_zero = sem("a_id_zero")
        SCALE = float(DC) ** -0.5

        def batches(eng, tile):
            for t in range(TPB):
                tile(t, t, 0)
            with eng.Fori(1, B) as b:
                for t in range(TPB):
                    tile(b * TPB + t, t, b)

        block = ctx.enter_context(nc.Block())

        @block.sync
        def _(sp):
            sp.dma_start(wT[:, 0, :], d["L0_WqT"]).then_inc(w_loaded, 16)
            sp.dma_start(wT[:, 1, :], d["L0_WkT"]).then_inc(w_loaded, 16)
            sp.dma_start(bias_qk[:, 0:1], d["L0_xattn_bq"].rearrange("(p o) -> p o", o=1)).then_inc(w_loaded, 16)
            sp.dma_start(bias_qk[:, 1:2], d["L0_xattn_bk"].rearrange("(p o) -> p o", o=1)).then_inc(w_loaded, 16)
            sp.dma_start(ctxT[:], d["ctxT"]).then_inc(w_loaded, 16)
            x_rows = d["x"].rearrange("(n p) c -> p n c", p=P)
            for b in range(B):
                sp.dma_start(x_res[:, TPB * b:TPB * (b + 1), :], x_rows[:, TPB * b:TPB * (b + 1), :]).then_inc(x_loaded[b], 16)
                if b == 0:
                    sp.dma_start(mask8[:], d["attn_mask"].rearrange("(t p) l -> p t l", p=P)).then_inc(m_loaded, 16)
                    sp.dma_start(pad8[:], d["pad_mask"].rearrange("(o b) l -> o b l", o=1).broadcast_to([P, B, S])).then_inc(m_loaded, 16)
            sp.dma_start(w_in["idx"][:], d["down_idx"].rearrange("(c p) -> p c", p=P), allow_slow_non_contiguous=True).then_inc(w_in["idx_loaded"], 16)
            sp.dma_start(w_in["raw_d"][:], d["L0_ffn_w_down"].rearrange("(c p) k -> p c k", p=P)).then_inc(w_in["down_loaded"], 16)

        @block.gpsimd
        def _(pool):
            pool.memset(ident[:], 0.0).then_inc(id_zero, 1)
            pool.memset(m_half[:], -0.5).then_inc(halves, 1)
            pool.wait_ge(id_zero, 1)
            pool.affine_select(out=ident[:], in_=ident[:], compare_op=ALU.not_equal, fill=1.0, base=0,
                               pattern=[[-1, P]], channel_multiplier=1).then_inc(id_zero, 1)
            pool.wait_ge(halves, 1)
            for b in range(B):
                tiles = slice(TPB * b, TPB * (b + 1))
                pool.wait_ge(stats_done, (2 * TPB + 2) * (b + 1))
                pool.tensor_tensor(rstd[:, tiles], var_eps[:, tiles], m_half[:, tiles], ALU.pow).then_inc(rstd_done, 1)
                if b == 0:
                    pool.wait_ge(bias_made, 2)
                    for t in range(TPB):
                        pool.tensor_tensor(both_bias[:, t, :], mask_bias[:, t, :], pad_bias[:, 0, :], ALU.add).then_inc(both_made, 1)
            gathers = [(h * FC + c, w, c) for h, w in enumerate(("L0_ffn_w_gate", "L0_ffn_w_up")) for c in range(FC)]
            pool.wait_ge(w_in["idx_loaded"], 16)
            for n in range(TPB, NT):
                pool.wait_ge(z_done, n - TPB + 1)
                pool.tensor_tensor(both_bias[:, n % TPB, :], mask_bias[:, n % TPB, :], pad_bias[:, n // TPB, :], ALU.add).then_inc(both_made, 1)
                for _ in range(2):
                    if gathers:
                        row, w, c = gathers.pop(0)
                        pool.indirect_dma_start(w_in["raw"][:, row, :], None, d[w],
                                                bass.IndirectOffsetOnAxis(ap=w_in["idx"][:, c:c + 1], axis=0)).then_inc(w_in["gathered"], 16)

        @block.tensor
        def _(pe):
            def queries(b):
                after(pe, q_ready, b)
                cols = ctxT[:, b * S:(b + 1) * S] if isinstance(b, int) else ctxT[:, bass.ds(b * S, S)]
                pe.matmul(ps_q[:], wT[:, 0, :], cols, start=True, stop=True).then_inc(q_mm, 1)

            def batch(b, last):
                pe.wait_ge(q_ready, b + 1)
                for t in range(TPB):
                    n = b * TPB + t
                    if t == 0:
                        pe.wait_ge(k_ready, b + 1)
                    after(pe, z_scaled, n - 1)
                    keys = kT[:, b, :] if isinstance(b, int) else tile_of(kT, b)
                    pe.matmul(ps_s[:, t % 2, :], qT[:, t * P:(t + 1) * P], keys, start=True, stop=True).then_inc(score_mm, 1)
                    if t == 1 and not last:
                        queries(b + 1)

            pe.wait_ge(w_loaded, 80)
            queries(0)
            for b in range(B):
                after(pe, k_ready, b - 1)
                pe.matmul(ps_k[:, b % 2, :], wT[:, 1, :], ctxT[:, b * S:(b + 1) * S], start=True, stop=True).then_inc(k_mm, 1)
            batch(0, False)
            with pe.Fori(1, B - 1) as b:
                batch(b, False)
            batch(B - 1, True)

        @block.scalar
        def _(act):
            def keep_queries(b):
                act.wait_ge(q_mm, b + 1)
                after(act, score_mm, b * TPB)
                act.activation(qT[:], ps_q[:], ACT.Identity, bias=bias_qk[:, 0:1]).then_inc(q_ready, 1)

            def exps(n, t):
                act.wait_ge(max_done, n + 1)
                after(act, x_done, n - 1)
                act.activation(prob[:, t % 2, :], z[:, t % 2, :], ACT.Exp, bias=nmax[:, t % 2:t % 2 + 1],
                               accum_out=rsum[:, t % 2:t % 2 + 1]).then_inc(exp_done, 1)

            act.wait_ge(w_loaded, 80)
            keep_queries(0)
            for b in range(B):
                act.wait_ge(k_mm, b + 1)
                act.activation(kT[:, b, :], ps_k[:, b % 2, :], ACT.Identity, bias=bias_qk[:, 1:2]).then_inc(k_ready, 1)
            act.wait_ge(m_loaded, 32)
            act.activation(mask_bias[:], mask8[:], ACT.Copy, scale=MASKED).then_inc(bias_made, 1)
            act.activation(pad_bias[:], pad8[:], ACT.Copy, scale=MASKED).then_inc(bias_made, 1)
            def batch(b, last):
                for t in range(TPB):
                    exps(b * TPB + t, t)
                    if t == TPB - 2 and not last:
                        keep_queries(b + 1)
            batch(0, False)
            with act.Fori(1, B - 1) as b:
                batch(b, False)
            batch(B - 1, True)

        @block.vector
        def _(dve):
            def statistics(b):
                first = (2 * TPB + 2) * b
                dve.wait_ge(x_loaded[b], 16)
                for n in range(TPB * b, TPB * (b + 1)):
                    dve.bn_stats(stats[:, n, :], x_res[:, n, :]).then_inc(stats_done, 1)
                dve.wait_ge(stats_done, first + TPB)
                for n in range(TPB * b, TPB * (b + 1)):
                    dve.bn_aggr(mv[:, n, :], stats[:, n, :]).then_inc(stats_done, 1)
                dve.wait_ge(stats_done, first + 2 * TPB)
                tiles = slice(TPB * b, TPB * (b + 1))
                dve.tensor_scalar(var_eps[:, tiles], mv[:, tiles, 1], LN_EPS, None, ALU.add).then_inc(stats_done, 1)
                dve.tensor_copy(mean[:, tiles], mv[:, tiles, 0]).then_inc(stats_done, 1)

            def update(n, s):
                dve.wait_ge(exp_done, n + 1)
                dve.reciprocal(rinv[:, s:s + 1], rsum[:, s:s + 1]).then_inc(rinv_done, 1)
                dve.wait_ge(rinv_done, n + 1)
                dve.scalar_tensor_tensor(tile_or(x_res, n), prob[:, s, :], rinv[:, s:s + 1], tile_or(x_res, n),
                                         ALU.mult, ALU.add).then_inc(x_done, 1)

            def tile(n, t, b):
                s = t % 2
                after(dve, z_scaled, n - 1)
                dve.tensor_scalar(xn[:, s, :], tile_or(x_res, n), column(mean, n), column(rstd, n),
                                  ALU.subtract, ALU.mult).then_inc(xn_done, 1)
                dve.wait_ge(xn_done, n + 1)
                dve.wait_ge(score_mm, n + 1)
                after(dve, exp_done, n - 1)
                dve.scalar_tensor_tensor(z[:, s, :], ps_s[:, s, :], SCALE, xn[:, s, :], ALU.mult, ALU.mult).then_inc(z_scaled, 1)
                dve.wait_ge(z_scaled, n + 1)
                dve.wait_ge(both_made, n + 1)
                dve.tensor_tensor(z[:, s, :], z[:, s, :], both_bias[:, t, :], ALU.add).then_inc(z_done, 1)
                dve.wait_ge(z_done, n + 1)
                dve.tensor_reduce(nmax[:, s:s + 1], z[:, s, :], AX_X, ALU.max, negate=True).then_inc(max_done, 1)
                if not isinstance(n, int) or n:
                    update(n - 1, 1 - s)

            for b in range(B):
                statistics(b)
            dve.wait_ge(rstd_done, B)
            dve.wait_ge(stats_done, (2 * TPB + 2) * B)
            batches(dve, tile)
            update(NT - 1, 1)
            dve.wait_ge(x_done, NT)


SUBNORMAL_TOP = 2.0 ** -6
MAGIC = 1.5 * 2.0 ** 20


def exponent_of(dve, e, v, done):
    dve.tensor_scalar(e.bitcast(U32), v.bitcast(U32), 0x7F800000, None, ALU.bitwise_and).then_inc(done, 1)


def rounder_of(dve, e, done):
    dve.tensor_scalar(e, e, SUBNORMAL_TOP, MAGIC, ALU.max, ALU.mult).then_inc(done, 1)


def stage_quantize(nc, sem, d, x_res, mean, rstd, w_guT, w_dT, scale_rows, ident_b, qT, out_scale, w_in):
    N = 2 * FC
    with ExitStack() as ctx:
        sb, ps, _ = ring(ctx, nc)
        raw, raw_d, gathered, down_loaded = w_in["raw"], w_in["raw_d"], w_in["gathered"], w_in["down_loaded"]
        top = sb("w_top", [P, N + KC])
        scale = sb("w_scale", [P, N + KC])
        inv = sb("w_inv", [P, N + KC])
        scaleT = sb("w_scaleT", [N + KC, P])
        identf = sb("w_identf", [P, P])
        v = sb("w_v", [P, 2 * FF])
        e = sb("w_e", [P, 2 * FF])
        q = sb("w_q", [P, 2 * FF], BF16)
        stats = sb("w_stats", [P, NT, 6])
        mv = sb("w_mv", [P, NT, 2])
        var_eps = sb("w_vareps", [P, NT])
        m_half = sb("w_mhalf", [P, NT])
        neg_mean = sb("w_negmean", [P, NT])
        tok_top = sb("w_toktop", [P, NT])
        tok_scale = sb("w_tokscale", [P, NT])
        tok_inv = sb("w_tokinv", [P, NT])
        ps_t = ps("w_pst", [P, 4, 1024], BF16)
        ps_st = ps("w_psst", [N + KC, 512])
        scale_dram = nc.dram_tensor("w_scale_rows", [N + KC, P], F32).ap()

        ids = sem("w_ids")
        halves = sem("w_halves")
        stats_done = sem("w_stats_done")
        rstd_done = sem("w_rstd_done")
        maxima = sem("w_maxima")
        scales = sem("w_scales")
        scaleT_mm = sem("w_scaleT_mm")
        scaleT_done = sem("w_scaleT_done")
        scale_stored = sem("w_scale_stored")
        rows_loaded = sem("w_rows_loaded")
        centred = sem("w_centred")
        tok_scales = sem("w_tok_scales")
        scaled = sem("w_scaled")
        exps = sem("w_exps")
        rounders = sem("w_rounders")
        shifted = sem("w_shifted")
        rounded = sem("w_rounded")
        turned = sem("w_turned")
        kept = sem("w_kept")

        WEIGHTS = dict(size=2, groups=FC, width=D, seen=0)
        TOKENS = dict(size=2, groups=NT // 2, width=D, seen=N)
        DOWN = dict(size=1, groups=KC, width=FF, seen=N + NT)
        ALL = N + NT + KC

        def groups(eng, kind, step):
            G = kind["groups"]
            for g in range(min(3, G + 1)):
                step(g, g % 2)
            rest = 3
            if G >= 7:
                pairs = (G - 4) // 2
                with eng.Fori(0, pairs) as i:
                    step(2 * i + 3, 1)
                    step(2 * i + 4, 0)
                rest = 3 + 2 * pairs
            for g in range(rest, G + 1):
                step(g, g % 2)

        def has(kind, g):
            return not isinstance(g, int) or 0 <= g < kind["groups"]

        def slots(kind, g, par):
            size, w = kind["size"], kind["width"]
            return [(size * g + s, size * par + s, slice((size * par + s) * w, (size * par + s + 1) * w)) for s in range(size)]

        def behind(eng, sem, kind, c):
            held = 2 * kind["size"]
            value = kind["seen"] + (c - held + 1 if not isinstance(c, int) or c >= held else 0)
            if not isinstance(value, int) or value > 0:
                eng.wait_ge(sem, value)

        block = ctx.enter_context(nc.Block())

        @block.sync
        def _(sp):
            sp.wait_ge(scaleT_done, 1)
            sp.dma_start(scale_dram, scaleT[:]).then_inc(scale_stored, 16)
            sp.wait_ge(scale_stored, 16)
            sp.dma_start(scale_rows[:], scale_dram.rearrange("(o c) p -> o (c p)", o=1).broadcast_to([P, (N + KC) * P])).then_inc(rows_loaded, 16)
            sp.wait_ge(rows_loaded, 16)

        @block.gpsimd
        def _(pool):
            pool.memset(m_half[:], -0.5).then_inc(halves, 1)
            pool.memset(identf[:], 0.0).then_inc(ids, 1)
            pool.memset(ident_b[:], 0.0).then_inc(ids, 1)
            pool.wait_ge(ids, 2)
            for m in (identf, ident_b):
                pool.affine_select(out=m[:], in_=m[:], compare_op=ALU.not_equal, fill=1.0, base=0,
                                   pattern=[[-1, P]], channel_multiplier=1).then_inc(ids, 1)
            pool.wait_ge(halves, 1)
            pool.wait_ge(stats_done, 2 * NT + 1)
            pool.tensor_tensor(rstd[:], var_eps[:], m_half[:], ALU.pow).then_inc(rstd_done, 1)
            for kind in (WEIGHTS, TOKENS, DOWN):
                def shift(g, par):
                    for c, _, cols in slots(kind, g, par) if has(kind, g) else ():
                        pool.wait_ge(rounders, kind["seen"] + c + 1)
                        pool.tensor_tensor(v[:, cols], v[:, cols], e[:, cols], ALU.add).then_inc(shifted, 1)
                groups(pool, kind, shift)

        @block.scalar
        def _(act):
            def scale_group(kind, g, par):
                for c, _, cols in slots(kind, g, par):
                    behind(act, rounded, kind, c)
                    if kind is WEIGHTS:
                        src, by = tile_or(raw, c), column(inv, c)
                    elif kind is TOKENS:
                        src, by = tile_or(raw, c), column(tok_inv, c)
                    else:
                        src, by = tile_or(raw_d, c), column(inv, N + c)
                    act.activation(v[:, cols], src, ACT.Copy, scale=by).then_inc(scaled, 1)

            def keep_group(kind, g, par):
                for c, slot, _ in slots(kind, g, par):
                    act.wait_ge(turned, kind["seen"] + c + 1)
                    if kind is DOWN:
                        for b, (x, y) in enumerate(((0, 8), (8, FC))):
                            ins = act.activation(w_dT[:, x:y, c * P:(c + 1) * P], ps_t[:, 2 * slot + b, :(y - x) * P].rearrange("p (c n) -> p c n", n=P), ACT.Copy)
                    elif kind is TOKENS:
                        out = qT[:, c, :, :] if isinstance(c, int) else qT[:, bass.ds(c, 1), :, :].rearrange("p o c n -> p (o c) n")
                        ins = act.activation(out, ps_t[:, slot, :D].rearrange("p (c n) -> p c n", n=P), ACT.Copy)
                    else:
                        out = w_guT[:, :, c * P:(c + 1) * P] if isinstance(c, int) else w_guT[:, :, bass.ds(c * P, P)]
                        ins = act.activation(out, ps_t[:, slot, :D].rearrange("p (c n) -> p c n", n=P), ACT.Copy)
                    ins.then_inc(kept, 1)

            act.wait_ge(scales, 2)
            act.wait_ge(scaleT_mm, 1)
            act.activation(scaleT[:], ps_st[:, :P], ACT.Copy).then_inc(scaleT_done, 1)
            for kind in (WEIGHTS, TOKENS, DOWN):
                if kind is TOKENS:
                    act.wait_ge(scaled, N)
                    act.wait_ge(stats_done, 2 * NT + 3)
                    for n in range(NT):
                        act.activation(raw[:, n, :], x_res[:, n, :], ACT.Identity, bias=neg_mean[:, n:n + 1]).then_inc(centred, 1)
                    act.wait_ge(tok_scales, 3)
                scale_group(kind, 0, 0)

                def step(g, par):
                    if has(kind, g + 1):
                        scale_group(kind, g + 1, 1 - par)
                    if has(kind, g - 1):
                        keep_group(kind, g - 1, 1 - par)
                groups(act, kind, step)

        @block.tensor
        def _(pe):
            pe.wait_ge(ids, 4)
            pe.wait_ge(scales, 2)
            pe.transpose(ps_st[:, :P], scale[:], identf[:]).then_inc(scaleT_mm, 1)
            for kind in (WEIGHTS, TOKENS, DOWN):
                def turn(g, par):
                    for c, slot, cols in slots(kind, g, par) if has(kind, g) else ():
                        pe.wait_ge(rounded, kind["seen"] + c + 1)
                        behind(pe, kept, kind, c)
                        for k in range(kind["width"] // P):
                            bank = 2 * slot + k // 8 if kind is DOWN else slot
                            ins = pe.transpose(ps_t[:, bank, (k % 8) * P:(k % 8 + 1) * P], q[:, cols.start + k * P:cols.start + (k + 1) * P], ident_b[:])
                        ins.then_inc(turned, 1)
                groups(pe, kind, turn)

        @block.vector
        def _(dve):
            for n in range(NT):
                dve.bn_stats(stats[:, n, :], x_res[:, n, :]).then_inc(stats_done, 1)
            for n in range(NT):
                dve.wait_ge(stats_done, n + 1)
                dve.bn_aggr(mv[:, n, :], stats[:, n, :]).then_inc(stats_done, 1)
            dve.wait_ge(stats_done, 2 * NT)
            dve.tensor_scalar(var_eps[:], mv[:, :, 1], LN_EPS, None, ALU.add).then_inc(stats_done, 1)
            dve.tensor_copy(mean[:], mv[:, :, 0]).then_inc(stats_done, 1)
            dve.tensor_scalar(neg_mean[:], mv[:, :, 0], -1.0, None, ALU.mult).then_inc(stats_done, 1)
            dve.wait_ge(down_loaded, 16)
            dve.tensor_reduce(top[:, N:], raw_d[:], AX_X, ALU.max, apply_absolute_value=True).then_inc(maxima, 1)
            dve.wait_ge(gathered, 16 * N)
            dve.tensor_reduce(top[:, :N], raw[:], AX_X, ALU.max, apply_absolute_value=True).then_inc(maxima, 1)
            dve.wait_ge(maxima, 2)
            dve.tensor_scalar(scale[:], top[:], 1.0 / FP8_MAX, None, ALU.mult).then_inc(scales, 1)
            dve.wait_ge(scales, 1)
            dve.reciprocal(inv[:], scale[:]).then_inc(scales, 1)

            def find_rounders(kind, g, par):
                for c, _, cols in slots(kind, g, par):
                    done = kind["seen"] + c + 1
                    dve.wait_ge(scaled, done)
                    exponent_of(dve, e[:, cols], v[:, cols], exps)
                    dve.wait_ge(exps, done)
                    rounder_of(dve, e[:, cols], rounders)

            def round_group(kind, g, par):
                for c, _, cols in slots(kind, g, par):
                    dve.wait_ge(shifted, kind["seen"] + c + 1)
                    behind(dve, turned, kind, c)
                    dve.tensor_tensor(q[:, cols], v[:, cols], e[:, cols], ALU.subtract).then_inc(rounded, 1)

            for kind in (WEIGHTS, TOKENS, DOWN):
                if kind is TOKENS:
                    for h in range(2):
                        tiles = slice(h * NT // 2, (h + 1) * NT // 2)
                        dve.wait_ge(centred, (h + 1) * NT // 2)
                        dve.tensor_reduce(tok_top[:, tiles], raw[:, tiles, :], AX_X, ALU.max, apply_absolute_value=True).then_inc(maxima, 1)
                    dve.wait_ge(maxima, 4)
                    dve.tensor_scalar(tok_scale[:], tok_top[:], 1.0 / FP8_MAX, None, ALU.mult).then_inc(tok_scales, 1)
                    dve.wait_ge(tok_scales, 1)
                    dve.reciprocal(tok_inv[:], tok_scale[:]).then_inc(tok_scales, 1)
                    dve.wait_ge(rstd_done, 1)
                    dve.tensor_tensor(out_scale[:], tok_scale[:], rstd[:], ALU.mult).then_inc(tok_scales, 1)

                def step(g, par):
                    if has(kind, g):
                        find_rounders(kind, g, par)
                    if has(kind, g - 1):
                        round_group(kind, g - 1, 1 - par)
                groups(dve, kind, step)
            dve.wait_ge(rounded, ALL)
            dve.wait_ge(kept, ALL)


def stage_quantized_gated(nc, sem, d, x_res, w_guT, w_dT, scale_rows, ident_b, qT, out_scale):
    with ExitStack() as ctx:
        sb, ps, _ = ring(ctx, nc)
        gate = sb("g_gate", [P, 2, FF])
        up = sb("g_up", [P, 2, FF])
        he = sb("g_he", [P, 2, FF])
        hq = sb("g_hq", [P, 2, FF], BF16)
        hqT = sb("g_hqT", [P, 2, FC, P], BF16)
        htop = sb("g_htop", [P, 2, 3])
        y_scale = sb("g_yscale", [P, NT])
        y = sb("g_y", [P, 2, D])
        ps_g = ps("g_psg", [P, 3, 512])
        ps_u = ps("g_psu", [P, 3, 512])
        ps_t = ps("g_pst", [P, 1024], BF16)
        ps_y = ps("g_psy", [P, D])

        gate_mm = sem("g_gate_mm")
        up_mm = sem("g_up_mm")
        gate_out = sem("g_gate_out")
        up_out = sem("g_up_out")
        silu_done = sem("g_silu_done")
        prod_done = sem("g_prod_done")
        htops = sem("g_htops")
        hscaled = sem("g_hscaled")
        hexps = sem("g_hexps")
        hrounders = sem("g_hrounders")
        hshifted = sem("g_hshifted")
        hrounded = sem("g_hrounded")
        hturned = sem("g_hturned")
        hqT_done = sem("g_hqT_done")
        down_mm = sem("g_down_mm")
        y_out = sem("g_y_out")
        x_done = sem("g_x_done")
        CH = ((0, 512), (512, 1024), (1024, FF))
        TURNS = ((0, 8), (8, FC))

        def steps(eng, step):
            for n in range(5):
                step(n, n % 2)
            with eng.Fori(2, NT // 2 - 1) as i:
                step(2 * i + 1, 1)
                step(2 * i + 2, 0)
            for n in range(NT - 1, NT + 3):
                step(n, n % 2)

        def runs(n, shift):
            return not isinstance(n, int) or 0 <= n + shift < NT

        block = ctx.enter_context(nc.Block())

        @block.gpsimd
        def _(pool):
            def step(n, s):
                if runs(n, 0):
                    pool.wait_ge(silu_done, n + 1)
                    pool.wait_ge(up_out, n + 1)
                    pool.tensor_tensor(gate[:, s, :], gate[:, s, :], up[:, s, :], ALU.mult).then_inc(prod_done, 1)
                if runs(n, -1):
                    pool.wait_ge(hrounders, n)
                    pool.tensor_tensor(gate[:, 1 - s, :], gate[:, 1 - s, :], he[:, 1 - s, :], ALU.add).then_inc(hshifted, 1)
            steps(pool, step)

        @block.scalar
        def _(act):
            def step(n, s):
                if runs(n, 0):
                    act.wait_ge(gate_out, n + 1)
                    act.activation(gate[:, s, :], gate[:, s, :], ACT.Silu, scale=column(out_scale, n)).then_inc(silu_done, 1)
                if runs(n, -2):
                    after(act, down_mm, n - 3)
                    for g, (a, b) in enumerate(TURNS):
                        act.wait_ge(hturned, 2 * (n - 2) + g + 1)
                        act.activation(hqT[:, s, a:b, :], ps_t[:, :(b - a) * P].rearrange("p (c n) -> p c n", n=P), ACT.Copy).then_inc(hqT_done, 1)
                if runs(n, 0):
                    act.wait_ge(htops, 4 * n + 3)
                    act.activation(gate[:, s, :], gate[:, s, :], ACT.Copy, scale=htop[:, s, 2:3]).then_inc(hscaled, 1)
            steps(act, step)

        @block.tensor
        def _(pe):
            def hidden(n, base, bank, free, done):
                after(pe, free, n)
                for j, (a, b) in enumerate(CH):
                    for c in range(KC):
                        left = qT[:, n, c, :] if isinstance(n, int) else qT[:, bass.ds(n, 1), c, :].rearrange("p o n -> p (o n)")
                        ins = pe.matmul(bank[:, j, :b - a], left, w_guT[:, c, base + a:base + b], start=(c == 0), stop=(c == KC - 1))
                ins.then_inc(done, 1)

            def gate_of(n):
                hidden(n, 0, ps_g, gate_out, gate_mm)

            def up_of(n):
                hidden(n, FF, ps_u, up_out, up_mm)

            def turn_hidden(n, s, g):
                a, b = TURNS[g]
                if g == 0:
                    pe.wait_ge(hrounded, n + 1)
                after(pe, hqT_done, 2 * n + g)
                for c in range(a, b):
                    ins = pe.transpose(ps_t[:, (c - a) * P:(c - a + 1) * P], hq[:, s, c * P:(c + 1) * P], ident_b[:])
                ins.then_inc(hturned, 1)

            gate_of(0)
            up_of(0)

            def step(n, s):
                if runs(n, -2):
                    turn_hidden(n - 2, s, 0)
                if runs(n, 1):
                    gate_of(n + 1)
                if runs(n, -2):
                    turn_hidden(n - 2, s, 1)
                if runs(n, 1):
                    up_of(n + 1)
                if runs(n, -2):
                    pe.wait_ge(hqT_done, 2 * (n - 2) + 2)
                    after(pe, y_out, n - 2)
                    for c in range(FC):
                        ins = pe.matmul(ps_y[:], hqT[:, s, c, :], w_dT[:, c, :], start=(c == 0), stop=(c == FC - 1))
                    ins.then_inc(down_mm, 1)
            steps(pe, step)
            pe.wait_ge(down_mm, NT)

        @block.vector
        def _(dve):
            def output(n, s):
                dve.wait_ge(down_mm, n + 1)
                after(dve, x_done, n - 1)
                dve.tensor_tensor(y[:, s, :], ps_y[:], scale_rows[:, 2 * FF:2 * FF + D], ALU.mult).then_inc(y_out, 1)
                dve.wait_ge(y_out, n + 1)
                dve.scalar_tensor_tensor(tile_or(x_res, n), y[:, s, :], column(y_scale, n), tile_or(x_res, n), ALU.mult, ALU.add).then_inc(x_done, 1)

            def step(n, s):
                if runs(n, 0):
                    dve.wait_ge(gate_mm, n + 1)
                    after(dve, hrounded, n - 1)
                    dve.tensor_tensor(gate[:, s, :], ps_g[:].rearrange("p b n -> p (b n)")[:, :FF], scale_rows[:, :FF], ALU.mult).then_inc(gate_out, 1)
                    dve.wait_ge(up_mm, n + 1)
                    dve.tensor_tensor(up[:, s, :], ps_u[:].rearrange("p b n -> p (b n)")[:, :FF], scale_rows[:, FF:2 * FF], ALU.mult).then_inc(up_out, 1)
                if runs(n, -1):
                    dve.wait_ge(hscaled, n)
                    exponent_of(dve, he[:, 1 - s, :], gate[:, 1 - s, :], hexps)
                    dve.wait_ge(hexps, n)
                    rounder_of(dve, he[:, 1 - s, :], hrounders)
                if runs(n, -3):
                    output(n - 3, 1 - s)
                if runs(n, 0):
                    dve.wait_ge(prod_done, n + 1)
                    dve.tensor_reduce(htop[:, s, 0:1], gate[:, s, :], AX_X, ALU.max, apply_absolute_value=True).then_inc(htops, 1)
                    dve.wait_ge(htops, 4 * n + 1)
                    dve.tensor_scalar(htop[:, s, 1:2], htop[:, s, 0:1], 1.0 / FP8_MAX, None, ALU.mult).then_inc(htops, 1)
                    dve.wait_ge(htops, 4 * n + 2)
                    dve.reciprocal(htop[:, s, 2:3], htop[:, s, 1:2]).then_inc(htops, 1)
                    dve.tensor_scalar(column(y_scale, n), htop[:, s, 1:2], column(out_scale, n), None, ALU.mult).then_inc(htops, 1)
                if runs(n, -1):
                    dve.wait_ge(hshifted, n)
                    after(dve, hturned, 2 * (n - 2))
                    dve.tensor_tensor(hq[:, 1 - s, :], gate[:, 1 - s, :], he[:, 1 - s, :], ALU.subtract).then_inc(hrounded, 1)
            steps(dve, step)
            dve.wait_ge(x_done, NT)


def weight_buffers(sb, sem):
    return {
        "idx": sb("w_idx", [P, FC], I32),
        "raw": sb("w_raw", [P, 2 * FC, D]),
        "raw_d": sb("w_rawd", [P, KC, FF]),
        "idx_loaded": sem("w_idx_loaded"),
        "gathered": sem("w_gathered"),
        "down_loaded": sem("w_down_loaded"),
    }

H = 16
HP = H // 2
R = 64
CQ = 384
QC = CQ // P
NP_ = B * HP
HALF = R


def scratch(nc, name, shape):
    return nc.dram_tensor(name, shape, F32).ap()


def one(a, n):
    names = "bcdefg"[:len(a.shape) - 1]
    spaced = " ".join(names)
    return a[bass.ds(n, 1)].rearrange(f"a {spaced} -> (a {names[0]}) {spaced[2:]}") if not isinstance(n, int) else a[n]


def stage_prepare_heads(nc, sem, d, scr, x_res, mean, rstd, ident, out_w):
    with ExitStack() as ctx:
        sb, ps, _ = ring(ctx, nc)
        kv = sb("p_kv", [P, NT, DC])
        cos = sb("p_cos", [P, TPB, DC])
        sin = sb("p_sin", [P, TPB, DC])
        rot = sb("p_rot", [P, TPB, DC])
        kvs = sb("p_kvs", [P, 2, TPB, DC], F32R)
        kvTs = sb("p_kvTs", [P, 2, S], F32R)
        wkr = sb("p_wkr", [P, H, 2, R])
        wkrs = sb("p_wkrs", [P, HP, 2, 2, P], F32R)
        cqT = sb("p_cqT", [P, 2, QC, P])
        wqr = sb("p_wqr", [P, 2, QC, R])
        wq = sb("p_wq", [P, 2, D])
        wkv = sb("p_wkv", [P, 2, DC])
        woT = sb("p_woT", [P, 2, D])
        mid = sb("p_mid", [P, 2, R])
        a_hl = sb("p_a", [P, KC, 2, P], F32R)
        xn = sb("p_xn", [P, 2, D])
        xT = sb("p_xT", [P, 2, KC, 2, P], F32R)
        stats = sb("p_stats", [P, NT, 6])
        mv = sb("p_mv", [P, NT, 2])
        var_eps = sb("p_vareps", [P, NT])
        m_half = sb("p_mhalf", [P, NT])
        ps_m = ps("p_psm", [P, 2, 512])
        ps_a = ps("p_psa", [P, KC, 2, R])
        ps_b = ps("p_psb", [P, 2, D])
        ps_t = ps("p_pst", [P, 2, 512])

        kv_loaded = sem("p_kv_loaded")
        kr_loaded = sem("p_kr_loaded")
        rope_done = sem("p_rope_done")
        kv_hi = sem("p_kv_hi")
        kv_lo = sem("p_kv_lo")
        kv_turned = sem("p_kv_turned")
        kvT_hi = sem("p_kvT_hi")
        kvT_lo = sem("p_kvT_lo")
        kv_stored = sem("p_kv_stored")
        kr_hi = sem("p_kr_hi")
        kr_lo = sem("p_kr_lo")
        w_loaded = [sem(f"p_w_loaded{s}") for s in range(2)]
        mid_mm = sem("p_mid_mm")
        mid_done = sem("p_mid_done")
        a_mm = sem("p_a_mm")
        a_hi = sem("p_a_hi")
        a_lo = sem("p_a_lo")
        a_stored = sem("p_a_stored")
        b_mm = sem("p_b_mm")
        b_hi = sem("p_b_hi")
        b_lo = sem("p_b_lo")
        halves = sem("p_halves")
        stats_done = sem("p_stats_done")
        rstd_done = sem("p_rstd_done")
        normed = sem("p_normed")
        x_turned = sem("p_x_turned")
        x_hi = sem("p_x_hi")
        x_lo = sem("p_x_lo")
        xT_stored = [sem(f"p_xT_stored{s}") for s in range(2)]
        x_stored = sem("p_x_stored")

        block = ctx.enter_context(nc.Block())

        @block.sync
        def _(sp):
            sp.dma_start(kv[:], d["ctx"].rearrange("(n p) c -> p n c", p=P)).then_inc(kv_loaded, 16)
            sp.dma_start(cos[:], d["rope_cos"].rearrange("(n p) c -> p n c", p=P)).then_inc(kv_loaded, 16)
            sp.dma_start(sin[:], d["rope_sin"].rearrange("(n p) c -> p n c", p=P)).then_inc(kv_loaded, 16)
            for j in range(2):
                sp.dma_start(wkr[:, :, j, :], d["W_krT"].rearrange("c (h r) -> c h r", r=R)).then_inc(kr_loaded, 16)
            sp.dma_start(scr["x2"].rearrange("(n p) c -> p n c", p=P), x_res[:]).then_inc(x_stored, 16)

            def load_head(i, s):
                h = 2 * i + s
                sp.dma_start(cqT[:, s, :, :], one(d["w_kc_qT"], h).rearrange("(c p) k -> p c k", p=P)).then_inc(w_loaded[s], 16)
                sp.dma_start(wqr[:, s, :, :], one(d["W_qr"], h).rearrange("(c p) r -> p c r", p=P)).then_inc(w_loaded[s], 16)
                sp.dma_start(wq[:, s, :], one(d["L1_Wq"], h)).then_inc(w_loaded[s], 16)
                sp.dma_start(wkv[:, s, :], one(d["w_kc_kv"], h)).then_inc(w_loaded[s], 16)
                sp.dma_start(woT[:, s, :], one(d["WoT"], h)).then_inc(w_loaded[s], 16)

            for s in range(2):
                load_head(0, s)
            for b in range(B):
                sp.wait_ge(kv_lo, b + 1)
                sp.dma_start(scr["kv"][b], kvs[:].rearrange("p a t c -> p (a t c)").bitcast(F32)).then_inc(kv_stored, 16)
                sp.wait_ge(kvT_lo, b + 1)
                sp.dma_start(scr["kvT"][b], kvTs[:].rearrange("p a l -> p (a l)").bitcast(F32)).then_inc(kv_stored, 16)
            sp.wait_ge(kr_lo, 2)
            sp.dma_start(scr["kr"].rearrange("g p n -> p g n"), wkrs[:].rearrange("p g h a n -> p g (h a n)").bitcast(F32)).then_inc(kv_stored, 16)
            with sp.Fori(0, HP - 1) as i:
                for s in range(2):
                    sp.wait_ge(a_mm, i + 2)
                    load_head(i + 1, s)
                sp.wait_ge(a_lo, i + 2)
                sp.dma_start(one(scr["a"], i), a_hl[:].rearrange("p c a n -> p (c a n)").bitcast(F32)).then_inc(a_stored, 16)
            sp.wait_ge(a_lo, HP + 1)
            sp.dma_start(scr["a"][HP - 1], a_hl[:].rearrange("p c a n -> p (c a n)").bitcast(F32)).then_inc(a_stored, 16)
            xT_dram = scr["xT"].rearrange("b p (c a t n) -> b t p c a n", c=KC, a=2, t=TPB)
            with sp.Fori(0, B) as b:
                for t in range(TPB):
                    sp.wait_ge(x_lo, TPB * b + t + 1 + 2)
                    sp.dma_start(one(xT_dram, b)[t].rearrange("p c a n -> p (c a) n"),
                                 xT[:, t % 2].rearrange("p c a n -> p (c a) n").bitcast(F32)).then_inc(xT_stored[t % 2], 16)
            sp.wait_ge(x_stored, 16)
            sp.wait_ge(kv_stored, 16 * (2 * B + 1))
            sp.wait_ge(a_stored, 16 * (HP + 1))
            for s in range(2):
                sp.wait_ge(xT_stored[s], 16 * (NT // 2 + 1))

        @block.gpsimd
        def _(pool):
            pool.memset(m_half[:], -0.5).then_inc(halves, 1)
            pool.wait_ge(kv_loaded, 48)
            for b in range(B):
                rows = kv[:, TPB * b:TPB * (b + 1), :]
                if b:
                    pool.wait_ge(rope_done, 4 * b)
                pool.tensor_tensor(rot[:, :, :DC // 2], rows[:, :, DC // 2:], sin[:, :, :DC // 2], ALU.mult).then_inc(rope_done, 1)
                pool.tensor_tensor(rot[:, :, DC // 2:], rows[:, :, :DC // 2], sin[:, :, DC // 2:], ALU.mult).then_inc(rope_done, 1)
                pool.wait_ge(rope_done, 4 * b + 2)
                pool.tensor_tensor(rows, rows, cos[:], ALU.mult).then_inc(rope_done, 1)
                pool.wait_ge(rope_done, 4 * b + 3)
                pool.tensor_tensor(rows, rows, rot[:], ALU.add).then_inc(rope_done, 1)
            pool.wait_ge(halves, 1)
            pool.wait_ge(stats_done, 2 * NT + 1)
            pool.tensor_tensor(rstd[:], var_eps[:], m_half[:], ALU.pow).then_inc(rstd_done, 1)

        @block.tensor
        def _(pe):
            for b in range(B):
                pe.wait_ge(rope_done, 4 * b + 4)
                if b >= 2:
                    pe.wait_ge(kvT_lo, b - 1)
                for t in range(TPB):
                    ins = pe.transpose(ps_t[:, b % 2, t * P:(t + 1) * P], kv[:, TPB * b + t, :], ident[:])
                ins.then_inc(kv_turned, 1)
            with pe.Fori(0, HP) as i:
                for s in range(2):
                    pe.wait_ge(w_loaded[s], 80 * (i + 1))
                    pe.wait_ge(mid_done, 2 * i + s + 1)
                    for c in range(QC):
                        ins = pe.matmul(ps_m[:, s, :R], cqT[:, s, c, :], wqr[:, s, c, :], start=(c == 0), stop=(c == QC - 1))
                    ins.then_inc(mid_mm, 1)
                for s in range(2):
                    pe.wait_ge(b_lo, 2 * i + s + 1)
                    pe.matmul(ps_b[:, s, :], wkv[:, s, :], woT[:, s, :], start=True, stop=True).then_inc(b_mm, 1)
                pe.wait_ge(a_lo, i + 1)
                for s in range(2):
                    pe.wait_ge(mid_done, 2 * i + s + 1 + 2)
                    for c in range(KC):
                        ins = pe.matmul(ps_a[:, c, s, :], wq[:, s, c * P:(c + 1) * P], mid[:, s, :], start=True, stop=True)
                ins.then_inc(a_mm, 1)
            with pe.Fori(0, B) as b:
                for t in range(TPB):
                    pe.wait_ge(normed, TPB * b + t + 1)
                    pe.wait_ge(x_lo, TPB * b + t + 1)
                    for c in range(KC):
                        ins = pe.transpose(ps_t[:, t % 2, c * P:(c + 1) * P], xn[:, t % 2, c * P:(c + 1) * P], ident[:])
                    ins.then_inc(x_turned, 1)

        @block.scalar
        def _(act):
            for b in range(B):
                act.wait_ge(rope_done, 4 * b + 4)
                if b:
                    act.wait_ge(kv_stored, 32 * b)
                act.activation(kvs[:, 0], kv[:, TPB * b:TPB * (b + 1), :], ACT.Copy).then_inc(kv_hi, 1)
                act.wait_ge(kv_turned, b + 1)
                act.activation(kvTs[:, 0, :], ps_t[:, b % 2, :], ACT.Copy).then_inc(kvT_hi, 1)
            act.wait_ge(kr_loaded, 32)
            for h in range(2):
                act.activation(wkrs[:, :, h, 0, :], wkr[:].rearrange("p (g h) j r -> p h g (j r)", h=2)[:, h], ACT.Copy).then_inc(kr_hi, 1)
            with act.Fori(0, HP) as i:
                for s in range(2):
                    act.wait_ge(mid_mm, 2 * i + s + 1)
                    act.wait_ge(a_mm, i + 1)
                    act.activation(mid[:, s, :], ps_m[:, s, :R], ACT.Copy).then_inc(mid_done, 1)
                for s in range(2):
                    act.wait_ge(b_mm, 2 * i + s + 1)
                    act.activation(out_w[:, bass.ds(2 * i + s, 1), 0, :].rearrange("p o n -> p (o n)"), ps_b[:, s, :], ACT.Copy).then_inc(b_hi, 1)
                act.wait_ge(a_mm, i + 2)
                act.wait_ge(a_stored, 16 * (i + 1))
                act.activation(a_hl[:, :, 0, :], ps_a[:].rearrange("p c s r -> p c (s r)"), ACT.Copy).then_inc(a_hi, 1)
            with act.Fori(0, B) as b:
                for t in range(TPB):
                    act.wait_ge(x_turned, TPB * b + t + 1 + 2)
                    act.wait_ge(xT_stored[t % 2], 16 * (2 * b + t // 2 + 1))
                    act.activation(xT[:, t % 2, :, 0, :], ps_t[:, t % 2, :].rearrange("p (c n) -> p c n", n=P), ACT.Copy).then_inc(x_hi, 1)

        @block.vector
        def _(dve):
            dve.sem_inc(mid_done, 2)
            dve.sem_inc(b_lo, 2)
            dve.sem_inc(a_lo, 1)
            dve.sem_inc(a_mm, 1)
            dve.sem_inc(a_stored, 16)
            dve.sem_inc(x_lo, 2)
            dve.sem_inc(x_turned, 2)
            for s in range(2):
                dve.sem_inc(xT_stored[s], 16)
            for n in range(NT):
                dve.bn_stats(stats[:, n, :], x_res[:, n, :]).then_inc(stats_done, 1)
            for n in range(NT):
                dve.wait_ge(stats_done, n + 1)
                dve.bn_aggr(mv[:, n, :], stats[:, n, :]).then_inc(stats_done, 1)
            dve.wait_ge(stats_done, 2 * NT)
            dve.tensor_scalar(var_eps[:], mv[:, :, 1], LN_EPS, None, ALU.add).then_inc(stats_done, 1)
            dve.tensor_copy(mean[:], mv[:, :, 0]).then_inc(stats_done, 1)
            for b in range(B):
                dve.wait_ge(kv_hi, b + 1)
                if b:
                    dve.wait_ge(kv_stored, 32 * b)
                dve.tensor_tensor(kvs[:, 1], kv[:, TPB * b:TPB * (b + 1), :], kvs[:, 0].bitcast(F32), ALU.subtract).then_inc(kv_lo, 1)
                dve.wait_ge(kvT_hi, b + 1)
                dve.tensor_tensor(kvTs[:, 1, :], ps_t[:, b % 2, :], kvTs[:, 0, :].bitcast(F32), ALU.subtract).then_inc(kvT_lo, 1)
            for h in range(2):
                dve.wait_ge(kr_hi, h + 1)
                dve.tensor_tensor(wkrs[:, :, h, 1, :], wkr[:].rearrange("p (g h) j r -> p h g (j r)", h=2)[:, h],
                                  wkrs[:, :, h, 0, :].bitcast(F32), ALU.subtract).then_inc(kr_lo, 1)
            with dve.Fori(0, HP) as i:
                for s in range(2):
                    dve.wait_ge(b_hi, 2 * i + s + 1)
                    dve.tensor_tensor(out_w[:, bass.ds(2 * i + s, 1), 1, :].rearrange("p o n -> p (o n)"), ps_b[:, s, :],
                                      out_w[:, bass.ds(2 * i + s, 1), 0, :].rearrange("p o n -> p (o n)").bitcast(F32), ALU.subtract).then_inc(b_lo, 1)
                dve.wait_ge(a_hi, i + 1)
                dve.tensor_tensor(a_hl[:, :, 1, :], ps_a[:].rearrange("p c s r -> p c (s r)"), a_hl[:, :, 0, :].bitcast(F32), ALU.subtract).then_inc(a_lo, 1)
            dve.wait_ge(rstd_done, 1)
            dve.wait_ge(stats_done, 2 * NT + 2)

            def norm(b, t):
                n = TPB * b + t
                dve.wait_ge(x_turned, n + 1)
                dve.tensor_scalar(xn[:, t % 2, :], tile_of(x_res, n), mean[:, bass.ds(n, 1)], rstd[:, bass.ds(n, 1)],
                                  ALU.subtract, ALU.mult).then_inc(normed, 1)
            with dve.Fori(0, B) as b:
                for t in range(TPB):
                    n = TPB * b + t
                    if t == 0:
                        norm(b, 0)
                    if t < TPB - 1:
                        norm(b, t + 1)
                    dve.wait_ge(x_hi, n + 1)
                    dve.wait_ge(xT_stored[t % 2], 16 * (2 * b + t // 2 + 1))
                    dve.tensor_tensor(xT[:, t % 2, :, 1, :], ps_t[:, t % 2, :].rearrange("p (c n) -> p c n", n=P),
                                      xT[:, t % 2, :, 0, :].bitcast(F32), ALU.subtract).then_inc(x_lo, 1)


def stage_latent_attention(nc, sem, scr, x_out, ident, out_w):
    UNITS, HEADS, ITERS = 32, 8, B * H // 8
    TURN_LAG, PV_LAG, OUT_LAG = 2, 6, 23
    QUAD = 4
    with ExitStack() as ctx:
        sb, ps, _ = ring(ctx, nc)
        a_w = sb("l_aw", [P, 2, KC, 2, P], F32R)
        kr_w = sb("l_krw", [P, 2, 2, 2, P], F32R)
        xT = sb("l_xT", [P, KC, 2, S], F32R)
        kvT = sb("l_kvT", [P, 2, S], F32R)
        kv = sb("l_kv", [P, 2, TPB, DC], F32R)
        q_st = sb("l_qst", [P, 2, 2, S], F32R)
        k_st = sb("l_kst", [P, 2, 2, 2, S], F32R)
        prob = sb("l_prob", [P, 4, S])
        pT = sb("l_pT", [P, 2, 2, TPB, S], F32R)
        cT = sb("l_cT", [P, HEADS, 2, S], F32R)
        acc = sb("l_acc", [P, TPB, D])
        nmax = sb("l_nmax", [P, 4])
        rsum = sb("l_rsum", [P, 4])
        rinv = sb("l_rinv", [P, 4])
        ps_s = ps("l_pss", [P, 2, S])
        ps_p = ps("l_psp", [P, 2, S])
        ps_qk = ps("l_psqk", [P, S])
        ps_c = ps("l_psc", [P, 2, S])
        ps_o = ps("l_pso", [P, D])

        w_loaded = [sem(f"l_w_loaded{s}") for s in range(2)]
        xT_loaded = [sem(f"l_xT_loaded{c}") for c in range(KC)]
        kvT_loaded = sem("l_kvT_loaded")
        kv_loaded = sem("l_kv_loaded")
        acc_loaded = [sem(f"l_acc_loaded{t}") for t in range(TPB)]
        acc_stored = [sem(f"l_acc_stored{t}") for t in range(TPB)]
        q_mm = sem("l_q_mm")
        k_mm = sem("l_k_mm")
        st_hi = sem("l_st_hi")
        st_lo = sem("l_st_lo")
        s_mm = sem("l_s_mm")
        max_done = sem("l_max_done")
        exp_done = sem("l_exp_done")
        rinv_done = sem("l_rinv_done")
        normed = sem("l_normed")
        turned = sem("l_turned")
        pT_hi = sem("l_pT_hi")
        pT_lo = sem("l_pT_lo")
        c_mm = sem("l_c_mm")
        c_hi = sem("l_c_hi")
        c_lo = sem("l_c_lo")
        out_mm = sem("l_out_mm")
        added = sem("l_added")

        def flat(a):
            letters = "bcdefg"[:len(a.shape) - 1]
            return a.rearrange(f"p {' '.join(letters)} -> p ({' '.join(letters)})").bitcast(F32)

        def iterations(eng, unit, tail):
            for j in range(UNITS):
                unit(0, j)
            with eng.Fori(1, ITERS - 1) as n:
                for j in range(UNITS):
                    unit(n, j)
            for j in range(UNITS):
                unit(ITERS - 1, j)
            for j in range(UNITS, UNITS + tail):
                unit(ITERS - 1, j)

        def lagged(n, j, lag):
            at = j - lag
            if isinstance(n, int) and n == 0 and at < 0:
                return None
            if at >= UNITS:
                return None
            return at

        def next_pair(n, j):
            if j >= UNITS or (isinstance(n, int) and n == ITERS - 1 and j >= UNITS - 8):
                return None
            return n * 4 + j // 8 + 1, (j // 8 + 1) % 2

        def out_step(n, j):
            at = j - OUT_LAG
            if isinstance(n, int) and n == 0 and at < 0:
                return None
            quad, i = at // 16, at % 16
            if isinstance(n, int) and n == ITERS - 1 and quad > 1:
                return None
            return quad, i // 4, i % 4

        block = ctx.enter_context(nc.Block())

        @block.sync
        def _(sp):
            def load_pair(p, slot, h):
                sp.dma_start(flat(a_w[:, slot]), one(scr["a"], h)).then_inc(w_loaded[slot], 16)
                sp.dma_start(flat(kr_w[:, slot]), one(scr["kr"], h)).then_inc(w_loaded[slot], 16)

            def load_tokens(b):
                for c in range(KC):
                    sp.dma_start(flat(xT[:, c]), one(scr["xT"], b)[:, c * 2 * S:(c + 1) * 2 * S]).then_inc(xT_loaded[c], 16)

            def load_keys(b):
                sp.dma_start(flat(kvT), one(scr["kvT"], b)).then_inc(kvT_loaded, 16)

            x2 = scr["x2"].rearrange("(b t p) c -> b t p c", b=B, p=P)
            x3 = x_out.rearrange("(b t p) c -> b t p c", b=B, p=P)

            load_pair(0, 0, 0)
            load_tokens(0)
            load_keys(0)
            load_pair(1, 1, 1)
            sp.dma_start(flat(kv), scr["kv"][0]).then_inc(kv_loaded, 16)
            for t in range(TPB):
                sp.dma_start(acc[:, t, :], x2[0, t]).then_inc(acc_loaded[t], 16)

            def batch(b, first=False, last=False):
                if not first:
                    sp.wait_ge(c_mm, H * b)
                    sp.dma_start(flat(kv), one(scr["kv"], b)).then_inc(kv_loaded, 16)
                for p in range(HP):
                    if p == HP - 1 and not last:
                        sp.wait_ge(q_mm, HP * (b + 1))
                        load_tokens(b + 1)
                    if not (last and p >= HP - 2):
                        sp.wait_ge(k_mm, 2 * (HP * b + p + 1))
                        load_pair(None, p % 2, (p + 2) % HP)
                    if p == HP - 1 and not last:
                        load_keys(b + 1)
                    if not first and p in (1, 2):
                        for t in (2 * p - 2, 2 * p - 1):
                            swap(b, t)

            def swap(b, t):
                sp.wait_ge(added, (4 * b - 1) * TPB + t + 1)
                sp.dma_start(one(x3, b - 1)[t], acc[:, t, :]).then_inc(acc_stored[t], 16)
                sp.wait_ge(acc_stored[t], 16 * b)
                sp.dma_start(acc[:, t, :], one(x2, b)[t]).then_inc(acc_loaded[t], 16)

            batch(0, first=True)
            with sp.Fori(1, B - 1) as b:
                batch(b)
            batch(B - 1, last=True)
            for t in range(TPB):
                sp.wait_ge(added, (4 * B - 1) * TPB + t + 1)
                sp.dma_start(x3[B - 1, t], acc[:, t, :]).then_inc(acc_stored[t], 16)
            for t in range(TPB):
                sp.wait_ge(acc_stored[t], 16 * B)

        @block.gpsimd
        def _(pool):
            def unit(n, j):
                if j < UNITS:
                    pool.wait_ge(rinv_done, UNITS * n + j + 1)
                    pool.tensor_tensor(prob[:, j % 4, :], prob[:, j % 4, :], rinv[:, j % 4:j % 4 + 1].broadcast_to([P, S]), ALU.mult).then_inc(normed, 1)
            iterations(pool, unit, 0)

        @block.tensor
        def _(pe):
            def queries(p, slot, c):
                if c == 0:
                    after(pe, st_lo, 4 * p)
                    pe.wait_ge(w_loaded[slot], 32 * (p // 2 + 1))
                pe.wait_ge(xT_loaded[c], 16 * (p // HP + 1))
                for m, (x, y) in enumerate(((0, 0), (0, 1), (1, 0))):
                    ins = pe.matmul(ps_qk[:], a_w[:, slot, c, x, :], xT[:, c, y, :], start=(c == 0 and m == 0), stop=(c == KC - 1 and m == 2))
                if c == KC - 1:
                    ins.then_inc(q_mm, 1)

            def keys(p, slot, h):
                pe.wait_ge(st_lo, 4 * p + 2 + h)
                pe.wait_ge(kvT_loaded, 16 * (p // HP + 1))
                for m, (x, y) in enumerate(((0, 0), (0, 1), (1, 0))):
                    ins = pe.matmul(ps_qk[:], kr_w[:, slot, h, x, :], kvT[:, y, :], start=(m == 0), stop=(m == 2))
                ins.then_inc(k_mm, 1)

            def unit(n, j):
                u = UNITS * n + j
                if j < UNITS:
                    pair, h, t = j // 8, j // 4 % 2, j % 4
                    if t == 0:
                        pe.wait_ge(st_lo, 4 * (4 * n + pair) + 3 + h)
                    after(pe, exp_done, u - 1)
                    for x in range(2):
                        ins = pe.matmul(ps_s[:, j % 2, :], q_st[:, pair % 2, h, t * P:(t + 1) * P], k_st[:, pair % 2, h, x, :],
                                        start=(x == 0), stop=(x == 1))
                    ins.then_inc(s_mm, 1)
                if (at := lagged(n, j, TURN_LAG)) is not None:
                    pe.wait_ge(normed, u - TURN_LAG + 1)
                    after(pe, pT_lo, u - TURN_LAG - 1)
                    for c in range(TPB):
                        ins = pe.transpose(ps_p[:, at % 2, c * P:(c + 1) * P], prob[:, at % 4, c * P:(c + 1) * P], ident[:])
                    ins.then_inc(turned, 1)
                if (at := lagged(n, j, PV_LAG)) is not None:
                    c = at % 4
                    g = HEADS * n + at // 4
                    slot = (at // 4) % 2
                    if c == 0:
                        pe.wait_ge(pT_lo, 4 * g + 4)
                        after(pe, c_lo, g - 1)
                        pe.wait_ge(kv_loaded, 16 * (g // H + 1))
                    for m, (x, y) in enumerate(((0, 0), (0, 1), (1, 0))):
                        ins = pe.matmul(ps_c[:, slot, :], kv[:, x, c, :], pT[:, slot, y, c, :],
                                        start=(c == 0 and m == 0), stop=(c == TPB - 1 and m == 2))
                    if c == TPB - 1:
                        ins.then_inc(c_mm, 1)
                if (at := out_step(n, j)) is not None:
                    quad, t, step = at
                    q_index = UNITS // 16 * n + quad
                    products = [(k, x, y) for k in range(QUAD) for x, y in ((0, 0), (0, 1), (1, 0))]
                    if step == 1:
                        after(pe, added, TPB * q_index + t)
                        if t == 0:
                            pe.wait_ge(c_lo, QUAD * (q_index + 1))
                    for k, x, y in products[4 * (step - 1):4 * step] if step else ():
                        slot = (QUAD * quad + k) % HEADS
                        g = (QUAD * (q_index % (H // QUAD))) + k
                        w = out_w[:, g, y, :] if isinstance(g, int) else out_w[:, bass.ds(g, 1), y, :].rearrange("p o n -> p (o n)")
                        ins = pe.matmul(ps_o[:], cT[:, slot, x, t * P:(t + 1) * P], w, start=((k, x, y) == products[0]), stop=((k, x, y) == products[-1]))
                    if step == 3:
                        ins.then_inc(out_mm, 1)
                if (np := next_pair(n, j)) is not None:
                    p, slot = np
                    prepare(p, slot, j % 8)

            def prepare(p, slot, i):
                if i == 2:
                    queries(p, slot, 0)
                elif i == 3:
                    for c in range(1, KC):
                        queries(p, slot, c)
                elif i in (5, 7):
                    keys(p, slot, (i - 5) // 2)

            for i in range(8):
                prepare(0, 0, i)
            iterations(pe, unit, OUT_LAG)

        @block.scalar
        def _(act):
            def keep_queries(p, slot):
                act.wait_ge(q_mm, p + 1)
                after(act, s_mm, 8 * (p - 1))
                for h in range(2):
                    rows = slice(h * R, (h + 1) * R)
                    act.activation(q_st[rows, slot, h, :], ps_qk[rows, :], ACT.Copy).then_inc(st_hi, 1)

            def keep_keys(p, slot, h):
                act.wait_ge(k_mm, 2 * p + h + 1)
                act.activation(k_st[:, slot, h, 0, :], ps_qk[:], ACT.Copy).then_inc(st_hi, 1)

            def prepare(p, slot, i):
                if i == 4:
                    keep_queries(p, slot)
                if i == 6:
                    keep_keys(p, slot, 0)

            def unit(n, j):
                u = UNITS * n + j
                if (at := lagged(n, j, TURN_LAG)) is not None:
                    act.wait_ge(turned, u - TURN_LAG + 1)
                    g = HEADS * n + at // 4
                    if at % 4 == 0:
                        after(act, c_mm, g - 1)
                    act.activation(pT[:, (at // 4) % 2, 0, :, (at % 4) * P:(at % 4 + 1) * P],
                                   ps_p[:, at % 2, :].rearrange("p (c n) -> p c n", n=P), ACT.Copy).then_inc(pT_hi, 1)
                if j < UNITS:
                    act.wait_ge(max_done, u + 1)
                    after(act, turned, u - 3)
                    act.activation(prob[:, j % 4, :], ps_s[:, j % 2, :], ACT.Exp, bias=nmax[:, j % 4:j % 4 + 1],
                                   accum_out=rsum[:, j % 4:j % 4 + 1]).then_inc(exp_done, 1)
                if j % 4 == 2 and (at := lagged(n, j, PV_LAG + 4)) is not None:
                    g = HEADS * n + at // 4
                    act.wait_ge(c_mm, g + 1)
                    after(act, out_mm, TPB * (UNITS // 16 * n + at // 16))
                    act.activation(cT[:, (at // 4) % HEADS, 0, :], ps_c[:, (at // 4) % 2, :], ACT.Copy).then_inc(c_hi, 1)
                if j % 8 == 0 and j < UNITS:
                    keep_keys(4 * n + j // 8, (j // 8) % 2, 1)
                if (np := next_pair(n, j)) is not None:
                    prepare(np[0], np[1], j % 8)

            for i in range(8):
                prepare(0, 0, i)
            iterations(act, unit, PV_LAG + 5)

        @block.vector
        def _(dve):
            def keep_queries(p, slot):
                for h in range(2):
                    rows, other = slice(h * R, (h + 1) * R), slice((1 - h) * R, (2 - h) * R)
                    dve.wait_ge(st_hi, 4 * p + h + 1)
                    dve.tensor_tensor(q_st[other, slot, h, :], ps_qk[rows, :], q_st[rows, slot, h, :].bitcast(F32), ALU.subtract).then_inc(st_lo, 1)

            def keep_keys(p, slot, h):
                dve.wait_ge(st_hi, 4 * p + 3 + h)
                dve.tensor_tensor(k_st[:, slot, h, 1, :], ps_qk[:], k_st[:, slot, h, 0, :].bitcast(F32), ALU.subtract).then_inc(st_lo, 1)

            def prepare(p, slot, i):
                if i == 4:
                    keep_queries(p, slot)
                if i == 6:
                    keep_keys(p, slot, 0)

            def invert(n, j):
                dve.wait_ge(exp_done, UNITS * n + j + 1)
                dve.reciprocal(rinv[:, j % 4:j % 4 + 1], rsum[:, j % 4:j % 4 + 1]).then_inc(rinv_done, 1)

            def unit(n, j):
                u = UNITS * n + j
                if (at := lagged(n, j, 1)) is not None:
                    invert(n, at)
                if j < UNITS:
                    dve.wait_ge(s_mm, u + 1)
                    dve.tensor_reduce(nmax[:, j % 4:j % 4 + 1], ps_s[:, j % 2, :], AX_X, ALU.max, negate=True).then_inc(max_done, 1)
                if (at := lagged(n, j, TURN_LAG)) is not None:
                    dve.wait_ge(pT_hi, u - TURN_LAG + 1)
                    slot, cols = (at // 4) % 2, slice((at % 4) * P, (at % 4 + 1) * P)
                    dve.tensor_tensor(pT[:, slot, 1, :, cols], ps_p[:, at % 2, :].rearrange("p (c n) -> p c n", n=P),
                                      pT[:, slot, 0, :, cols].bitcast(F32), ALU.subtract).then_inc(pT_lo, 1)
                if j % 4 == 2 and (at := lagged(n, j, PV_LAG + 4)) is not None:
                    g = HEADS * n + at // 4
                    dve.wait_ge(c_hi, g + 1)
                    slot = (at // 4) % HEADS
                    dve.tensor_tensor(cT[:, slot, 1, :], ps_c[:, (at // 4) % 2, :], cT[:, slot, 0, :].bitcast(F32), ALU.subtract).then_inc(c_lo, 1)
                if j % 4 == 3 and (at := out_step(n, j - 1)) is not None:
                    quad, t, _ = at
                    q_index = UNITS // 16 * n + quad
                    dve.wait_ge(out_mm, TPB * q_index + t + 1 + TPB)
                    dve.wait_ge(acc_loaded[t], 16 * (q_index // (H // QUAD) + 1))
                    dve.wait_ge(added, TPB * q_index + t) if not isinstance(n, int) or n or quad or t else None
                    dve.tensor_tensor(acc[:, t, :], ps_o[:], acc[:, t, :], ALU.add).then_inc(added, 1)
                if j % 8 == 0 and j < UNITS:
                    keep_keys(4 * n + j // 8, (j // 8) % 2, 1)
                if (np := next_pair(n, j)) is not None:
                    prepare(np[0], np[1], j % 8)

            dve.sem_inc(out_mm, TPB)
            for i in range(8):
                prepare(0, 0, i)
            iterations(dve, unit, OUT_LAG + 1)

E = 32
RE = 16
TOP = 2


def stage_routed_experts(nc, sem, d, x_in, out, ident):
    with ExitStack() as ctx:
        sb, ps, _ = ring(ctx, nc)
        raw_u = sb("e_rawu", [P, KC, E * RE])
        raw_v = sb("e_rawv", [P, KC, D])
        raw_r = sb("e_rawr", [P, KC, E])
        u_w = sb("e_uw", [P, KC, 2, E * RE], F32R)
        v_w = sb("e_vw", [P, KC, 2, D], F32R)
        r_w = sb("e_rw", [P, KC, 2, E], F32R)
        attr = sb("e_attr", [P, E, 32])
        wa = sb("e_wa", [P, 32])
        aw = sb("e_aw", [P, 4, E])
        order = sb("e_order", [P, E])
        eps = sb("e_eps", [P, 2])
        x = sb("e_x", [P, NT, D])
        xn = sb("e_xn", [P, D])
        stats = sb("e_stats", [P, 2, 6])
        mv = sb("e_mv", [P, 2, 2])
        var_eps = sb("e_vareps", [P, 2])
        rstd = sb("e_rstd", [P, 2])
        xT = sb("e_xT", [P, 2, KC, 2, P], F32R)
        sc = sb("e_sc", [P, 2, E])
        best = sb("e_best", [P, 2, 8])
        which = sb("e_which", [P, 2, 8], U32)
        whichf = sb("e_whichf", [P, 2, TOP])
        nbest = sb("e_nbest", [P, 2])
        g = sb("e_g", [P, 2, 4, E])
        small = sb("e_small", [P, 2, 8])
        y_gate = sb("e_ygate", [P, NT])
        hid = sb("e_hid", [P, 2, E * RE])
        hT = sb("e_hT", [P, 2, KC, 2, P], F32R)
        res = sb("e_res", [P, 2, D])
        ps_t = ps("e_pst", [P, 2, D])
        ps_s = ps("e_pss", [P, 2, D])
        ps_h = ps("e_psh", [P, 2, E * RE])
        ps_v = ps("e_psv", [P, 2, D])

        w_loaded = [sem(f"e_w_loaded{i}") for i in range(3)]
        a_loaded = sem("e_a_loaded")
        x_loaded = [sem(f"e_x_loaded{b}") for b in range(B)]
        setup = sem("e_setup")
        aw_done = sem("e_aw_done")
        aw_exp = sem("e_aw_exp")
        w_hi = sem("e_w_hi")
        w_lo = sem("e_w_lo")
        stats_done = sem("e_stats_done")
        rstd_done = sem("e_rstd_done")
        normed = sem("e_normed")
        x_turned = sem("e_x_turned")
        xT_hi = sem("e_xT_hi")
        xT_lo = sem("e_xT_lo")
        route_mm = sem("e_route_mm")
        hid_mm = sem("e_hid_mm")
        route = sem("e_route")
        exp_done = sem("e_exp_done")
        hid_done = sem("e_hid_done")
        hid_turned = sem("e_hid_turned")
        hT_hi = sem("e_hT_hi")
        hT_lo = sem("e_hT_lo")
        v_mm = sem("e_v_mm")
        res_done = sem("e_res_done")
        stored = [sem(f"e_stored{s}") for s in range(2)]
        ticks = sem("e_ticks")
        ROUTE_STEPS = 16
        passes = ((0, 0), (0, 1), (1, 0))

        def steps(eng, step):
            for n in range(5):
                step(n, n % 2)
            with eng.Fori(2, NT // 2 - 2) as i:
                step(2 * i + 1, 1)
                step(2 * i + 2, 0)
            for n in range(NT - 3, NT + 2):
                step(n, n % 2)

        def runs(n, shift):
            return not isinstance(n, int) or 0 <= n + shift < NT

        block = ctx.enter_context(nc.Block())

        @block.sync
        def _(sp):
            out_rows = out.rearrange("(n p) c -> n p c", p=P)
            def load_x(b):
                sp.dma_start(x[:, TPB * b:TPB * (b + 1), :], x_in.rearrange("(n p) c -> p n c", p=P)[:, TPB * b:TPB * (b + 1), :]).then_inc(x_loaded[b], 16)

            sp.dma_start(raw_r[:], d["WrT"].rearrange("(c p) n -> p c n", p=P)).then_inc(w_loaded[0], 16)
            load_x(0)
            sp.dma_start(raw_u[:], d["U"].rearrange("(c p) n -> p c n", p=P)).then_inc(w_loaded[1], 16)
            sp.dma_start(attr[:], d["attr"].rearrange("(o e) a -> o e a", o=1).broadcast_to([P, E, 32])).then_inc(a_loaded, 16)
            sp.dma_start(wa[:], d["Wa"].broadcast_to([P, 32])).then_inc(a_loaded, 16)
            sp.dma_start(raw_v[:], d["V"].rearrange("(c p) n -> p c n", p=P)).then_inc(w_loaded[2], 16)
            for b in range(1, B):
                load_x(b)

            def store(n, s):
                sp.wait_ge(res_done, n + 1)
                sp.dma_start(out_rows[n] if isinstance(n, int) else one(out_rows, n), res[:, s, :]).then_inc(stored[s], 16)

            def step(n, s):
                if runs(n, -2):
                    store(n - 2, s)
            steps(sp, step)
            for s in range(2):
                sp.wait_ge(stored[s], 16 * (NT // 2 + 1))

        @block.gpsimd
        def _(pool):
            pool.iota(order[:], pattern=[[1, E]], base=0, channel_multiplier=0, allow_small_or_imprecise_dtypes=True).then_inc(setup, 1)
            pool.memset(eps[:], -0.5).then_inc(setup, 1)
            pool.wait_ge(setup, 2)

            def invert_std(n, s):
                pool.wait_ge(stats_done, 3 * (n + 1))
                pool.tensor_tensor(rstd[:, s:s + 1], var_eps[:, s:s + 1], eps[:, 0:1], ALU.pow).then_inc(rstd_done, 1)

            for n in range(2):
                invert_std(n, n)

            def step(n, s):
                if runs(n, 2):
                    invert_std(n + 2, s)
            steps(pool, step)

        @block.scalar
        def _(act):
            def split(i, raw, w):
                act.wait_ge(w_loaded[i], 16)
                act.activation(w[:, :, 0, :], raw[:], ACT.Copy).then_inc(w_hi, 1)

            def keep_xT(n, s):
                act.wait_ge(x_turned, n + 1)
                after(act, hid_mm, n - 1)
                act.activation(xT[:, s, :, 0, :], ps_t[:, 0, :].rearrange("p (c n) -> p c n", n=P), ACT.Copy).then_inc(xT_hi, 1)

            split(0, raw_r, r_w)
            keep_xT(0, 0)
            split(1, raw_u, u_w)
            keep_xT(1, 1)
            act.wait_ge(aw_done, 2)
            act.activation(aw[:, 1, :], aw[:, 0, :], ACT.Exp, scale=-1.0).then_inc(aw_exp, 1)
            split(2, raw_v, v_w)

            def step(n, s):
                if runs(n, 0):
                    act.wait_ge(route, ROUTE_STEPS * n + 2)
                    act.activation(g[:, s, 0, :], sc[:, s, :], ACT.Exp, bias=nbest[:, s:s + 1], accum_out=small[:, s, 0:1]).then_inc(exp_done, 1)
                if runs(n, -1):
                    act.wait_ge(hid_turned, n)
                    after(act, v_mm, n - 2)
                    act.activation(hT[:, 1 - s, :, 0, :], ps_t[:, 1, :].rearrange("p (c n) -> p c n", n=P), ACT.Copy).then_inc(hT_hi, 1)
                if runs(n, 2):
                    keep_xT(n + 2, s)
            steps(act, step)

        @block.tensor
        def _(pe):
            def turn_x(n):
                pe.wait_ge(normed, n + 1)
                after(pe, xT_lo, n)
                for c in range(KC):
                    ins = pe.transpose(ps_t[:, 0, c * P:(c + 1) * P], xn[:, c * P:(c + 1) * P], ident[:])
                ins.then_inc(x_turned, 1)

            turn_x(0)
            turn_x(1)

            def step(n, s):
                if runs(n, 0):
                    if isinstance(n, int) and n == 0:
                        pe.wait_ge(w_lo, 1)
                    pe.wait_ge(xT_lo, n + 1)
                    after(pe, route, ROUTE_STEPS * (n - 1))
                    for c in range(KC):
                        for m, (a, b) in enumerate(passes):
                            ins = pe.matmul(ps_s[:, s, :E], xT[:, s, c, a, :], r_w[:, c, b, :], start=(c == 0 and m == 0), stop=(c == KC - 1 and m == 2))
                    ins.then_inc(route_mm, 1)
                    if isinstance(n, int) and n == 0:
                        pe.wait_ge(w_lo, 2)
                    after(pe, hid_done, n - 1)
                    for c in range(KC):
                        for m, (a, b) in enumerate(passes):
                            ins = pe.matmul(ps_h[:, s, :], xT[:, s, c, a, :], u_w[:, c, b, :], start=(c == 0 and m == 0), stop=(c == KC - 1 and m == 2))
                    ins.then_inc(hid_mm, 1)
                if runs(n, -1):
                    pe.wait_ge(hid_done, n)
                    after(pe, hT_lo, n - 1)
                    for c in range(KC):
                        ins = pe.transpose(ps_t[:, 1, c * P:(c + 1) * P], hid[:, 1 - s, c * P:(c + 1) * P], ident[:])
                    ins.then_inc(hid_turned, 1)
                if runs(n, 2):
                    turn_x(n + 2)
                if runs(n, -2):
                    if isinstance(n, int) and n == 2:
                        pe.wait_ge(w_lo, 3)
                    pe.wait_ge(hT_lo, n - 1)
                    after(pe, res_done, n - 3)
                    for c in range(KC):
                        for m, (a, b) in enumerate(passes):
                            ins = pe.matmul(ps_v[:, s, :], hT[:, s, c, a, :], v_w[:, c, b, :], start=(c == 0 and m == 0), stop=(c == KC - 1 and m == 2))
                    ins.then_inc(v_mm, 1)
            steps(pe, step)

        @block.vector
        def _(dve):
            def split(i, raw, w):
                dve.wait_ge(w_hi, i + 1)
                dve.tensor_tensor(w[:, :, 1, :], raw[:], w[:, :, 0, :].bitcast(F32), ALU.subtract).then_inc(w_lo, 1)

            def statistics(n, s):
                dve.bn_stats(stats[:, s, :], tile_or(x, n)).then_inc(stats_done, 1)

            def aggregate(n, s):
                past(dve, stats_done, 3 * n + 1, ticks)
                dve.bn_aggr(mv[:, s, :], stats[:, s, :]).then_inc(stats_done, 1)

            def add_eps(n, s):
                dve.wait_ge(stats_done, 3 * n + 2)
                dve.tensor_scalar(var_eps[:, s:s + 1], mv[:, s, 1:2], LN_EPS, None, ALU.add).then_inc(stats_done, 1)

            def normalize(n, s):
                dve.wait_ge(rstd_done, n + 1)
                after(dve, x_turned, n)
                dve.tensor_scalar(xn[:], tile_or(x, n), mv[:, s, 0:1], rstd[:, s:s + 1], ALU.subtract, ALU.mult).then_inc(normed, 1)

            def split_xT(n, s):
                dve.wait_ge(xT_hi, n + 1)
                dve.tensor_tensor(xT[:, s, :, 1, :], ps_t[:, 0, :].rearrange("p (c n) -> p c n", n=P),
                                  xT[:, s, :, 0, :].bitcast(F32), ALU.subtract).then_inc(xT_lo, 1)

            for s in range(2):
                dve.sem_inc(stored[s], 16)
            dve.wait_ge(x_loaded[0], 16)
            for n in range(2):
                statistics(n, n)
                aggregate(n, n)
                add_eps(n, n)
            normalize(0, 0)
            split(0, raw_r, r_w)
            split_xT(0, 0)
            normalize(1, 1)
            split(1, raw_u, u_w)
            split_xT(1, 1)
            dve.wait_ge(a_loaded, 32)
            dve.tensor_tensor(attr[:], attr[:], wa[:].rearrange("p (o a) -> p o a", o=1).broadcast_to([P, E, 32]), ALU.mult).then_inc(aw_done, 1)
            dve.wait_ge(aw_done, 1)
            dve.tensor_reduce(aw[:, 0, :], attr[:], AX_X, ALU.add).then_inc(aw_done, 1)
            dve.wait_ge(aw_exp, 1)
            dve.tensor_scalar(aw[:, 2, :], aw[:, 1, :], 1.0, None, ALU.add).then_inc(aw_done, 1)
            dve.wait_ge(aw_done, 3)
            dve.reciprocal(aw[:, 3, :], aw[:, 2, :]).then_inc(aw_done, 1)
            dve.wait_ge(aw_done, 4)

            def step(n, s):
                routed, ahead, turning, output = runs(n, 0), runs(n, 2), runs(n, -1), runs(n, -2)
                base = ROUTE_STEPS * n
                if isinstance(n, int) and n == 2:
                    for b in range(1, B):
                        dve.wait_ge(x_loaded[b], 16)
                if routed:
                    dve.wait_ge(route_mm, n + 1)
                    dve.tensor_copy(sc[:, s, :], ps_s[:, s, :E]).then_inc(route, 1)
                    dve.tensor_reduce(nbest[:, s:s + 1], ps_s[:, s, :E], AX_X, ALU.max, negate=True).then_inc(route, 1)
                if ahead:
                    statistics(n + 2, s)
                if routed:
                    past(dve, route, base + 2, ticks)
                    dve.max(best[:, s, :], sc[:, s, :]).then_inc(route, 1)
                if ahead:
                    aggregate(n + 2, s)
                if routed:
                    past(dve, route, base + 3, ticks)
                    dve.max_index(which[:, s, :], best[:, s, :], sc[:, s, :]).then_inc(route, 1)
                if ahead:
                    add_eps(n + 2, s)
                if routed:
                    dve.wait_ge(route, base + 4)
                    dve.tensor_copy(whichf[:, s, :], which[:, s, :TOP]).then_inc(route, 1)
                if routed:
                    dve.wait_ge(route, base + 5)
                    dve.tensor_scalar(g[:, s, 1, :], order[:], whichf[:, s, 0:1], None, ALU.is_equal).then_inc(route, 1)
                if ahead:
                    normalize(n + 2, s)
                if routed:
                    dve.wait_ge(route, base + 6)
                    dve.scalar_tensor_tensor(g[:, s, 2, :], order[:], whichf[:, s, 1:2], g[:, s, 1, :], ALU.is_equal, ALU.add).then_inc(route, 1)
                    dve.wait_ge(exp_done, n + 1)
                    dve.reciprocal(small[:, s, 1:2], small[:, s, 0:1]).then_inc(route, 1)
                if turning:
                    dve.wait_ge(hT_hi, n)
                    dve.tensor_tensor(hT[:, 1 - s, :, 1, :], ps_t[:, 1, :].rearrange("p (c n) -> p c n", n=P),
                                      hT[:, 1 - s, :, 0, :].bitcast(F32), ALU.subtract).then_inc(hT_lo, 1)
                if routed:
                    dve.wait_ge(route, base + 8)
                    dve.scalar_tensor_tensor(g[:, s, 3, :], g[:, s, 0, :], small[:, s, 1:2], g[:, s, 2, :], ALU.mult, ALU.mult).then_inc(route, 1)
                    dve.wait_ge(route, base + 9)
                    dve.tensor_reduce(small[:, s, 2:3], g[:, s, 3, :], AX_X, ALU.add).then_inc(route, 1)
                    dve.wait_ge(route, base + 10)
                    dve.tensor_scalar(small[:, s, 3:4], small[:, s, 2:3], 1e-8, None, ALU.add).then_inc(route, 1)
                    dve.wait_ge(route, base + 11)
                    dve.reciprocal(small[:, s, 4:5], small[:, s, 3:4]).then_inc(route, 1)
                    dve.wait_ge(route, base + 12)
                    dve.tensor_scalar(g[:, s, 0, :], g[:, s, 3, :], small[:, s, 4:5], None, ALU.mult).then_inc(route, 1)
                    dve.wait_ge(route, base + 13)
                    dve.wait_ge(hid_mm, n + 1)
                    after(dve, hid_turned, n - 1)
                    dve.tensor_tensor(hid[:, s, :].rearrange("p (e r) -> p e r", r=RE), ps_h[:, s, :].rearrange("p (e r) -> p e r", r=RE),
                                      g[:, s, 0, :].rearrange("p (e o) -> p e o", o=1).broadcast_to([P, E, RE]), ALU.mult).then_inc(hid_done, 1)
                    dve.tensor_tensor(g[:, s, 1, :], g[:, s, 0, :], aw[:, 3, :], ALU.mult).then_inc(route, 1)
                if ahead:
                    split_xT(n + 2, s)
                if routed:
                    dve.wait_ge(route, base + 14)
                    dve.tensor_reduce(small[:, s, 5:6], g[:, s, 1, :], AX_X, ALU.add).then_inc(route, 1)
                    dve.wait_ge(route, base + 15)
                    dve.tensor_scalar(column(y_gate, n), small[:, s, 5:6], 0.2, 0.9, ALU.mult, ALU.add).then_inc(route, 1)
                    dve.wait_ge(route, base + 16)
                if output:
                    dve.wait_ge(v_mm, n - 1)
                    after(dve, stored[s], 16 * ((n - 2) // 2 + 1))
                    dve.scalar_tensor_tensor(res[:, s, :], ps_v[:, s, :], column(y_gate, n - 2), tile_or(x, n - 2), ALU.mult, ALU.add).then_inc(res_done, 1)
                if isinstance(n, int) and n == 0:
                    split(2, raw_v, v_w)
            steps(dve, step)


def latent_tables():
    step = np.float32(1.0) / np.float32(10000.0) ** (np.arange(0, DC, 2, dtype=np.float32) / np.float32(DC))
    angle = np.arange(S, dtype=np.float32)[:, None] * step[None, :]
    sin, cos = np.repeat(np.sin(angle), 2, axis=-1), np.repeat(np.cos(angle), 2, axis=-1)
    sin[:, :DC // 2] *= -1
    return cos, sin


def stage(nc, build, *args):
    with ExitStack() as ctx:
        used = []

        def sem(name):
            used.append(ctx.enter_context(nc.semaphore(name)))
            return used[-1]

        build(nc, sem, *args)
        with nc.Block() as block:
            @block.sync
            def _(sp):
                for s in used:
                    sp.sem_clear(s)


def program(nc, d, out):
    with ExitStack() as ctx:
        sb, _, _ = ring(ctx, nc)
        ident = sb("ident", [P, P])
        scr = {
            "x2": scratch(nc, "s_x2", [T, D]),
            "x3": scratch(nc, "s_x3", [T, D]),
            "kv": scratch(nc, "s_kv", [B, P, 2 * TPB * DC]),
            "kvT": scratch(nc, "s_kvT", [B, P, 2 * S]),
            "kr": scratch(nc, "s_kr", [HP, P, 4 * P]),
            "a": scratch(nc, "s_a", [HP, P, 2 * KC * P]),
            "xT": scratch(nc, "s_xT", [B, P, 2 * KC * S]),
        }
        with ExitStack() as heads:
            with ExitStack() as first:
                sb1, _, _ = ring(first, nc)
                x_res = sb1("x_res", [P, NT, D])
                mean = sb1("mean", [P, NT])
                rstd = sb1("rstd", [P, NT])
                with ExitStack() as gated:
                    def far(name, shape, dt=F32):
                        return gated.enter_context(nc.sbuf_tensor(name, shape, dt, side="right"))

                    with ExitStack() as loads:
                        sb_in, _, sem_in = ring(loads, nc)
                        w_in = weight_buffers(sb_in, sem_in)
                        stage(nc, stage_masked_attention, d, x_res, mean, rstd, ident, w_in)
                        w_guT = far("w_guT", [P, KC, 2 * FF], BF16)
                        w_dT = far("w_dT", [P, FC, D], BF16)
                        scale_rows = far("scale_rows", [P, 2 * FF + D])
                        ident_b = far("ident_b", [P, P], BF16)
                        qT = far("tokens_qT", [P, NT, KC, P], BF16)
                        out_scale = far("out_scale", [P, NT])
                        stage(nc, stage_quantize, d, x_res, mean, rstd, w_guT, w_dT, scale_rows, ident_b, qT, out_scale, w_in)
                    stage(nc, stage_quantized_gated, d, x_res, w_guT, w_dT, scale_rows, ident_b, qT, out_scale)
                out_w = heads.enter_context(nc.sbuf_tensor("out_w", [P, H, 2, D], F32R, side="right"))
                stage(nc, stage_prepare_heads, d, scr, x_res, mean, rstd, ident, out_w)
            stage(nc, stage_latent_attention, scr, scr["x3"], ident, out_w)
        stage(nc, stage_routed_experts, d, scr["x3"], out, ident)


def kernel(**inputs):
    import concourse.bacc as bacc
    from concourse.bass_utils import run_bass_kernel_spmd

    def laid(a, *axes):
        a = np.asarray(a)
        return np.ascontiguousarray(a.transpose(axes) if axes else a)

    cos, sin = latent_tables()
    flat_ctx = laid(inputs["ctx_512"]).reshape(T, DC)
    arrays = {
        "x": laid(inputs["x"]).reshape(T, D),
        "ctx": flat_ctx,
        "ctxT": laid(flat_ctx, 1, 0),
        "attn_mask": laid(inputs["mask_SxS2_bk1"]),
        "pad_mask": laid(inputs["mask_BxS2_bf0"]),
        "L0_WqT": laid(inputs["L0_xattn_Wq"], 1, 0),
        "L0_WkT": laid(inputs["L0_xattn_Wk"], 1, 0),
        "L0_xattn_bq": laid(inputs["L0_xattn_bq"]),
        "L0_xattn_bk": laid(inputs["L0_xattn_bk"]),
        "L0_ffn_w_gate": laid(inputs["L0_ffn_w_gate"]),
        "L0_ffn_w_up": laid(inputs["L0_ffn_w_up"]),
        "L0_ffn_w_down": laid(inputs["L0_ffn_w_down"]),
        "down_idx": laid(inputs["L0_ffn_down_reorder_index"]),
        "rope_cos": cos,
        "rope_sin": sin,
        "W_krT": laid(inputs["L1_xattn_W_kr"], 1, 0, 2).reshape(DC, H * R),
        "w_kc_qT": laid(inputs["L1_xattn_w_kc_q"], 0, 2, 1),
        "W_qr": laid(inputs["L1_xattn_W_qr"]),
        "L1_Wq": laid(inputs["L1_xattn_Wq"]).reshape(H, P, D),
        "w_kc_kv": laid(inputs["L1_xattn_w_kc_kv"]),
        "WoT": laid(inputs["L1_xattn_Wo"], 1, 0).reshape(H, P, D),
        "U": laid(inputs["L1_ffn_U"], 1, 0, 2).reshape(D, E * RE),
        "V": laid(inputs["L1_ffn_V"]).reshape(E * RE, D),
        "WrT": laid(inputs["L1_ffn_Wr"], 1, 0),
        "attr": laid(inputs["L1_ffn_attr"]),
        "Wa": laid(inputs["L1_ffn_Wa"]),
    }
    nc = bacc.Bacc("TRN2", target_bir_lowering=False, num_devices=1)
    d = {k: nc.dram_tensor(f"in_{k}", a.shape, mybir.dt.from_np(a.dtype), kind="ExternalInput").ap() for k, a in arrays.items()}
    out = nc.dram_tensor("out_x", [T, D], F32, kind="ExternalOutput").ap()
    program(nc, d, out)
    r = run_bass_kernel_spmd(nc, [{f"in_{k}": a for k, a in arrays.items()}], core_ids=[0])
    return r.results[0]["out_x"].reshape(B, S, D)
```

```python
from contextlib import ExitStack

import numpy as np

import concourse.bass as bass
from concourse import mybir

P = 128
B, S, D = 4, 512, 512
T = B * S
NT = T // P
TPB = S // P
KC = D // P
DC = 128
FF = 1408
FC = FF // P
LN_EPS = 1e-5
FP8_MAX = 448.0
MASKED = -1e30

F32 = mybir.dt.float32
F32R = mybir.dt.float32r
BF16 = mybir.dt.bfloat16
U32 = mybir.dt.uint32
I32 = mybir.dt.int32
U8 = mybir.dt.uint8
ALU = mybir.AluOpType
ACT = mybir.ActivationFunctionType
AX_X = mybir.AxisListType.X


def ring(ctx, nc):
    def sb(name, shape, dt=F32):
        return ctx.enter_context(nc.sbuf_tensor(name, shape, dt))

    def ps(name, shape, dt=F32):
        return ctx.enter_context(nc.psum_tensor(name, shape, dt))

    def sem(name):
        return ctx.enter_context(nc.semaphore(name))
    return sb, ps, sem


def tile_of(a, n):
    return a[:, bass.ds(n, 1), :].rearrange("p o d -> p (o d)")


def tile_or(a, n):
    return a[:, n, :] if isinstance(n, int) else tile_of(a, n)


def column(a, n):
    return a[:, n:n + 1] if isinstance(n, int) else a[:, bass.ds(n, 1)]


def after(eng, sem, value):
    if not isinstance(value, int) or value > 0:
        eng.wait_ge(sem, value)


def past(eng, sem, value, ticks):
    eng.wait_ge(sem, value)
    if not isinstance(value, int):
        eng.sem_inc(ticks, 1)


def stage_masked_attention(nc, sem, d, x_res, mean, rstd, ident, w_in):
    with ExitStack() as ctx:
        sb, ps, _ = ring(ctx, nc)
        ctxT = sb("a_ctxT", [P, T])
        wT = sb("a_wT", [P, 2, P])
        bias_qk = sb("a_bqk", [P, 2])
        mask8 = sb("a_mask8", [P, TPB, S], U8)
        pad8 = sb("a_pad8", [P, B, S], U8)
        mask_bias = sb("a_maskb", [P, TPB, S])
        pad_bias = sb("a_padb", [P, B, S])
        both_bias = sb("a_bothb", [P, TPB, S])
        stats = sb("a_stats", [P, NT, 6])
        mv = sb("a_mv", [P, NT, 2])
        var_eps = sb("a_vareps", [P, NT])
        m_half = sb("a_mhalf", [P, NT])
        qT = sb("a_qT", [P, S])
        kT = sb("a_kT", [P, B, S])
        xn = sb("a_xn", [P, 2, S])
        z = sb("a_z", [P, 2, S])
        prob = sb("a_prob", [P, 2, S])
        nmax = sb("a_nmax", [P, 2])
        rsum = sb("a_rsum", [P, 2])
        rinv = sb("a_rinv", [P, 2])
        ps_q = ps("a_psq", [P, S])
        ps_k = ps("a_psk", [P, 2, S])
        ps_s = ps("a_pss", [P, 2, S])

        x_loaded = [sem(f"a_x_loaded{b}") for b in range(B)]
        w_loaded = sem("a_w_loaded")
        m_loaded = sem("a_m_loaded")
        halves = sem("a_halves")
        stats_done = sem("a_stats_done")
        rstd_done = sem("a_rstd_done")
        bias_made = sem("a_bias_made")
        both_made = sem("a_both_made")
        k_mm = sem("a_k_mm")
        k_ready = sem("a_k_ready")
        q_mm = sem("a_q_mm")
        q_ready = sem("a_q_ready")
        score_mm = sem("a_score_mm")
        xn_done = sem("a_xn_done")
        z_scaled = sem("a_z_scaled")
        z_done = sem("a_z_done")
        max_done = sem("a_max_done")
        exp_done = sem("a_exp_done")
        rinv_done = sem("a_rinv_done")
        x_done = sem("a_x_done")
        id_zero = sem("a_id_zero")
        SCALE = float(DC) ** -0.5

        def batches(eng, tile):
            for t in range(TPB):
                tile(t, t, 0)
            with eng.Fori(1, B) as b:
                for t in range(TPB):
                    tile(b * TPB + t, t, b)

        block = ctx.enter_context(nc.Block())

        @block.sync
        def _(sp):
            sp.dma_start(wT[:, 0, :], d["L0_WqT"]).then_inc(w_loaded, 16)
            sp.dma_start(wT[:, 1, :], d["L0_WkT"]).then_inc(w_loaded, 16)
            sp.dma_start(bias_qk[:, 0:1], d["L0_xattn_bq"].rearrange("(p o) -> p o", o=1)).then_inc(w_loaded, 16)
            sp.dma_start(bias_qk[:, 1:2], d["L0_xattn_bk"].rearrange("(p o) -> p o", o=1)).then_inc(w_loaded, 16)
            sp.dma_start(ctxT[:], d["ctxT"]).then_inc(w_loaded, 16)
            x_rows = d["x"].rearrange("(n p) c -> p n c", p=P)
            for b in range(B):
                sp.dma_start(x_res[:, TPB * b:TPB * (b + 1), :], x_rows[:, TPB * b:TPB * (b + 1), :]).then_inc(x_loaded[b], 16)
                if b == 0:
                    sp.dma_start(mask8[:], d["attn_mask"].rearrange("(t p) l -> p t l", p=P)).then_inc(m_loaded, 16)
                    sp.dma_start(pad8[:], d["pad_mask"].rearrange("(o b) l -> o b l", o=1).broadcast_to([P, B, S])).then_inc(m_loaded, 16)
            sp.dma_start(w_in["idx"][:], d["down_idx"].rearrange("(c p) -> p c", p=P), allow_slow_non_contiguous=True).then_inc(w_in["idx_loaded"], 16)
            sp.dma_start(w_in["raw_d"][:], d["L0_ffn_w_down"].rearrange("(c p) k -> p c k", p=P)).then_inc(w_in["down_loaded"], 16)

        @block.gpsimd
        def _(pool):
            pool.memset(ident[:], 0.0).then_inc(id_zero, 1)
            pool.memset(m_half[:], -0.5).then_inc(halves, 1)
            pool.wait_ge(id_zero, 1)
            pool.affine_select(out=ident[:], in_=ident[:], compare_op=ALU.not_equal, fill=1.0, base=0,
                               pattern=[[-1, P]], channel_multiplier=1).then_inc(id_zero, 1)
            pool.wait_ge(halves, 1)
            for b in range(B):
                tiles = slice(TPB * b, TPB * (b + 1))
                pool.wait_ge(stats_done, (2 * TPB + 2) * (b + 1))
                pool.tensor_tensor(rstd[:, tiles], var_eps[:, tiles], m_half[:, tiles], ALU.pow).then_inc(rstd_done, 1)
                if b == 0:
                    pool.wait_ge(bias_made, 2)
                    for t in range(TPB):
                        pool.tensor_tensor(both_bias[:, t, :], mask_bias[:, t, :], pad_bias[:, 0, :], ALU.add).then_inc(both_made, 1)
            gathers = [(h * FC + c, w, c) for h, w in enumerate(("L0_ffn_w_gate", "L0_ffn_w_up")) for c in range(FC)]
            pool.wait_ge(w_in["idx_loaded"], 16)
            for n in range(TPB, NT):
                pool.wait_ge(z_done, n - TPB + 1)
                pool.tensor_tensor(both_bias[:, n % TPB, :], mask_bias[:, n % TPB, :], pad_bias[:, n // TPB, :], ALU.add).then_inc(both_made, 1)
                for _ in range(2):
                    if gathers:
                        row, w, c = gathers.pop(0)
                        pool.indirect_dma_start(w_in["raw"][:, row, :], None, d[w],
                                                bass.IndirectOffsetOnAxis(ap=w_in["idx"][:, c:c + 1], axis=0)).then_inc(w_in["gathered"], 16)

        @block.tensor
        def _(pe):
            def queries(b):
                after(pe, q_ready, b)
                cols = ctxT[:, b * S:(b + 1) * S] if isinstance(b, int) else ctxT[:, bass.ds(b * S, S)]
                pe.matmul(ps_q[:], wT[:, 0, :], cols, start=True, stop=True).then_inc(q_mm, 1)

            def batch(b, last):
                pe.wait_ge(q_ready, b + 1)
                for t in range(TPB):
                    n = b * TPB + t
                    if t == 0:
                        pe.wait_ge(k_ready, b + 1)
                    after(pe, z_scaled, n - 1)
                    keys = kT[:, b, :] if isinstance(b, int) else tile_of(kT, b)
                    pe.matmul(ps_s[:, t % 2, :], qT[:, t * P:(t + 1) * P], keys, start=True, stop=True).then_inc(score_mm, 1)
                    if t == 1 and not last:
                        queries(b + 1)

            pe.wait_ge(w_loaded, 80)
            queries(0)
            for b in range(B):
                after(pe, k_ready, b - 1)
                pe.matmul(ps_k[:, b % 2, :], wT[:, 1, :], ctxT[:, b * S:(b + 1) * S], start=True, stop=True).then_inc(k_mm, 1)
            batch(0, False)
            with pe.Fori(1, B - 1) as b:
                batch(b, False)
            batch(B - 1, True)

        @block.scalar
        def _(act):
            def keep_queries(b):
                act.wait_ge(q_mm, b + 1)
                after(act, score_mm, b * TPB)
                act.activation(qT[:], ps_q[:], ACT.Identity, bias=bias_qk[:, 0:1]).then_inc(q_ready, 1)

            def exps(n, t):
                act.wait_ge(max_done, n + 1)
                after(act, x_done, n - 1)
                act.activation(prob[:, t % 2, :], z[:, t % 2, :], ACT.Exp, bias=nmax[:, t % 2:t % 2 + 1],
                               accum_out=rsum[:, t % 2:t % 2 + 1]).then_inc(exp_done, 1)

            act.wait_ge(w_loaded, 80)
            keep_queries(0)
            for b in range(B):
                act.wait_ge(k_mm, b + 1)
                act.activation(kT[:, b, :], ps_k[:, b % 2, :], ACT.Identity, bias=bias_qk[:, 1:2]).then_inc(k_ready, 1)
            act.wait_ge(m_loaded, 32)
            act.activation(mask_bias[:], mask8[:], ACT.Copy, scale=MASKED).then_inc(bias_made, 1)
            act.activation(pad_bias[:], pad8[:], ACT.Copy, scale=MASKED).then_inc(bias_made, 1)
            def batch(b, last):
                for t in range(TPB):
                    exps(b * TPB + t, t)
                    if t == TPB - 2 and not last:
                        keep_queries(b + 1)
            batch(0, False)
            with act.Fori(1, B - 1) as b:
                batch(b, False)
            batch(B - 1, True)

        @block.vector
        def _(dve):
            def statistics(b):
                first = (2 * TPB + 2) * b
                dve.wait_ge(x_loaded[b], 16)
                for n in range(TPB * b, TPB * (b + 1)):
                    dve.bn_stats(stats[:, n, :], x_res[:, n, :]).then_inc(stats_done, 1)
                dve.wait_ge(stats_done, first + TPB)
                for n in range(TPB * b, TPB * (b + 1)):
                    dve.bn_aggr(mv[:, n, :], stats[:, n, :]).then_inc(stats_done, 1)
                dve.wait_ge(stats_done, first + 2 * TPB)
                tiles = slice(TPB * b, TPB * (b + 1))
                dve.tensor_scalar(var_eps[:, tiles], mv[:, tiles, 1], LN_EPS, None, ALU.add).then_inc(stats_done, 1)
                dve.tensor_copy(mean[:, tiles], mv[:, tiles, 0]).then_inc(stats_done, 1)

            def update(n, s):
                dve.wait_ge(exp_done, n + 1)
                dve.reciprocal(rinv[:, s:s + 1], rsum[:, s:s + 1]).then_inc(rinv_done, 1)
                dve.wait_ge(rinv_done, n + 1)
                dve.scalar_tensor_tensor(tile_or(x_res, n), prob[:, s, :], rinv[:, s:s + 1], tile_or(x_res, n),
                                         ALU.mult, ALU.add).then_inc(x_done, 1)

            def tile(n, t, b):
                s = t % 2
                after(dve, z_scaled, n - 1)
                dve.tensor_scalar(xn[:, s, :], tile_or(x_res, n), column(mean, n), column(rstd, n),
                                  ALU.subtract, ALU.mult).then_inc(xn_done, 1)
                dve.wait_ge(xn_done, n + 1)
                dve.wait_ge(score_mm, n + 1)
                after(dve, exp_done, n - 1)
                dve.scalar_tensor_tensor(z[:, s, :], ps_s[:, s, :], SCALE, xn[:, s, :], ALU.mult, ALU.mult).then_inc(z_scaled, 1)
                dve.wait_ge(z_scaled, n + 1)
                dve.wait_ge(both_made, n + 1)
                dve.tensor_tensor(z[:, s, :], z[:, s, :], both_bias[:, t, :], ALU.add).then_inc(z_done, 1)
                dve.wait_ge(z_done, n + 1)
                dve.tensor_reduce(nmax[:, s:s + 1], z[:, s, :], AX_X, ALU.max, negate=True).then_inc(max_done, 1)
                if not isinstance(n, int) or n:
                    update(n - 1, 1 - s)

            for b in range(B):
                statistics(b)
            dve.wait_ge(rstd_done, B)
            dve.wait_ge(stats_done, (2 * TPB + 2) * B)
            batches(dve, tile)
            update(NT - 1, 1)
            dve.wait_ge(x_done, NT)


SUBNORMAL_TOP = 2.0 ** -6
MAGIC = 1.5 * 2.0 ** 20


def exponent_of(dve, e, v, done):
    dve.tensor_scalar(e.bitcast(U32), v.bitcast(U32), 0x7F800000, None, ALU.bitwise_and).then_inc(done, 1)


def rounder_of(dve, e, done):
    dve.tensor_scalar(e, e, SUBNORMAL_TOP, MAGIC, ALU.max, ALU.mult).then_inc(done, 1)


def stage_quantize(nc, sem, d, x_res, mean, rstd, w_guT, w_dT, scale_rows, ident_b, qT, out_scale, w_in):
    N = 2 * FC
    with ExitStack() as ctx:
        sb, ps, _ = ring(ctx, nc)
        raw, raw_d, gathered, down_loaded = w_in["raw"], w_in["raw_d"], w_in["gathered"], w_in["down_loaded"]
        top = sb("w_top", [P, N + KC])
        scale = sb("w_scale", [P, N + KC])
        inv = sb("w_inv", [P, N + KC])
        scaleT = sb("w_scaleT", [N + KC, P])
        identf = sb("w_identf", [P, P])
        v = sb("w_v", [P, 2 * FF])
        e = sb("w_e", [P, 2 * FF])
        q = sb("w_q", [P, 2 * FF], BF16)
        tok_sum = sb("w_toksum", [P, NT])
        tok_sq = sb("w_toksq", [P, NT])
        unread = sb("w_unread", [P, D])
        var_eps = sb("w_vareps", [P, NT])
        m_half = sb("w_mhalf", [P, NT])
        neg_mean = sb("w_negmean", [P, NT])
        tok_top = sb("w_toktop", [P, NT])
        tok_scale = sb("w_tokscale", [P, NT])
        tok_inv = sb("w_tokinv", [P, NT])
        ps_t = ps("w_pst", [P, 4, 1024], BF16)
        ps_st = ps("w_psst", [N + KC, 512])
        scale_dram = nc.dram_tensor("w_scale_rows", [N + KC, P], F32).ap()

        ids = sem("w_ids")
        halves = sem("w_halves")
        summed = sem("w_summed")
        squared = sem("w_squared")
        means = sem("w_means")
        var_done = sem("w_var_done")
        rstd_done = sem("w_rstd_done")
        maxima = sem("w_maxima")
        scales = sem("w_scales")
        scaleT_mm = sem("w_scaleT_mm")
        scaleT_done = sem("w_scaleT_done")
        scale_stored = sem("w_scale_stored")
        rows_loaded = sem("w_rows_loaded")
        centred = sem("w_centred")
        tok_scales = sem("w_tok_scales")
        scaled = sem("w_scaled")
        exps = sem("w_exps")
        rounders = sem("w_rounders")
        shifted = sem("w_shifted")
        rounded = sem("w_rounded")
        turned = sem("w_turned")
        kept = sem("w_kept")

        WEIGHTS = dict(chunks=N, width=D, slots=4, lag=2, seen=0)
        TOKENS = dict(chunks=NT, width=D, slots=4, lag=2, seen=N)
        DOWN = dict(chunks=KC, width=FF, slots=2, lag=1, seen=N + NT)
        ALL = N + NT + KC
        SQUARES = (0, 6, 10, 13, 16, 16, 16, 16)

        def steps(eng, kind, step):
            count, slots, lag = kind["chunks"], kind["slots"], kind["lag"]
            last = count + lag
            first = slots + lag + 1
            turns = max(0, (count - 1 - first) // slots)
            for c in range(min(first, last + 1)):
                step(c, c % slots)
            if turns:
                with eng.Fori(0, turns) as k:
                    for s in range(slots):
                        step(slots * k + first + s, (first + s) % slots)
            for c in range(first + slots * turns, last + 1):
                step(c, c % slots)

        def has(kind, c):
            return not isinstance(c, int) or 0 <= c < kind["chunks"]

        def columns(kind, slot):
            return slice(slot * kind["width"], (slot + 1) * kind["width"])

        def behind(eng, sem, kind, c):
            held = kind["slots"]
            value = kind["seen"] + (c - held + 1 if not isinstance(c, int) or c >= held else 0)
            if not isinstance(value, int) or value > 0:
                eng.wait_ge(sem, value)

        block = ctx.enter_context(nc.Block())

        @block.sync
        def _(sp):
            sp.wait_ge(scaleT_done, 1)
            sp.dma_start(scale_dram, scaleT[:]).then_inc(scale_stored, 16)
            sp.wait_ge(scale_stored, 16)
            sp.dma_start(scale_rows[:], scale_dram.rearrange("(o c) p -> o (c p)", o=1).broadcast_to([P, (N + KC) * P])).then_inc(rows_loaded, 16)
            sp.wait_ge(rows_loaded, 16)

        @block.gpsimd
        def _(pool):
            pool.memset(m_half[:], -0.5).then_inc(halves, 1)
            pool.memset(identf[:], 0.0).then_inc(ids, 1)
            pool.memset(ident_b[:], 0.0).then_inc(ids, 1)
            pool.wait_ge(ids, 2)
            for m in (identf, ident_b):
                pool.affine_select(out=m[:], in_=m[:], compare_op=ALU.not_equal, fill=1.0, base=0,
                                   pattern=[[-1, P]], channel_multiplier=1).then_inc(ids, 1)
            for kind in (WEIGHTS, TOKENS, DOWN):
                def shift(c, slot):
                    if has(kind, c):
                        cols = columns(kind, slot)
                        pool.wait_ge(rounders, kind["seen"] + c + 1)
                        pool.tensor_tensor(v[:, cols], v[:, cols], e[:, cols], ALU.add).then_inc(shifted, 1)
                steps(pool, kind, shift)
            pool.wait_ge(halves, 1)
            pool.wait_ge(var_done, 1)
            pool.tensor_tensor(rstd[:], var_eps[:], m_half[:], ALU.pow).then_inc(rstd_done, 1)

        @block.scalar
        def _(act):
            def scale_chunk(kind, c, slot):
                behind(act, rounded, kind, c)
                if kind is WEIGHTS:
                    src, by = tile_or(raw, c), column(inv, c)
                elif kind is TOKENS:
                    src, by = tile_or(raw, c), column(tok_inv, c)
                else:
                    src, by = tile_or(raw_d, c), column(inv, N + c)
                act.activation(v[:, columns(kind, slot)], src, ACT.Copy, scale=by).then_inc(scaled, 1)

            def keep_chunk(kind, c, slot):
                act.wait_ge(turned, kind["seen"] + c + 1)
                if kind is DOWN:
                    for b, (x, y) in enumerate(((0, 8), (8, FC))):
                        ins = act.activation(w_dT[:, x:y, c * P:(c + 1) * P], ps_t[:, 2 * slot + b, :(y - x) * P].rearrange("p (c n) -> p c n", n=P), ACT.Copy)
                elif kind is TOKENS:
                    out = qT[:, c, :, :] if isinstance(c, int) else qT[:, bass.ds(c, 1), :, :].rearrange("p o c n -> p (o c) n")
                    ins = act.activation(out, ps_t[:, slot, :D].rearrange("p (c n) -> p c n", n=P), ACT.Copy)
                else:
                    out = w_guT[:, :, c * P:(c + 1) * P] if isinstance(c, int) else w_guT[:, :, bass.ds(c * P, P)]
                    ins = act.activation(out, ps_t[:, slot, :D].rearrange("p (c n) -> p c n", n=P), ACT.Copy)
                ins.then_inc(kept, 1)

            def centre(n):
                act.wait_ge(scaled, n + 1)
                act.activation(tile_or(raw, n), tile_or(x_res, n), ACT.Identity, bias=column(neg_mean, n)).then_inc(centred, 1)

            def square(n):
                if n:
                    act.wait_ge(squared, n)
                act.activation(unread[:], x_res[:, n, :], ACT.Square, bias=neg_mean[:, n:n + 1], accum_out=tok_sq[:, n:n + 1]).then_inc(squared, 1)

            for n in range(NT):
                if n:
                    act.wait_ge(summed, n)
                act.activation(unread[:], x_res[:, n, :], ACT.Copy, accum_out=tok_sum[:, n:n + 1]).then_inc(summed, 1)
            act.wait_ge(means, 2)
            act.wait_ge(scales, 2)
            act.wait_ge(scaleT_mm, 1)
            act.activation(scaleT[:], ps_st[:, :P], ACT.Copy).then_inc(scaleT_done, 1)
            for kind in (WEIGHTS, TOKENS, DOWN):
                if kind is TOKENS:
                    for n in range(FC, NT):
                        centre(n)
                    act.wait_ge(tok_scales, 2)
                scale_chunk(kind, 0, 0)

                def step(c, slot):
                    if has(kind, c + 1):
                        scale_chunk(kind, c + 1, (slot + 1) % kind["slots"])
                    behind_by = kind["lag"] + 1
                    if has(kind, c - behind_by):
                        keep_chunk(kind, c - behind_by, (slot - behind_by) % kind["slots"])
                    if kind is DOWN:
                        for n in range(SQUARES[c], SQUARES[c + 1]):
                            square(n)
                    if kind is WEIGHTS and has(kind, c) and slot % 2 == 1:
                        centre(c // 2)
                steps(act, kind, step)

        @block.tensor
        def _(pe):
            pe.wait_ge(ids, 4)
            pe.wait_ge(scales, 2)
            pe.transpose(ps_st[:, :P], scale[:], identf[:]).then_inc(scaleT_mm, 1)
            for kind in (WEIGHTS, TOKENS, DOWN):
                def turn(c, slot):
                    if has(kind, c):
                        pe.wait_ge(rounded, kind["seen"] + c + 1)
                        behind(pe, kept, kind, c)
                        start = columns(kind, slot).start
                        for k in range(kind["width"] // P):
                            bank = 2 * slot + k // 8 if kind is DOWN else slot
                            ins = pe.transpose(ps_t[:, bank, (k % 8) * P:(k % 8 + 1) * P], q[:, start + k * P:start + (k + 1) * P], ident_b[:])
                        ins.then_inc(turned, 1)
                steps(pe, kind, turn)

        @block.vector
        def _(dve):
            dve.wait_ge(down_loaded, 16)
            dve.tensor_reduce(top[:, N:], raw_d[:], AX_X, ALU.max, apply_absolute_value=True).then_inc(maxima, 1)
            dve.wait_ge(gathered, 16 * N)
            dve.tensor_reduce(top[:, :N], raw[:], AX_X, ALU.max, apply_absolute_value=True).then_inc(maxima, 1)
            dve.wait_ge(summed, NT)
            dve.tensor_scalar(mean[:], tok_sum[:], 1.0 / D, None, ALU.mult).then_inc(means, 1)
            dve.tensor_scalar(neg_mean[:], tok_sum[:], -1.0 / D, None, ALU.mult).then_inc(means, 1)
            dve.wait_ge(maxima, 2)
            dve.tensor_scalar(scale[:], top[:], 1.0 / FP8_MAX, None, ALU.mult).then_inc(scales, 1)
            dve.wait_ge(scales, 1)
            dve.reciprocal(inv[:], scale[:]).then_inc(scales, 1)

            def find_rounder(kind, c, slot):
                cols = columns(kind, slot)
                done = kind["seen"] + c + 1
                dve.wait_ge(scaled, done)
                exponent_of(dve, e[:, cols], v[:, cols], exps)
                dve.wait_ge(exps, done)
                rounder_of(dve, e[:, cols], rounders)

            def round_chunk(kind, c, slot):
                cols = columns(kind, slot)
                dve.wait_ge(shifted, kind["seen"] + c + 1)
                behind(dve, turned, kind, c)
                dve.tensor_tensor(q[:, cols], v[:, cols], e[:, cols], ALU.subtract).then_inc(rounded, 1)

            for kind in (WEIGHTS, TOKENS, DOWN):
                if kind is TOKENS:
                    for h in range(2):
                        tiles = slice(h * NT // 2, (h + 1) * NT // 2)
                        dve.wait_ge(centred, (h + 1) * NT // 2)
                        dve.tensor_reduce(tok_top[:, tiles], raw[:, tiles, :], AX_X, ALU.max, apply_absolute_value=True).then_inc(maxima, 1)
                    dve.wait_ge(maxima, 4)
                    dve.tensor_scalar(tok_scale[:], tok_top[:], 1.0 / FP8_MAX, None, ALU.mult).then_inc(tok_scales, 1)
                    dve.wait_ge(tok_scales, 1)
                    dve.reciprocal(tok_inv[:], tok_scale[:]).then_inc(tok_scales, 1)

                def step(c, slot):
                    if has(kind, c):
                        find_rounder(kind, c, slot)
                    if has(kind, c - kind["lag"]):
                        round_chunk(kind, c - kind["lag"], (slot - kind["lag"]) % kind["slots"])
                steps(dve, kind, step)
            dve.wait_ge(squared, NT)
            dve.tensor_scalar(var_eps[:], tok_sq[:], 1.0 / D, LN_EPS, ALU.mult, ALU.add).then_inc(var_done, 1)
            dve.wait_ge(rstd_done, 1)
            dve.tensor_tensor(out_scale[:], tok_scale[:], rstd[:], ALU.mult).then_inc(tok_scales, 1)
            dve.wait_ge(tok_scales, 3)
            dve.wait_ge(rounded, ALL)
            dve.wait_ge(kept, ALL)


def stage_quantized_gated(nc, sem, d, x_res, w_guT, w_dT, scale_rows, ident_b, qT, out_scale, x_out, x_stored, load_next):
    with ExitStack() as ctx:
        sb, ps, _ = ring(ctx, nc)
        gate = sb("g_gate", [P, 2, FF])
        up = sb("g_up", [P, 2, FF])
        he = sb("g_he", [P, 2, FF])
        hq = sb("g_hq", [P, 2, FF], BF16)
        hqT = sb("g_hqT", [P, 2, FC, P], BF16)
        htop = sb("g_htop", [P, 2, 3])
        y_scale = sb("g_yscale", [P, NT])
        y = sb("g_y", [P, 2, D])
        ps_g = ps("g_psg", [P, 3, 512])
        ps_u = ps("g_psu", [P, 3, 512])
        ps_t = ps("g_pst", [P, 1024], BF16)
        ps_y = ps("g_psy", [P, D])

        gate_mm = sem("g_gate_mm")
        up_mm = sem("g_up_mm")
        gate_out = sem("g_gate_out")
        up_out = sem("g_up_out")
        silu_done = sem("g_silu_done")
        prod_done = sem("g_prod_done")
        rest_done = sem("g_rest_done")
        rest_shifted = sem("g_rest_shifted")
        htops = sem("g_htops")
        hscaled = sem("g_hscaled")
        hexps = sem("g_hexps")
        hrounders = sem("g_hrounders")
        hshifted = sem("g_hshifted")
        hrounded = sem("g_hrounded")
        hturned = sem("g_hturned")
        hqT_done = sem("g_hqT_done")
        down_mm = sem("g_down_mm")
        y_out = sem("g_y_out")
        y_scaled = sem("g_y_scaled")
        ticks = sem("g_ticks")
        x_done = sem("g_x_done")
        SHARE = 9 * P
        SHIFTS = 9 * P
        CH = ((0, 512), (512, 1024), (1024, FF))
        TURNS = ((0, 8), (8, FC))

        def steps(eng, step):
            for n in range(5):
                step(n, n % 2)
            with eng.Fori(2, NT // 2 - 1) as i:
                step(2 * i + 1, 1)
                step(2 * i + 2, 0)
            for n in range(NT - 1, NT + 3):
                step(n, n % 2)

        def runs(n, shift):
            return not isinstance(n, int) or 0 <= n + shift < NT

        block = ctx.enter_context(nc.Block())

        @block.sync
        def _(sp):
            load_next(sp)
            x_rows = x_out.rearrange("(n p) c -> p n c", p=P)
            for b in range(B):
                sp.wait_ge(x_done, TPB * (b + 1))
                sp.dma_start(x_rows[:, TPB * b:TPB * (b + 1), :], x_res[:, TPB * b:TPB * (b + 1), :]).then_inc(x_stored, 16)

        @block.gpsimd
        def _(pool):
            def step(n, s):
                if runs(n, 0):
                    pool.wait_ge(silu_done, n + 1)
                    pool.wait_ge(up_out, n + 1)
                    pool.tensor_tensor(gate[:, s, :SHARE], gate[:, s, :SHARE], up[:, s, :SHARE], ALU.mult).then_inc(prod_done, 1)
                if runs(n, -1):
                    pool.wait_ge(hrounders, n)
                    pool.tensor_tensor(gate[:, 1 - s, :SHIFTS], gate[:, 1 - s, :SHIFTS], he[:, 1 - s, :SHIFTS], ALU.add).then_inc(hshifted, 1)
                if runs(n, -3):
                    past(pool, y_scaled, n - 2, ticks)
                    pool.tensor_tensor(tile_or(x_res, n - 3), tile_or(x_res, n - 3), y[:, 1 - s, :], ALU.add).then_inc(x_done, 1)
            steps(pool, step)

        @block.scalar
        def _(act):
            def step(n, s):
                if runs(n, 0):
                    act.wait_ge(gate_out, n + 1)
                    act.activation(gate[:, s, :], gate[:, s, :], ACT.Silu, scale=column(out_scale, n)).then_inc(silu_done, 1)
                if runs(n, -2):
                    after(act, down_mm, n - 3)
                    for g, (a, b) in enumerate(TURNS):
                        act.wait_ge(hturned, 2 * (n - 2) + g + 1)
                        act.activation(hqT[:, s, a:b, :], ps_t[:, :(b - a) * P].rearrange("p (c n) -> p c n", n=P), ACT.Copy).then_inc(hqT_done, 1)
                if runs(n, -3):
                    act.wait_ge(y_out, n - 2)
                    act.activation(y[:, 1 - s, :], y[:, 1 - s, :], ACT.Copy, scale=column(y_scale, n - 3)).then_inc(y_scaled, 1)
                if runs(n, 0):
                    act.wait_ge(htops, 4 * n + 3)
                    act.activation(gate[:, s, :], gate[:, s, :], ACT.Copy, scale=htop[:, s, 2:3]).then_inc(hscaled, 1)
            steps(act, step)

        @block.tensor
        def _(pe):
            def hidden(n, base, bank, free, done):
                after(pe, free, n)
                for j, (a, b) in enumerate(CH):
                    for c in range(KC):
                        left = qT[:, n, c, :] if isinstance(n, int) else qT[:, bass.ds(n, 1), c, :].rearrange("p o n -> p (o n)")
                        ins = pe.matmul(bank[:, j, :b - a], left, w_guT[:, c, base + a:base + b], start=(c == 0), stop=(c == KC - 1))
                ins.then_inc(done, 1)

            def gate_of(n):
                hidden(n, 0, ps_g, gate_out, gate_mm)

            def up_of(n):
                hidden(n, FF, ps_u, up_out, up_mm)

            def turn_hidden(n, s, g):
                a, b = TURNS[g]
                if g == 0:
                    pe.wait_ge(hrounded, n + 1)
                after(pe, hqT_done, 2 * n + g)
                for c in range(a, b):
                    ins = pe.transpose(ps_t[:, (c - a) * P:(c - a + 1) * P], hq[:, s, c * P:(c + 1) * P], ident_b[:])
                ins.then_inc(hturned, 1)

            gate_of(0)
            up_of(0)

            def step(n, s):
                if runs(n, -2):
                    turn_hidden(n - 2, s, 0)
                if runs(n, 1):
                    gate_of(n + 1)
                if runs(n, -2):
                    turn_hidden(n - 2, s, 1)
                if runs(n, 1):
                    up_of(n + 1)
                if runs(n, -2):
                    pe.wait_ge(hqT_done, 2 * (n - 2) + 2)
                    after(pe, y_out, n - 2)
                    for c in range(FC):
                        ins = pe.matmul(ps_y[:], hqT[:, s, c, :], w_dT[:, c, :], start=(c == 0), stop=(c == FC - 1))
                    ins.then_inc(down_mm, 1)
            steps(pe, step)
            pe.wait_ge(down_mm, NT)

        @block.vector
        def _(dve):
            def output(n, s):
                dve.wait_ge(down_mm, n + 1)
                after(dve, x_done, n - 1)
                dve.tensor_tensor(y[:, s, :], ps_y[:], scale_rows[:, 2 * FF:2 * FF + D], ALU.mult).then_inc(y_out, 1)

            def step(n, s):
                if runs(n, 0):
                    dve.wait_ge(gate_mm, n + 1)
                    after(dve, hrounded, n - 1)
                    dve.tensor_tensor(gate[:, s, :], ps_g[:].rearrange("p b n -> p (b n)")[:, :FF], scale_rows[:, :FF], ALU.mult).then_inc(gate_out, 1)
                    dve.wait_ge(up_mm, n + 1)
                    dve.tensor_tensor(up[:, s, :], ps_u[:].rearrange("p b n -> p (b n)")[:, :FF], scale_rows[:, FF:2 * FF], ALU.mult).then_inc(up_out, 1)
                    dve.wait_ge(silu_done, n + 1)
                    dve.wait_ge(up_out, n + 1)
                    dve.tensor_tensor(gate[:, s, SHARE:], gate[:, s, SHARE:], up[:, s, SHARE:], ALU.mult).then_inc(rest_done, 1)
                if runs(n, -1):
                    dve.wait_ge(hscaled, n)
                    exponent_of(dve, he[:, 1 - s, :], gate[:, 1 - s, :], hexps)
                    dve.wait_ge(hexps, n)
                    rounder_of(dve, he[:, 1 - s, :], hrounders)
                    dve.wait_ge(hrounders, n)
                    dve.tensor_tensor(gate[:, 1 - s, SHIFTS:], gate[:, 1 - s, SHIFTS:], he[:, 1 - s, SHIFTS:], ALU.add).then_inc(rest_shifted, 1)
                if runs(n, -3):
                    output(n - 3, 1 - s)
                if runs(n, 0):
                    dve.wait_ge(prod_done, n + 1)
                    dve.wait_ge(rest_done, n + 1)
                    dve.tensor_reduce(htop[:, s, 0:1], gate[:, s, :], AX_X, ALU.max, apply_absolute_value=True).then_inc(htops, 1)
                    dve.wait_ge(htops, 4 * n + 1)
                    dve.tensor_scalar(htop[:, s, 1:2], htop[:, s, 0:1], 1.0 / FP8_MAX, None, ALU.mult).then_inc(htops, 1)
                    dve.wait_ge(htops, 4 * n + 2)
                    dve.reciprocal(htop[:, s, 2:3], htop[:, s, 1:2]).then_inc(htops, 1)
                    dve.tensor_scalar(column(y_scale, n), htop[:, s, 1:2], column(out_scale, n), None, ALU.mult).then_inc(htops, 1)
                if runs(n, -1):
                    dve.wait_ge(hshifted, n)
                    dve.wait_ge(rest_shifted, n)
                    after(dve, hturned, 2 * (n - 2))
                    dve.tensor_tensor(hq[:, 1 - s, :], gate[:, 1 - s, :], he[:, 1 - s, :], ALU.subtract).then_inc(hrounded, 1)
            steps(dve, step)
            dve.wait_ge(x_done, NT)


def weight_buffers(sb, sem):
    return {
        "idx": sb("w_idx", [P, FC], I32),
        "raw": sb("w_raw", [P, 2 * FC, D]),
        "raw_d": sb("w_rawd", [P, KC, FF]),
        "idx_loaded": sem("w_idx_loaded"),
        "gathered": sem("w_gathered"),
        "down_loaded": sem("w_down_loaded"),
    }

H = 16
HP = H // 2
R = 64
CQ = 384
QC = CQ // P
NP_ = B * HP
HALF = R


def scratch(nc, name, shape):
    return nc.dram_tensor(name, shape, F32).ap()


def one(a, n):
    names = "bcdefg"[:len(a.shape) - 1]
    spaced = " ".join(names)
    return a[bass.ds(n, 1)].rearrange(f"a {spaced} -> (a {names[0]}) {spaced[2:]}") if not isinstance(n, int) else a[n]


HEAD_WEIGHTS = (("cqT", QC * P), ("wqr", QC * R), ("wq", D), ("wkv", DC), ("woT", D))
HEAD_WIDTH = sum(width for _, width in HEAD_WEIGHTS)


def head_buffers(sb, sem):
    return {
        "kv": sb("p_kv", [P, NT, DC]),
        "cos": sb("p_cos", [P, TPB, DC]),
        "sin": sb("p_sin", [P, TPB, DC]),
        "w": sb("p_w", [P, 2, 2, HEAD_WIDTH]),
        "kv_loaded": sem("p_kv_loaded"),
        "x_stored": sem("p_x_stored"),
        "w_loaded": [sem(f"p_w_loaded{s}") for s in range(2)],
    }


def load_pair(sp, d, h_in, i, par):
    sp.dma_start(h_in["w"][:, par].rearrange("p h n -> p (h n)"), one(d["head_weights"], i)).then_inc(h_in["w_loaded"][par], 16)


def load_heads(sp, d, h_in):
    sp.dma_start(h_in["kv"][:], d["ctx"].rearrange("(n p) c -> p n c", p=P)).then_inc(h_in["kv_loaded"], 16)
    sp.dma_start(h_in["cos"][:], d["rope_cos"].rearrange("(n p) c -> p n c", p=P)).then_inc(h_in["kv_loaded"], 16)
    sp.dma_start(h_in["sin"][:], d["rope_sin"].rearrange("(n p) c -> p n c", p=P)).then_inc(h_in["kv_loaded"], 16)
    for i in range(2):
        load_pair(sp, d, h_in, i, i)


def stage_prepare_heads(nc, sem, d, scr, x_res, mean, rstd, ident, out_w, h_in):
    with ExitStack() as ctx:
        sb, ps, _ = ring(ctx, nc)
        kv, cos, sin = h_in["kv"], h_in["cos"], h_in["sin"]
        kv_loaded, w_loaded = h_in["kv_loaded"], h_in["w_loaded"]
        rot = sb("p_rot", [P, TPB, DC])
        kvs = sb("p_kvs", [P, 2, TPB, DC], F32R)
        kvTs = sb("p_kvTs", [P, 2, S], F32R)
        mid = sb("p_mid", [P, 2, R])
        a_sb = sb("p_a", [P, KC, P])
        xn = sb("p_xn", [P, 2, D])
        xT = sb("p_xT", [P, 4, KC, 2, P], F32R)
        stats = sb("p_stats", [P, NT, 6])
        mv = sb("p_mv", [P, NT, 2])
        var_eps = sb("p_vareps", [P, NT])
        m_half = sb("p_mhalf", [P, NT])
        ps_m = ps("p_psm", [P, 2, 512])
        ps_a = ps("p_psa", [P, KC, 2, R])
        ps_b = ps("p_psb", [P, 2, D])
        ps_t = ps("p_pst", [P, 2, 512])
        ps_k = ps("p_psk", [P, 512])

        rope_done = sem("p_rope_done")
        kv_hi = sem("p_kv_hi")
        kv_lo = sem("p_kv_lo")
        kv_turned = sem("p_kv_turned")
        kvT_hi = sem("p_kvT_hi")
        kvT_lo = sem("p_kvT_lo")
        kv_stored = sem("p_kv_stored")
        kvT_stored = sem("p_kvT_stored")
        mid_mm = sem("p_mid_mm")
        mid_done = sem("p_mid_done")
        a_mm = sem("p_a_mm")
        a_kept = sem("p_a_kept")
        a_stored = sem("p_a_stored")
        b_mm = sem("p_b_mm")
        b_hi = sem("p_b_hi")
        b_lo = sem("p_b_lo")
        halves = sem("p_halves")
        stats_done = sem("p_stats_done")
        rstd_done = sem("p_rstd_done")
        normed = sem("p_normed")
        x_turned = sem("p_x_turned")
        x_hi = sem("p_x_hi")
        x_lo = sem("p_x_lo")
        xT_stored = [sem(f"p_xT_stored{s}") for s in range(4)]

        def steps(eng, step):
            for i in range(B):
                step(i, i % 2, i // 2)
            with eng.Fori(B // 2, HP // 2) as k:
                step(2 * k, 0, k)
                step(2 * k + 1, 1, k)

        def weights(par, h, name, chunks=None):
            start = 0
            for key, width in HEAD_WEIGHTS:
                if key == name:
                    break
                start += width
            a = h_in["w"][:, par, h, start:start + width]
            return a if chunks is None else a.rearrange("p (c n) -> p c n", c=chunks)

        block = ctx.enter_context(nc.Block())

        @block.sync
        def _(sp):
            xT_dram = scr["xT"].rearrange("b p (c a t n) -> b t p c a n", c=KC, a=2, t=TPB)

            def step(i, par, half, load=True):
                if load:
                    sp.wait_ge(a_mm, i + 1)
                    sp.wait_ge(b_mm, 2 * i + 2)
                    load_pair(sp, d, h_in, i + 2, par)
                sp.wait_ge(a_kept, i + 1)
                sp.dma_start(one(scr["a"], i), a_sb[:].rearrange("p c n -> p (c n)")).then_inc(a_stored, 16)
                for t in range(2):
                    sp.wait_ge(x_lo, 2 * i + t + 1)
                    slot = 2 * par + t
                    sp.dma_start(one(xT_dram, half)[slot].rearrange("p c a n -> p (c a) n"),
                                 xT[:, slot].rearrange("p c a n -> p (c a) n").bitcast(F32)).then_inc(xT_stored[slot], 16)

            for i in range(B):
                step(i, i % 2, i // 2)
            with sp.Fori(B // 2, HP // 2 - 1) as k:
                step(2 * k, 0, k)
                step(2 * k + 1, 1, k)
            for i in range(HP - 2, HP):
                step(i, i % 2, i // 2, load=False)
            sp.wait_ge(h_in["x_stored"], 16 * B)
            sp.wait_ge(kv_stored, 16 * B)
            sp.wait_ge(kvT_stored, 16 * B)
            sp.wait_ge(a_stored, 16 * HP)
            for s in range(4):
                sp.wait_ge(xT_stored[s], 16 * (NT // 4))

        @block.gpsimd
        def _(pool):
            pool.memset(m_half[:], -0.5).then_inc(halves, 1)
            pool.wait_ge(kv_loaded, 48)
            for b in range(B):
                rows = kv[:, TPB * b:TPB * (b + 1), :]
                if b:
                    pool.wait_ge(rope_done, 4 * b)
                pool.tensor_tensor(rot[:, :, :DC // 2], rows[:, :, DC // 2:], sin[:, :, :DC // 2], ALU.mult).then_inc(rope_done, 1)
                pool.tensor_tensor(rot[:, :, DC // 2:], rows[:, :, :DC // 2], sin[:, :, DC // 2:], ALU.mult).then_inc(rope_done, 1)
                pool.wait_ge(rope_done, 4 * b + 2)
                pool.tensor_tensor(rows, rows, cos[:], ALU.mult).then_inc(rope_done, 1)
                pool.wait_ge(rope_done, 4 * b + 3)
                pool.tensor_tensor(rows, rows, rot[:], ALU.add).then_inc(rope_done, 1)
                if b == 1:
                    pool.wait_ge(halves, 1)
                    pool.wait_ge(stats_done, 2 * NT + 1)
                    pool.tensor_tensor(rstd[:], var_eps[:], m_half[:], ALU.pow).then_inc(rstd_done, 1)
            for b in range(B):
                pool.wait_ge(kv_lo, b + 1)
                pool.dma_start(scr["kv"][b], kvs[:].rearrange("p a t c -> p (a t c)").bitcast(F32)).then_inc(kv_stored, 16)
                pool.wait_ge(kvT_lo, b + 1)
                pool.dma_start(scr["kvT"][b], kvTs[:].rearrange("p a l -> p (a l)").bitcast(F32)).then_inc(kvT_stored, 16)

        @block.tensor
        def _(pe):
            def step(i, par, half):
                pe.wait_ge(w_loaded[par], 16 * (half + 1))
                for h in range(2):
                    after(pe, mid_done, 2 * i - 1 + h)
                    for c in range(QC):
                        ins = pe.matmul(ps_m[:, h, :R], weights(par, h, "cqT", QC)[:, c, :], weights(par, h, "wqr", QC)[:, c, :], start=(c == 0), stop=(c == QC - 1))
                    ins.then_inc(mid_mm, 1)
                for h in range(2):
                    after(pe, b_lo, 2 * i - 1 + h)
                    pe.matmul(ps_b[:, h, :], weights(par, h, "wkv"), weights(par, h, "woT"), start=True, stop=True).then_inc(b_mm, 1)
                pe.wait_ge(mid_done, 2 * i + 2)
                after(pe, a_kept, i)
                for h in range(2):
                    for c in range(KC):
                        ins = pe.matmul(ps_a[:, c, h, :], weights(par, h, "wq")[:, c * P:(c + 1) * P], mid[:, h, :], start=True, stop=True)
                ins.then_inc(a_mm, 1)
                for t in range(2):
                    pe.wait_ge(normed, 2 * i + t + 1)
                    after(pe, x_lo, 2 * i + t - 1)
                    for c in range(KC):
                        ins = pe.transpose(ps_t[:, t, c * P:(c + 1) * P], xn[:, t, c * P:(c + 1) * P], ident[:])
                    ins.then_inc(x_turned, 1)
                if isinstance(i, int):
                    pe.wait_ge(rope_done, 4 * i + 4)
                    after(pe, kvT_lo, i)
                    for t in range(TPB):
                        ins = pe.transpose(ps_k[:, t * P:(t + 1) * P], kv[:, TPB * i + t, :], ident[:])
                    ins.then_inc(kv_turned, 1)
            steps(pe, step)

        @block.scalar
        def _(act):
            def step(i, par, half):
                after(act, a_mm, i)
                for h in range(2):
                    act.wait_ge(mid_mm, 2 * i + h + 1)
                    act.activation(mid[:, h, :], ps_m[:, h, :R], ACT.Copy).then_inc(mid_done, 1)
                for h in range(2):
                    act.wait_ge(b_mm, 2 * i + h + 1)
                    act.activation(tile_or(out_w[:, :, 0, :], 2 * i + h), ps_b[:, h, :], ACT.Copy).then_inc(b_hi, 1)
                act.wait_ge(a_mm, i + 1)
                after(act, a_stored, 16 * i)
                act.activation(a_sb[:], ps_a[:].rearrange("p c s r -> p c (s r)"), ACT.Copy).then_inc(a_kept, 1)
                for t in range(2):
                    slot = 2 * par + t
                    act.wait_ge(x_turned, 2 * i + t + 1)
                    after(act, xT_stored[slot], 16 * half)
                    act.activation(xT[:, slot, :, 0, :], ps_t[:, t, :].rearrange("p (c n) -> p c n", n=P), ACT.Copy).then_inc(x_hi, 1)
                if isinstance(i, int):
                    after(act, kv_stored, 16 * i)
                    act.wait_ge(rope_done, 4 * i + 4)
                    act.activation(kvs[:, 0], kv[:, TPB * i:TPB * (i + 1), :], ACT.Copy).then_inc(kv_hi, 1)
                    act.wait_ge(kv_turned, i + 1)
                    after(act, kvT_stored, 16 * i)
                    act.activation(kvTs[:, 0, :], ps_k[:], ACT.Copy).then_inc(kvT_hi, 1)
            steps(act, step)

        @block.vector
        def _(dve):
            for n in range(NT):
                dve.bn_stats(stats[:, n, :], x_res[:, n, :]).then_inc(stats_done, 1)
            for n in range(NT):
                dve.wait_ge(stats_done, n + 1)
                dve.bn_aggr(mv[:, n, :], stats[:, n, :]).then_inc(stats_done, 1)
            dve.wait_ge(stats_done, 2 * NT)
            dve.tensor_scalar(var_eps[:], mv[:, :, 1], LN_EPS, None, ALU.add).then_inc(stats_done, 1)
            dve.tensor_copy(mean[:], mv[:, :, 0]).then_inc(stats_done, 1)

            def step(i, par, half):
                for h in range(2):
                    dve.wait_ge(b_hi, 2 * i + h + 1)
                    dve.tensor_tensor(tile_or(out_w[:, :, 1, :], 2 * i + h), ps_b[:, h, :],
                                      tile_or(out_w[:, :, 0, :], 2 * i + h).bitcast(F32), ALU.subtract).then_inc(b_lo, 1)
                if isinstance(i, int) and i == 0:
                    dve.wait_ge(rstd_done, 1)
                    dve.wait_ge(stats_done, 2 * NT + 2)
                for t in range(2):
                    n = 2 * i + t
                    after(dve, x_turned, n - 1)
                    dve.tensor_scalar(xn[:, t, :], tile_or(x_res, n), column(mean, n), column(rstd, n), ALU.subtract, ALU.mult).then_inc(normed, 1)
                for t in range(2):
                    slot = 2 * par + t
                    dve.wait_ge(x_hi, 2 * i + t + 1)
                    dve.tensor_tensor(xT[:, slot, :, 1, :], ps_t[:, t, :].rearrange("p (c n) -> p c n", n=P),
                                      xT[:, slot, :, 0, :].bitcast(F32), ALU.subtract).then_inc(x_lo, 1)
                if isinstance(i, int):
                    dve.wait_ge(kv_hi, i + 1)
                    dve.tensor_tensor(kvs[:, 1], kv[:, TPB * i:TPB * (i + 1), :], kvs[:, 0].bitcast(F32), ALU.subtract).then_inc(kv_lo, 1)
                    dve.wait_ge(kvT_hi, i + 1)
                    dve.tensor_tensor(kvTs[:, 1, :], ps_k[:], kvTs[:, 0, :].bitcast(F32), ALU.subtract).then_inc(kvT_lo, 1)
            steps(dve, step)


def stage_latent_attention(nc, sem, d, scr, x_out, ident, out_w):
    UNITS, HEADS, ITERS = 32, 8, B * H // 8
    TURN_LAG, PV_LAG, OUT_LAG = 2, 6, 23
    QUAD = 4
    with ExitStack() as ctx:
        sb, ps, _ = ring(ctx, nc)
        a_raw = sb("l_araw", [P, 2, KC, P])
        kr_raw = sb("l_krraw", [P, 2, 2, P])
        a_w = sb("l_aw", [P, 2, KC, P], F32R)
        kr_w = sb("l_krw", [P, 2, 2, P], F32R)
        xT = sb("l_xT", [P, KC, 2, S], F32R)
        kvT = sb("l_kvT", [P, 2, S], F32R)
        kv = sb("l_kv", [P, 2, TPB, DC], F32R)
        q_st = sb("l_qst", [P, 2, 2, S], F32R)
        k_st = sb("l_kst", [P, 2, 2, 2, S], F32R)
        prob = sb("l_prob", [P, 4, S])
        pT = sb("l_pT", [P, 2, 2, TPB, S], F32R)
        cT = sb("l_cT", [P, HEADS, 2, S], F32R)
        acc = sb("l_acc", [P, TPB, D])
        nmax = sb("l_nmax", [P, 4])
        rsum = sb("l_rsum", [P, 4])
        rinv = sb("l_rinv", [P, 4])
        ps_s = ps("l_pss", [P, 2, S])
        ps_p = ps("l_psp", [P, 2, S])
        ps_qk = ps("l_psqk", [P, S])
        ps_c = ps("l_psc", [P, 2, S])
        ps_o = ps("l_pso", [P, D])

        w_loaded = [sem(f"l_w_loaded{s}") for s in range(2)]
        w_hi = sem("l_w_hi")
        w_lo = sem("l_w_lo")
        xT_loaded = [sem(f"l_xT_loaded{c}") for c in range(KC)]
        kvT_loaded = sem("l_kvT_loaded")
        kv_loaded = sem("l_kv_loaded")
        acc_loaded = [sem(f"l_acc_loaded{t}") for t in range(TPB)]
        acc_stored = [sem(f"l_acc_stored{t}") for t in range(TPB)]
        q_mm = sem("l_q_mm")
        k_mm = sem("l_k_mm")
        st_hi = sem("l_st_hi")
        st_lo = sem("l_st_lo")
        s_mm = sem("l_s_mm")
        max_done = sem("l_max_done")
        exp_done = sem("l_exp_done")
        rinv_done = sem("l_rinv_done")
        normed = sem("l_normed")
        turned = sem("l_turned")
        pT_hi = sem("l_pT_hi")
        pT_lo = sem("l_pT_lo")
        c_mm = sem("l_c_mm")
        c_hi = sem("l_c_hi")
        c_lo = sem("l_c_lo")
        out_mm = sem("l_out_mm")
        added = sem("l_added")

        def flat(a):
            letters = "bcdefg"[:len(a.shape) - 1]
            return a.rearrange(f"p {' '.join(letters)} -> p ({' '.join(letters)})").bitcast(F32)

        def iterations(eng, unit, tail):
            for j in range(UNITS):
                unit(0, j)
            with eng.Fori(1, ITERS - 1) as n:
                for j in range(UNITS):
                    unit(n, j)
            for j in range(UNITS):
                unit(ITERS - 1, j)
            for j in range(UNITS, UNITS + tail):
                unit(ITERS - 1, j)

        def lagged(n, j, lag):
            at = j - lag
            if isinstance(n, int) and n == 0 and at < 0:
                return None
            if at >= UNITS:
                return None
            return at

        def next_pair(n, j):
            if j >= UNITS or (isinstance(n, int) and n == ITERS - 1 and j >= UNITS - 8):
                return None
            return n * 4 + j // 8 + 1, (j // 8 + 1) % 2

        ACT_SPLITS = {7: (0, 2), 1: (1, 1)}
        DVE_SPLITS = {1: (0, 1), 3: (1, 1)}

        def to_split(splits, n, j):
            which, ahead = splits.get(j % 8, (None, 0))
            if which is None or j >= UNITS or (isinstance(n, int) and n == ITERS - 1 and j // 8 + ahead >= UNITS // 8):
                return None
            return which, n * 4 + j // 8 + ahead, (j // 8 + ahead) % 2

        def out_step(n, j):
            at = j - OUT_LAG
            if isinstance(n, int) and n == 0 and at < 0:
                return None
            quad, i = at // 16, at % 16
            if isinstance(n, int) and n == ITERS - 1 and quad > 1:
                return None
            return quad, i // 4, i % 4

        block = ctx.enter_context(nc.Block())

        @block.sync
        def _(sp):
            def load_pair(p, slot, h):
                sp.dma_start(flat(a_raw[:, slot]), one(scr["a"], h)).then_inc(w_loaded[slot], 16)
                sp.dma_start(flat(kr_raw[:, slot]), one(d["kr_pairs"], h)).then_inc(w_loaded[slot], 16)

            def load_tokens(b):
                for c in range(KC):
                    sp.dma_start(flat(xT[:, c]), one(scr["xT"], b)[:, c * 2 * S:(c + 1) * 2 * S]).then_inc(xT_loaded[c], 16)

            def load_keys(b):
                sp.dma_start(flat(kvT), one(scr["kvT"], b)).then_inc(kvT_loaded, 16)

            x2 = scr["x2"].rearrange("(b t p) c -> b t p c", b=B, p=P)
            x3 = x_out.rearrange("(b t p) c -> b t p c", b=B, p=P)

            load_pair(0, 0, 0)
            load_tokens(0)
            load_keys(0)
            load_pair(1, 1, 1)
            sp.dma_start(flat(kv), scr["kv"][0]).then_inc(kv_loaded, 16)
            for t in range(TPB):
                sp.dma_start(acc[:, t, :], x2[0, t]).then_inc(acc_loaded[t], 16)

            def batch(b, first=False, last=False):
                for p in range(HP):
                    if p == HP - 1 and not last:
                        sp.wait_ge(q_mm, HP * (b + 1))
                        load_tokens(b + 1)
                    if not (last and p >= HP - 2):
                        sp.wait_ge(w_lo, 2 * (HP * b + p + 1))
                        load_pair(None, p % 2, (p + 2) % HP)
                    if p == HP - 1 and not last:
                        sp.wait_ge(k_mm, 2 * HP * (b + 1))
                        load_keys(b + 1)
                    if not first and p == 1:
                        sp.wait_ge(c_mm, H * b)
                        sp.dma_start(flat(kv), one(scr["kv"], b)).then_inc(kv_loaded, 16)
                    if not first and p in (1, 2):
                        for t in (2 * p - 2, 2 * p - 1):
                            swap(b, t)

            def swap(b, t):
                sp.wait_ge(added, (4 * b - 1) * TPB + t + 1)
                sp.dma_start(one(x3, b - 1)[t], acc[:, t, :]).then_inc(acc_stored[t], 16)
                sp.wait_ge(acc_stored[t], 16 * b)
                sp.dma_start(acc[:, t, :], one(x2, b)[t]).then_inc(acc_loaded[t], 16)

            batch(0, first=True)
            with sp.Fori(1, B - 1) as b:
                batch(b)
            batch(B - 1, last=True)
            for t in range(TPB):
                sp.wait_ge(added, (4 * B - 1) * TPB + t + 1)
                sp.dma_start(x3[B - 1, t], acc[:, t, :]).then_inc(acc_stored[t], 16)
            for t in range(TPB):
                sp.wait_ge(acc_stored[t], 16 * B)

        @block.gpsimd
        def _(pool):
            def unit(n, j):
                if j < UNITS:
                    pool.wait_ge(rinv_done, UNITS * n + j + 1)
                    pool.tensor_tensor(prob[:, j % 4, :], prob[:, j % 4, :], rinv[:, j % 4:j % 4 + 1].broadcast_to([P, S]), ALU.mult).then_inc(normed, 1)
            iterations(pool, unit, 0)

        @block.tensor
        def _(pe):
            def queries(p, slot, c):
                if c == 0:
                    after(pe, st_lo, 4 * p)
                    pe.wait_ge(w_lo, 2 * p + 1)
                pe.wait_ge(xT_loaded[c], 16 * (p // HP + 1))
                for m, (x, y) in enumerate(((0, 0), (0, 1), (1, 0))):
                    ins = pe.matmul(ps_qk[:], a_w[:, x, c, :], xT[:, c, y, :], start=(c == 0 and m == 0), stop=(c == KC - 1 and m == 2))
                if c == KC - 1:
                    ins.then_inc(q_mm, 1)

            def keys(p, slot, h):
                pe.wait_ge(st_lo, 4 * p + 2 + h)
                pe.wait_ge(w_lo, 2 * p + 2)
                pe.wait_ge(kvT_loaded, 16 * (p // HP + 1))
                for m, (x, y) in enumerate(((0, 0), (0, 1), (1, 0))):
                    ins = pe.matmul(ps_qk[:], kr_w[:, x, h, :], kvT[:, y, :], start=(m == 0), stop=(m == 2))
                ins.then_inc(k_mm, 1)

            def unit(n, j):
                u = UNITS * n + j
                if j < UNITS:
                    pair, h, t = j // 8, j // 4 % 2, j % 4
                    if t == 0:
                        pe.wait_ge(st_lo, 4 * (4 * n + pair) + 3 + h)
                    after(pe, exp_done, u - 1)
                    for x in range(2):
                        ins = pe.matmul(ps_s[:, j % 2, :], q_st[:, pair % 2, h, t * P:(t + 1) * P], k_st[:, pair % 2, h, x, :],
                                        start=(x == 0), stop=(x == 1))
                    ins.then_inc(s_mm, 1)
                if (at := lagged(n, j, TURN_LAG)) is not None:
                    pe.wait_ge(normed, u - TURN_LAG + 1)
                    after(pe, pT_lo, u - TURN_LAG - 1)
                    for c in range(TPB):
                        ins = pe.transpose(ps_p[:, at % 2, c * P:(c + 1) * P], prob[:, at % 4, c * P:(c + 1) * P], ident[:])
                    ins.then_inc(turned, 1)
                if (at := lagged(n, j, PV_LAG)) is not None:
                    c = at % 4
                    g = HEADS * n + at // 4
                    slot = (at // 4) % 2
                    if c == 0:
                        pe.wait_ge(pT_lo, 4 * g + 4)
                        after(pe, c_lo, g - 1)
                        pe.wait_ge(kv_loaded, 16 * (g // H + 1))
                    for m, (x, y) in enumerate(((0, 0), (0, 1), (1, 0))):
                        ins = pe.matmul(ps_c[:, slot, :], kv[:, x, c, :], pT[:, slot, y, c, :],
                                        start=(c == 0 and m == 0), stop=(c == TPB - 1 and m == 2))
                    if c == TPB - 1:
                        ins.then_inc(c_mm, 1)
                if (at := out_step(n, j)) is not None:
                    quad, t, step = at
                    q_index = UNITS // 16 * n + quad
                    products = [(k, x, y) for k in range(QUAD) for x, y in ((0, 0), (0, 1), (1, 0))]
                    if step == 1:
                        after(pe, added, TPB * q_index + t)
                        if t == 0:
                            pe.wait_ge(c_lo, QUAD * (q_index + 1))
                    for k, x, y in products[4 * (step - 1):4 * step] if step else ():
                        slot = (QUAD * quad + k) % HEADS
                        g = (QUAD * (q_index % (H // QUAD))) + k
                        w = out_w[:, g, y, :] if isinstance(g, int) else out_w[:, bass.ds(g, 1), y, :].rearrange("p o n -> p (o n)")
                        ins = pe.matmul(ps_o[:], cT[:, slot, x, t * P:(t + 1) * P], w, start=((k, x, y) == products[0]), stop=((k, x, y) == products[-1]))
                    if step == 3:
                        ins.then_inc(out_mm, 1)
                if (np := next_pair(n, j)) is not None:
                    p, slot = np
                    prepare(p, slot, j % 8)

            def prepare(p, slot, i):
                if i == 2:
                    queries(p, slot, 0)
                elif i == 3:
                    for c in range(1, KC):
                        queries(p, slot, c)
                elif i in (5, 7):
                    keys(p, slot, (i - 5) // 2)

            for i in range(8):
                prepare(0, 0, i)
            iterations(pe, unit, OUT_LAG)

        @block.scalar
        def _(act):
            def keep_queries(p, slot):
                act.wait_ge(q_mm, p + 1)
                after(act, s_mm, 8 * (p - 1))
                for h in range(2):
                    rows = slice(h * R, (h + 1) * R)
                    act.activation(q_st[rows, slot, h, :], ps_qk[rows, :], ACT.Copy).then_inc(st_hi, 1)

            def keep_keys(p, slot, h):
                act.wait_ge(k_mm, 2 * p + h + 1)
                act.activation(k_st[:, slot, h, 0, :], ps_qk[:], ACT.Copy).then_inc(st_hi, 1)

            def prepare(p, slot, i):
                if i == 4:
                    keep_queries(p, slot)
                if i == 6:
                    keep_keys(p, slot, 0)

            def split_weights(which, p, slot):
                act.wait_ge(w_loaded[slot], 32 * (p // 2 + 1))
                if which == 0:
                    after(act, q_mm, p)
                    act.activation(a_w[:, 0], a_raw[:, slot], ACT.Copy).then_inc(w_hi, 1)
                else:
                    after(act, k_mm, 2 * p)
                    act.activation(kr_w[:, 0], kr_raw[:, slot], ACT.Copy).then_inc(w_hi, 1)

            def unit(n, j):
                u = UNITS * n + j
                if (at := lagged(n, j, TURN_LAG)) is not None:
                    act.wait_ge(turned, u - TURN_LAG + 1)
                    g = HEADS * n + at // 4
                    if at % 4 == 0:
                        after(act, c_mm, g - 1)
                    act.activation(pT[:, (at // 4) % 2, 0, :, (at % 4) * P:(at % 4 + 1) * P],
                                   ps_p[:, at % 2, :].rearrange("p (c n) -> p c n", n=P), ACT.Copy).then_inc(pT_hi, 1)
                if j < UNITS:
                    act.wait_ge(max_done, u + 1)
                    after(act, turned, u - 3)
                    act.activation(prob[:, j % 4, :], ps_s[:, j % 2, :], ACT.Exp, bias=nmax[:, j % 4:j % 4 + 1],
                                   accum_out=rsum[:, j % 4:j % 4 + 1]).then_inc(exp_done, 1)
                if j % 4 == 2 and (at := lagged(n, j, PV_LAG + 4)) is not None:
                    g = HEADS * n + at // 4
                    act.wait_ge(c_mm, g + 1)
                    after(act, out_mm, TPB * (UNITS // 16 * n + at // 16))
                    act.activation(cT[:, (at // 4) % HEADS, 0, :], ps_c[:, (at // 4) % 2, :], ACT.Copy).then_inc(c_hi, 1)
                if j % 8 == 0 and j < UNITS:
                    keep_keys(4 * n + j // 8, (j // 8) % 2, 1)
                if (np := next_pair(n, j)) is not None:
                    prepare(np[0], np[1], j % 8)
                if (np := to_split(ACT_SPLITS, n, j)) is not None:
                    split_weights(*np)

            split_weights(0, 0, 0)
            split_weights(1, 0, 0)
            for i in range(8):
                prepare(0, 0, i)
            split_weights(0, 1, 1)
            iterations(act, unit, PV_LAG + 5)

        @block.vector
        def _(dve):
            def keep_queries(p, slot):
                for h in range(2):
                    rows, other = slice(h * R, (h + 1) * R), slice((1 - h) * R, (2 - h) * R)
                    dve.wait_ge(st_hi, 4 * p + h + 1)
                    dve.tensor_tensor(q_st[other, slot, h, :], ps_qk[rows, :], q_st[rows, slot, h, :].bitcast(F32), ALU.subtract).then_inc(st_lo, 1)

            def keep_keys(p, slot, h):
                dve.wait_ge(st_hi, 4 * p + 3 + h)
                dve.tensor_tensor(k_st[:, slot, h, 1, :], ps_qk[:], k_st[:, slot, h, 0, :].bitcast(F32), ALU.subtract).then_inc(st_lo, 1)

            def prepare(p, slot, i):
                if i == 4:
                    keep_queries(p, slot)
                if i == 6:
                    keep_keys(p, slot, 0)

            def split_weights(which, p, slot):
                w, raw = ((a_w, a_raw), (kr_w, kr_raw))[which]
                dve.wait_ge(w_hi, 2 * p + 1 + which)
                dve.tensor_tensor(w[:, 1], raw[:, slot], w[:, 0].bitcast(F32), ALU.subtract).then_inc(w_lo, 1)

            def invert(n, j):
                dve.wait_ge(exp_done, UNITS * n + j + 1)
                dve.reciprocal(rinv[:, j % 4:j % 4 + 1], rsum[:, j % 4:j % 4 + 1]).then_inc(rinv_done, 1)

            def unit(n, j):
                u = UNITS * n + j
                if (at := lagged(n, j, 1)) is not None:
                    invert(n, at)
                if j < UNITS:
                    dve.wait_ge(s_mm, u + 1)
                    dve.tensor_reduce(nmax[:, j % 4:j % 4 + 1], ps_s[:, j % 2, :], AX_X, ALU.max, negate=True).then_inc(max_done, 1)
                if (at := lagged(n, j, TURN_LAG)) is not None:
                    dve.wait_ge(pT_hi, u - TURN_LAG + 1)
                    slot, cols = (at // 4) % 2, slice((at % 4) * P, (at % 4 + 1) * P)
                    dve.tensor_tensor(pT[:, slot, 1, :, cols], ps_p[:, at % 2, :].rearrange("p (c n) -> p c n", n=P),
                                      pT[:, slot, 0, :, cols].bitcast(F32), ALU.subtract).then_inc(pT_lo, 1)
                if j % 4 == 2 and (at := lagged(n, j, PV_LAG + 4)) is not None:
                    g = HEADS * n + at // 4
                    dve.wait_ge(c_hi, g + 1)
                    slot = (at // 4) % HEADS
                    dve.tensor_tensor(cT[:, slot, 1, :], ps_c[:, (at // 4) % 2, :], cT[:, slot, 0, :].bitcast(F32), ALU.subtract).then_inc(c_lo, 1)
                if j % 4 == 3 and (at := out_step(n, j - 1)) is not None:
                    quad, t, _ = at
                    q_index = UNITS // 16 * n + quad
                    dve.wait_ge(out_mm, TPB * q_index + t + 1 + TPB)
                    dve.wait_ge(acc_loaded[t], 16 * (q_index // (H // QUAD) + 1))
                    after(dve, added, TPB * q_index + t)
                    dve.tensor_tensor(acc[:, t, :], ps_o[:], acc[:, t, :], ALU.add).then_inc(added, 1)
                if j % 8 == 0 and j < UNITS:
                    keep_keys(4 * n + j // 8, (j // 8) % 2, 1)
                if (np := next_pair(n, j)) is not None:
                    prepare(np[0], np[1], j % 8)
                if (np := to_split(DVE_SPLITS, n, j)) is not None:
                    split_weights(*np)

            dve.sem_inc(out_mm, TPB)
            split_weights(0, 0, 0)
            split_weights(1, 0, 0)
            for i in range(8):
                prepare(0, 0, i)
            iterations(dve, unit, OUT_LAG + 1)

E = 32
RE = 16
TOP = 2


def stage_routed_experts(nc, sem, d, x_in, out, ident):
    with ExitStack() as ctx:
        sb, ps, _ = ring(ctx, nc)
        raw_u = sb("e_rawu", [P, KC, E * RE])
        raw_v = sb("e_rawv", [P, KC, D])
        raw_r = sb("e_rawr", [P, KC, E])
        u_w = sb("e_uw", [P, KC, 2, E * RE], F32R)
        v_w = sb("e_vw", [P, KC, 2, D], F32R)
        r_w = sb("e_rw", [P, KC, 2, E], F32R)
        attr = sb("e_attr", [P, E, 32])
        wa = sb("e_wa", [P, 32])
        aw = sb("e_aw", [P, 4, E])
        order = sb("e_order", [P, E])
        eps = sb("e_eps", [P, 2])
        x = sb("e_x", [P, NT, D])
        xn = sb("e_xn", [P, D])
        stats = sb("e_stats", [P, 2, 6])
        mv = sb("e_mv", [P, 2, 2])
        var_eps = sb("e_vareps", [P, 2])
        rstd = sb("e_rstd", [P, 2])
        xT = sb("e_xT", [P, 2, KC, 2, P], F32R)
        sc = sb("e_sc", [P, 2, E])
        best = sb("e_best", [P, 2, 8])
        which = sb("e_which", [P, 2, 8], U32)
        whichf = sb("e_whichf", [P, 2, TOP])
        nbest = sb("e_nbest", [P, 2])
        g = sb("e_g", [P, 2, 4, E])
        small = sb("e_small", [P, 2, 8])
        y_gate = sb("e_ygate", [P, NT])
        hid = sb("e_hid", [P, 2, E * RE])
        hT = sb("e_hT", [P, 2, KC, 2, P], F32R)
        res = sb("e_res", [P, 2, D])
        ps_t = ps("e_pst", [P, 2, D])
        ps_s = ps("e_pss", [P, 2, D])
        ps_h = ps("e_psh", [P, 2, E * RE])
        ps_v = ps("e_psv", [P, 2, D])

        w_loaded = [sem(f"e_w_loaded{i}") for i in range(3)]
        a_loaded = sem("e_a_loaded")
        x_loaded = [sem(f"e_x_loaded{b}") for b in range(B)]
        setup = sem("e_setup")
        aw_done = sem("e_aw_done")
        aw_exp = sem("e_aw_exp")
        w_hi = sem("e_w_hi")
        w_lo = sem("e_w_lo")
        stats_done = sem("e_stats_done")
        rstd_done = sem("e_rstd_done")
        normed = sem("e_normed")
        x_turned = sem("e_x_turned")
        xT_hi = sem("e_xT_hi")
        xT_lo = sem("e_xT_lo")
        route_mm = sem("e_route_mm")
        hid_mm = sem("e_hid_mm")
        route = sem("e_route")
        exp_done = sem("e_exp_done")
        hid_done = sem("e_hid_done")
        hid_turned = sem("e_hid_turned")
        hT_hi = sem("e_hT_hi")
        hT_lo = sem("e_hT_lo")
        v_mm = sem("e_v_mm")
        res_done = sem("e_res_done")
        stored = [sem(f"e_stored{s}") for s in range(2)]
        ticks = sem("e_ticks")
        ROUTE_STEPS = 16
        passes = ((0, 0), (0, 1), (1, 0))

        def steps(eng, step):
            for n in range(5):
                step(n, n % 2)
            with eng.Fori(2, NT // 2 - 2) as i:
                step(2 * i + 1, 1)
                step(2 * i + 2, 0)
            for n in range(NT - 3, NT + 2):
                step(n, n % 2)

        def runs(n, shift):
            return not isinstance(n, int) or 0 <= n + shift < NT

        block = ctx.enter_context(nc.Block())

        @block.sync
        def _(sp):
            out_rows = out.rearrange("(n p) c -> n p c", p=P)
            def load_x(b):
                sp.dma_start(x[:, TPB * b:TPB * (b + 1), :], x_in.rearrange("(n p) c -> p n c", p=P)[:, TPB * b:TPB * (b + 1), :]).then_inc(x_loaded[b], 16)

            sp.dma_start(raw_r[:], d["WrT"].rearrange("(c p) n -> p c n", p=P)).then_inc(w_loaded[0], 16)
            load_x(0)
            sp.dma_start(raw_u[:], d["U"].rearrange("(c p) n -> p c n", p=P)).then_inc(w_loaded[1], 16)
            sp.dma_start(attr[:], d["attr"].rearrange("(o e) a -> o e a", o=1).broadcast_to([P, E, 32])).then_inc(a_loaded, 16)
            sp.dma_start(wa[:], d["Wa"].broadcast_to([P, 32])).then_inc(a_loaded, 16)
            sp.dma_start(raw_v[:], d["V"].rearrange("(c p) n -> p c n", p=P)).then_inc(w_loaded[2], 16)
            for b in range(1, B):
                load_x(b)

            def store(n, s):
                sp.wait_ge(res_done, n + 1)
                sp.dma_start(out_rows[n] if isinstance(n, int) else one(out_rows, n), res[:, s, :]).then_inc(stored[s], 16)

            def step(n, s):
                if runs(n, -2):
                    store(n - 2, s)
            steps(sp, step)
            for s in range(2):
                sp.wait_ge(stored[s], 16 * (NT // 2 + 1))

        @block.gpsimd
        def _(pool):
            pool.iota(order[:], pattern=[[1, E]], base=0, channel_multiplier=0, allow_small_or_imprecise_dtypes=True).then_inc(setup, 1)
            pool.memset(eps[:], -0.5).then_inc(setup, 1)
            pool.wait_ge(setup, 2)

            def invert_std(n, s):
                pool.wait_ge(stats_done, 3 * (n + 1))
                pool.tensor_tensor(rstd[:, s:s + 1], var_eps[:, s:s + 1], eps[:, 0:1], ALU.pow).then_inc(rstd_done, 1)

            for n in range(2):
                invert_std(n, n)

            def step(n, s):
                if runs(n, 2):
                    invert_std(n + 2, s)
            steps(pool, step)

        @block.scalar
        def _(act):
            def split(i, raw, w):
                act.wait_ge(w_loaded[i], 16)
                act.activation(w[:, :, 0, :], raw[:], ACT.Copy).then_inc(w_hi, 1)

            def keep_xT(n, s):
                act.wait_ge(x_turned, n + 1)
                after(act, hid_mm, n - 1)
                act.activation(xT[:, s, :, 0, :], ps_t[:, 0, :].rearrange("p (c n) -> p c n", n=P), ACT.Copy).then_inc(xT_hi, 1)

            split(0, raw_r, r_w)
            keep_xT(0, 0)
            split(1, raw_u, u_w)
            keep_xT(1, 1)
            act.wait_ge(aw_done, 2)
            act.activation(aw[:, 1, :], aw[:, 0, :], ACT.Exp, scale=-1.0).then_inc(aw_exp, 1)
            split(2, raw_v, v_w)

            def step(n, s):
                if runs(n, 0):
                    act.wait_ge(route, ROUTE_STEPS * n + 2)
                    act.activation(g[:, s, 0, :], sc[:, s, :], ACT.Exp, bias=nbest[:, s:s + 1], accum_out=small[:, s, 0:1]).then_inc(exp_done, 1)
                if runs(n, -1):
                    act.wait_ge(hid_turned, n)
                    after(act, v_mm, n - 2)
                    act.activation(hT[:, 1 - s, :, 0, :], ps_t[:, 1, :].rearrange("p (c n) -> p c n", n=P), ACT.Copy).then_inc(hT_hi, 1)
                if runs(n, 2):
                    keep_xT(n + 2, s)
            steps(act, step)

        @block.tensor
        def _(pe):
            def turn_x(n):
                pe.wait_ge(normed, n + 1)
                after(pe, xT_lo, n)
                for c in range(KC):
                    ins = pe.transpose(ps_t[:, 0, c * P:(c + 1) * P], xn[:, c * P:(c + 1) * P], ident[:])
                ins.then_inc(x_turned, 1)

            turn_x(0)
            turn_x(1)

            def step(n, s):
                if runs(n, 0):
                    if isinstance(n, int) and n == 0:
                        pe.wait_ge(w_lo, 1)
                    pe.wait_ge(xT_lo, n + 1)
                    after(pe, route, ROUTE_STEPS * (n - 1))
                    for c in range(KC):
                        for m, (a, b) in enumerate(passes):
                            ins = pe.matmul(ps_s[:, s, :E], xT[:, s, c, a, :], r_w[:, c, b, :], start=(c == 0 and m == 0), stop=(c == KC - 1 and m == 2))
                    ins.then_inc(route_mm, 1)
                    if isinstance(n, int) and n == 0:
                        pe.wait_ge(w_lo, 2)
                    after(pe, hid_done, n - 1)
                    for c in range(KC):
                        for m, (a, b) in enumerate(passes):
                            ins = pe.matmul(ps_h[:, s, :], xT[:, s, c, a, :], u_w[:, c, b, :], start=(c == 0 and m == 0), stop=(c == KC - 1 and m == 2))
                    ins.then_inc(hid_mm, 1)
                if runs(n, -1):
                    pe.wait_ge(hid_done, n)
                    after(pe, hT_lo, n - 1)
                    for c in range(KC):
                        ins = pe.transpose(ps_t[:, 1, c * P:(c + 1) * P], hid[:, 1 - s, c * P:(c + 1) * P], ident[:])
                    ins.then_inc(hid_turned, 1)
                if runs(n, 2):
                    turn_x(n + 2)
                if runs(n, -2):
                    if isinstance(n, int) and n == 2:
                        pe.wait_ge(w_lo, 3)
                    pe.wait_ge(hT_lo, n - 1)
                    after(pe, res_done, n - 3)
                    for c in range(KC):
                        for m, (a, b) in enumerate(passes):
                            ins = pe.matmul(ps_v[:, s, :], hT[:, s, c, a, :], v_w[:, c, b, :], start=(c == 0 and m == 0), stop=(c == KC - 1 and m == 2))
                    ins.then_inc(v_mm, 1)
            steps(pe, step)

        @block.vector
        def _(dve):
            def split(i, raw, w):
                dve.wait_ge(w_hi, i + 1)
                dve.tensor_tensor(w[:, :, 1, :], raw[:], w[:, :, 0, :].bitcast(F32), ALU.subtract).then_inc(w_lo, 1)

            def statistics(n, s):
                dve.bn_stats(stats[:, s, :], tile_or(x, n)).then_inc(stats_done, 1)

            def aggregate(n, s):
                past(dve, stats_done, 3 * n + 1, ticks)
                dve.bn_aggr(mv[:, s, :], stats[:, s, :]).then_inc(stats_done, 1)

            def add_eps(n, s):
                dve.wait_ge(stats_done, 3 * n + 2)
                dve.tensor_scalar(var_eps[:, s:s + 1], mv[:, s, 1:2], LN_EPS, None, ALU.add).then_inc(stats_done, 1)

            def normalize(n, s):
                dve.wait_ge(rstd_done, n + 1)
                after(dve, x_turned, n)
                dve.tensor_scalar(xn[:], tile_or(x, n), mv[:, s, 0:1], rstd[:, s:s + 1], ALU.subtract, ALU.mult).then_inc(normed, 1)

            def split_xT(n, s):
                dve.wait_ge(xT_hi, n + 1)
                dve.tensor_tensor(xT[:, s, :, 1, :], ps_t[:, 0, :].rearrange("p (c n) -> p c n", n=P),
                                  xT[:, s, :, 0, :].bitcast(F32), ALU.subtract).then_inc(xT_lo, 1)

            for s in range(2):
                dve.sem_inc(stored[s], 16)
            dve.wait_ge(x_loaded[0], 16)
            for n in range(2):
                statistics(n, n)
                aggregate(n, n)
                add_eps(n, n)
            normalize(0, 0)
            split(0, raw_r, r_w)
            split_xT(0, 0)
            normalize(1, 1)
            split(1, raw_u, u_w)
            split_xT(1, 1)
            dve.wait_ge(a_loaded, 32)
            dve.tensor_tensor(attr[:], attr[:], wa[:].rearrange("p (o a) -> p o a", o=1).broadcast_to([P, E, 32]), ALU.mult).then_inc(aw_done, 1)
            dve.wait_ge(aw_done, 1)
            dve.tensor_reduce(aw[:, 0, :], attr[:], AX_X, ALU.add).then_inc(aw_done, 1)
            dve.wait_ge(aw_exp, 1)
            dve.tensor_scalar(aw[:, 2, :], aw[:, 1, :], 1.0, None, ALU.add).then_inc(aw_done, 1)
            dve.wait_ge(aw_done, 3)
            dve.reciprocal(aw[:, 3, :], aw[:, 2, :]).then_inc(aw_done, 1)
            dve.wait_ge(aw_done, 4)

            def step(n, s):
                routed, ahead, turning, output = runs(n, 0), runs(n, 2), runs(n, -1), runs(n, -2)
                base = ROUTE_STEPS * n
                if isinstance(n, int) and n == 2:
                    for b in range(1, B):
                        dve.wait_ge(x_loaded[b], 16)
                if routed:
                    dve.wait_ge(route_mm, n + 1)
                    dve.tensor_copy(sc[:, s, :], ps_s[:, s, :E]).then_inc(route, 1)
                    dve.tensor_reduce(nbest[:, s:s + 1], ps_s[:, s, :E], AX_X, ALU.max, negate=True).then_inc(route, 1)
                if ahead:
                    statistics(n + 2, s)
                if routed:
                    past(dve, route, base + 2, ticks)
                    dve.max(best[:, s, :], sc[:, s, :]).then_inc(route, 1)
                if ahead:
                    aggregate(n + 2, s)
                if routed:
                    past(dve, route, base + 3, ticks)
                    dve.max_index(which[:, s, :], best[:, s, :], sc[:, s, :]).then_inc(route, 1)
                if ahead:
                    add_eps(n + 2, s)
                if routed:
                    dve.wait_ge(route, base + 4)
                    dve.tensor_copy(whichf[:, s, :], which[:, s, :TOP]).then_inc(route, 1)
                if routed:
                    dve.wait_ge(route, base + 5)
                    dve.tensor_scalar(g[:, s, 1, :], order[:], whichf[:, s, 0:1], None, ALU.is_equal).then_inc(route, 1)
                if ahead:
                    normalize(n + 2, s)
                if routed:
                    dve.wait_ge(route, base + 6)
                    dve.scalar_tensor_tensor(g[:, s, 2, :], order[:], whichf[:, s, 1:2], g[:, s, 1, :], ALU.is_equal, ALU.add).then_inc(route, 1)
                    dve.wait_ge(exp_done, n + 1)
                    dve.reciprocal(small[:, s, 1:2], small[:, s, 0:1]).then_inc(route, 1)
                if turning:
                    dve.wait_ge(hT_hi, n)
                    dve.tensor_tensor(hT[:, 1 - s, :, 1, :], ps_t[:, 1, :].rearrange("p (c n) -> p c n", n=P),
                                      hT[:, 1 - s, :, 0, :].bitcast(F32), ALU.subtract).then_inc(hT_lo, 1)
                if routed:
                    dve.wait_ge(route, base + 8)
                    dve.scalar_tensor_tensor(g[:, s, 3, :], g[:, s, 0, :], small[:, s, 1:2], g[:, s, 2, :], ALU.mult, ALU.mult).then_inc(route, 1)
                    dve.wait_ge(route, base + 9)
                    dve.tensor_reduce(small[:, s, 2:3], g[:, s, 3, :], AX_X, ALU.add).then_inc(route, 1)
                    dve.wait_ge(route, base + 10)
                    dve.tensor_scalar(small[:, s, 3:4], small[:, s, 2:3], 1e-8, None, ALU.add).then_inc(route, 1)
                    dve.wait_ge(route, base + 11)
                    dve.reciprocal(small[:, s, 4:5], small[:, s, 3:4]).then_inc(route, 1)
                    dve.wait_ge(route, base + 12)
                    dve.tensor_scalar(g[:, s, 0, :], g[:, s, 3, :], small[:, s, 4:5], None, ALU.mult).then_inc(route, 1)
                    dve.wait_ge(route, base + 13)
                    dve.wait_ge(hid_mm, n + 1)
                    after(dve, hid_turned, n - 1)
                    dve.tensor_tensor(hid[:, s, :].rearrange("p (e r) -> p e r", r=RE), ps_h[:, s, :].rearrange("p (e r) -> p e r", r=RE),
                                      g[:, s, 0, :].rearrange("p (e o) -> p e o", o=1).broadcast_to([P, E, RE]), ALU.mult).then_inc(hid_done, 1)
                    dve.tensor_tensor(g[:, s, 1, :], g[:, s, 0, :], aw[:, 3, :], ALU.mult).then_inc(route, 1)
                if ahead:
                    split_xT(n + 2, s)
                if routed:
                    dve.wait_ge(route, base + 14)
                    dve.tensor_reduce(small[:, s, 5:6], g[:, s, 1, :], AX_X, ALU.add).then_inc(route, 1)
                    dve.wait_ge(route, base + 15)
                    dve.tensor_scalar(column(y_gate, n), small[:, s, 5:6], 0.2, 0.9, ALU.mult, ALU.add).then_inc(route, 1)
                    dve.wait_ge(route, base + 16)
                if output:
                    dve.wait_ge(v_mm, n - 1)
                    after(dve, stored[s], 16 * ((n - 2) // 2 + 1))
                    dve.scalar_tensor_tensor(res[:, s, :], ps_v[:, s, :], column(y_gate, n - 2), tile_or(x, n - 2), ALU.mult, ALU.add).then_inc(res_done, 1)
                if isinstance(n, int) and n == 0:
                    split(2, raw_v, v_w)
            steps(dve, step)


def latent_tables():
    step = np.float32(1.0) / np.float32(10000.0) ** (np.arange(0, DC, 2, dtype=np.float32) / np.float32(DC))
    angle = np.arange(S, dtype=np.float32)[:, None] * step[None, :]
    sin, cos = np.repeat(np.sin(angle), 2, axis=-1), np.repeat(np.cos(angle), 2, axis=-1)
    sin[:, :DC // 2] *= -1
    return cos, sin


def stage(nc, build, *args):
    with ExitStack() as ctx:
        used = []

        def sem(name):
            used.append(ctx.enter_context(nc.semaphore(name)))
            return used[-1]

        build(nc, sem, *args)
        with nc.Block() as block:
            @block.sync
            def _(sp):
                for s in used:
                    sp.sem_clear(s)


def program(nc, d, out):
    with ExitStack() as ctx:
        sb, _, _ = ring(ctx, nc)
        ident = sb("ident", [P, P])
        scr = {
            "x2": scratch(nc, "s_x2", [T, D]),
            "x3": scratch(nc, "s_x3", [T, D]),
            "kv": scratch(nc, "s_kv", [B, P, 2 * TPB * DC]),
            "kvT": scratch(nc, "s_kvT", [B, P, 2 * S]),
            "a": scratch(nc, "s_a", [HP, P, KC * P]),
            "xT": scratch(nc, "s_xT", [B, P, 2 * KC * S]),
        }
        with ExitStack() as heads:
            with ExitStack() as first:
                sb1, _, sem1 = ring(first, nc)
                x_res = sb1("x_res", [P, NT, D])
                mean = sb1("mean", [P, NT])
                rstd = sb1("rstd", [P, NT])
                with ExitStack() as gated:
                    def far(name, shape, dt=F32):
                        return gated.enter_context(nc.sbuf_tensor(name, shape, dt, side="right"))

                    with ExitStack() as loads:
                        sb_in, _, sem_in = ring(loads, nc)
                        w_in = weight_buffers(sb_in, sem_in)
                        stage(nc, stage_masked_attention, d, x_res, mean, rstd, ident, w_in)
                        w_guT = far("w_guT", [P, KC, 2 * FF], BF16)
                        w_dT = far("w_dT", [P, FC, D], BF16)
                        scale_rows = far("scale_rows", [P, 2 * FF + D])
                        ident_b = far("ident_b", [P, P], BF16)
                        qT = far("tokens_qT", [P, NT, KC, P], BF16)
                        out_scale = far("out_scale", [P, NT])
                        stage(nc, stage_quantize, d, x_res, mean, rstd, w_guT, w_dT, scale_rows, ident_b, qT, out_scale, w_in)
                    h_in = head_buffers(sb1, sem1)
                    stage(nc, stage_quantized_gated, d, x_res, w_guT, w_dT, scale_rows, ident_b, qT, out_scale,
                          scr["x2"], h_in["x_stored"], lambda sp: load_heads(sp, d, h_in))
                out_w = heads.enter_context(nc.sbuf_tensor("out_w", [P, H, 2, D], F32R, side="right"))
                stage(nc, stage_prepare_heads, d, scr, x_res, mean, rstd, ident, out_w, h_in)
            stage(nc, stage_latent_attention, d, scr, scr["x3"], ident, out_w)
        stage(nc, stage_routed_experts, d, scr["x3"], out, ident)


def head_weights(inputs):
    def rows_by_chunks(a):
        return a.reshape(H, QC, P, -1).transpose(0, 2, 1, 3).reshape(H, P, -1)

    parts = {
        "cqT": rows_by_chunks(np.asarray(inputs["L1_xattn_w_kc_q"]).transpose(0, 2, 1)),
        "wqr": rows_by_chunks(np.asarray(inputs["L1_xattn_W_qr"])),
        "wq": np.asarray(inputs["L1_xattn_Wq"]).reshape(H, P, D),
        "wkv": np.asarray(inputs["L1_xattn_w_kc_kv"]),
        "woT": np.asarray(inputs["L1_xattn_Wo"]).T.reshape(H, P, D),
    }
    by_head = np.concatenate([parts[name] for name, _ in HEAD_WEIGHTS], axis=2)
    return np.ascontiguousarray(by_head.reshape(HP, 2, P, HEAD_WIDTH).transpose(0, 2, 1, 3).reshape(HP, P, 2 * HEAD_WIDTH))


def key_weights(inputs):
    a = np.asarray(inputs["L1_xattn_W_kr"]).transpose(1, 0, 2)
    twice = np.stack([a, a], axis=2).reshape(DC, HP, 2 * P)
    return np.ascontiguousarray(twice.transpose(1, 0, 2))


def kernel(**inputs):
    import concourse.bacc as bacc
    from concourse.bass_utils import run_bass_kernel_spmd

    def laid(a, *axes):
        a = np.asarray(a)
        return np.ascontiguousarray(a.transpose(axes) if axes else a)

    cos, sin = latent_tables()
    flat_ctx = laid(inputs["ctx_512"]).reshape(T, DC)
    arrays = {
        "x": laid(inputs["x"]).reshape(T, D),
        "ctx": flat_ctx,
        "ctxT": laid(flat_ctx, 1, 0),
        "attn_mask": laid(inputs["mask_SxS2_bk1"]),
        "pad_mask": laid(inputs["mask_BxS2_bf0"]),
        "L0_WqT": laid(inputs["L0_xattn_Wq"], 1, 0),
        "L0_WkT": laid(inputs["L0_xattn_Wk"], 1, 0),
        "L0_xattn_bq": laid(inputs["L0_xattn_bq"]),
        "L0_xattn_bk": laid(inputs["L0_xattn_bk"]),
        "L0_ffn_w_gate": laid(inputs["L0_ffn_w_gate"]),
        "L0_ffn_w_up": laid(inputs["L0_ffn_w_up"]),
        "L0_ffn_w_down": laid(inputs["L0_ffn_w_down"]),
        "down_idx": laid(inputs["L0_ffn_down_reorder_index"]),
        "rope_cos": cos,
        "rope_sin": sin,
        "kr_pairs": key_weights(inputs),
        "head_weights": head_weights(inputs),
        "U": laid(inputs["L1_ffn_U"], 1, 0, 2).reshape(D, E * RE),
        "V": laid(inputs["L1_ffn_V"]).reshape(E * RE, D),
        "WrT": laid(inputs["L1_ffn_Wr"], 1, 0),
        "attr": laid(inputs["L1_ffn_attr"]),
        "Wa": laid(inputs["L1_ffn_Wa"]),
    }
    nc = bacc.Bacc("TRN2", target_bir_lowering=False, num_devices=1)
    d = {k: nc.dram_tensor(f"in_{k}", a.shape, mybir.dt.from_np(a.dtype), kind="ExternalInput").ap() for k, a in arrays.items()}
    out = nc.dram_tensor("out_x", [T, D], F32, kind="ExternalOutput").ap()
    program(nc, d, out)
    r = run_bass_kernel_spmd(nc, [{f"in_{k}": a for k, a in arrays.items()}], core_ids=[0])
    return r.results[0]["out_x"].reshape(B, S, D)
```
